# Optimizing a Trainium2 kernel written in Bass

```python
import numpy as np
import jax
import jax.numpy as jnp

def _softmax(x, axis=-1):
    return jax.nn.softmax(x, axis=axis)

def _gelu(x):
    return jax.nn.gelu(x, approximate=True)

def _silu(x):
    return jax.nn.silu(x)

def _sigmoid(x):
    return jax.nn.sigmoid(x)

def _layernorm(x, axis=-1, eps=1e-05):
    m = jnp.mean(x, axis=axis, keepdims=True)
    v = jnp.var(x, axis=axis, keepdims=True)
    return (x - m) / jnp.sqrt(v + eps)

def _scatter_add(tgt, idx, src, axis=0):
    return tgt.at[idx].add(src)

def _segment_sum(src, seg, n):
    return jax.ops.segment_sum(src, seg, n)
kernel_name = 'mk_hybrid_d1_jaxref_r8_40dc5c'

def setup_inputs(seed: int=0):
    np.random.seed(seed)
    _w = jnp.asarray

    def _L0_attn_a_setup():
        import jax, jax.numpy as jnp
        import numpy as np
        import math
        N_EMBD = 128
        N_HEAD = 16
        N_LAYER = 12
        key = jax.random.key(seed)
        kx, kw, kb = jax.random.split(key, 3)
        B, T, C = (4, 256, N_EMBD)
        x = jax.random.normal(kx, (B, T, C), dtype=jnp.float32)
        bound = 1.0 / math.sqrt(C)
        W = jax.random.uniform(kw, (3 * C, C), minval=-bound, maxval=bound, dtype=jnp.float32)
        W = W * (1.0 / math.sqrt(N_LAYER * 2))
        b = jax.random.uniform(kb, (3 * C,), minval=-bound, maxval=bound, dtype=jnp.float32)
        return {'x': x, 'W': W, 'b': b}
    _L0_attn_a_in = _L0_attn_a_setup()

    def _L0_attn_b_setup():
        import jax, jax.numpy as jnp
        import numpy as np
        H = 16
        HD = 64
        W = 128
        G = 32
        EPS = 1e-06
        NEG = -1e+30
        key = jax.random.key(seed)
        ks = jax.random.split(key, 7)
        B, S, D = (1, 1024, 128)
        inner = H * HD
        s = 0.02
        return {'x': jax.random.normal(ks[0], (B, S, D), jnp.float32), 'norm_w': jnp.ones((D,), jnp.float32), 'w_q': jax.random.normal(ks[1], (D, inner), jnp.float32) * s, 'w_k': jax.random.normal(ks[2], (D, inner), jnp.float32) * s, 'w_v': jax.random.normal(ks[3], (D, inner), jnp.float32) * s, 'w_out': jax.random.normal(ks[4], (inner, D), jnp.float32) * s, 'scorer_w': jax.random.normal(ks[5], (D, 1), jnp.float32) * s, 'scorer_b': jnp.zeros((1,), jnp.float32)}
    _L0_attn_b_in = _L0_attn_b_setup()

    def _L0_ffn_setup():
        import jax, jax.numpy as jnp
        import numpy as np
        B, S, IN, OUT = (4, 1024, 128, 128)
        EPS = 1e-06

        def _xla_quantized_matmul(x2d, weight_q, weight_scale):
            amax = jnp.max(jnp.abs(x2d), axis=-1, keepdims=True)
            x_scale = jnp.maximum(amax, EPS) / 127.0
            x_q = jnp.clip(jnp.round(x2d / x_scale), -128, 127).astype(jnp.int8)
            acc = jax.lax.dot_general(x_q, weight_q, (((1,), (1,)), ((), ())), preferred_element_type=jnp.int32)
            return acc.astype(jnp.float32) * x_scale * weight_scale[None, :]
        key = jax.random.key(seed)
        k1, k2, k3, k4 = jax.random.split(key, 4)
        x = jax.random.normal(k1, (B, S, IN), dtype=jnp.float32)
        weight_q = jax.random.randint(k2, (OUT, IN), -128, 128, dtype=jnp.int32).astype(jnp.int8)
        weight_scale = jax.random.uniform(k3, (OUT,), dtype=jnp.float32, minval=0.001, maxval=0.01)
        bias = jax.random.normal(k4, (OUT,), dtype=jnp.float32) * 0.01
        return {'x': x, 'weight_q': weight_q, 'weight_scale': weight_scale, 'bias': bias}
    _L0_ffn_in = _L0_ffn_setup()
    _d = {'L0_attn_a_x': _L0_attn_a_in['x'], 'L0_attn_a_W': _L0_attn_a_in['W'], 'L0_attn_a_b': _L0_attn_a_in['b'], 'L0_attn_b_norm_w': _L0_attn_b_in['norm_w'], 'L0_attn_b_w_q': _L0_attn_b_in['w_q'], 'L0_attn_b_w_k': _L0_attn_b_in['w_k'], 'L0_attn_b_w_v': _L0_attn_b_in['w_v'], 'L0_attn_b_w_out': _L0_attn_b_in['w_out'], 'L0_attn_b_scorer_w': _L0_attn_b_in['scorer_w'], 'L0_attn_b_scorer_b': _L0_attn_b_in['scorer_b'], 'L0_ffn_weight_q': _L0_ffn_in['weight_q'], 'L0_ffn_weight_scale': _L0_ffn_in['weight_scale'], 'L0_ffn_bias': _L0_ffn_in['bias']}
    _x0 = _d['L0_attn_a_x']
    _d['L0_attn_a_x'] = jax.random.normal(jax.random.fold_in(jax.random.key(seed), 1), (2, 1024, 128), dtype=_x0.dtype)
    del _x0
    return _d

def reference(L0_attn_a_x, L0_attn_a_W, L0_attn_a_b, L0_attn_b_norm_w, L0_attn_b_w_q, L0_attn_b_w_k, L0_attn_b_w_v, L0_attn_b_w_out, L0_attn_b_scorer_w, L0_attn_b_scorer_b, L0_ffn_weight_q, L0_ffn_weight_scale, L0_ffn_bias):

    def _L0_attn_a_ref(x, W, b):
        import jax, jax.numpy as jnp
        import numpy as np
        import math
        N_EMBD = 128
        N_HEAD = 16
        N_LAYER = 12
        B, T, C = x.shape
        H = N_HEAD
        D = C // H
        qkv = jnp.einsum('btc,oc->bto', x, W) + b
        q, k, v = jnp.split(qkv, 3, axis=-1)
        q = q.reshape(B, T, H, D).transpose(0, 2, 1, 3)
        k = k.reshape(B, T, H, D).transpose(0, 2, 1, 3)
        v = v.reshape(B, T, H, D).transpose(0, 2, 1, 3)
        att = jnp.einsum('bhtd,bhsd->bhts', q, k) / math.sqrt(D)
        causal = jnp.tril(jnp.ones((T, T), dtype=bool))
        att = jnp.where(causal, att, -jnp.inf)
        att = jax.nn.softmax(att, axis=-1)
        y = jnp.einsum('bhts,bhsd->bhtd', att, v)
        return y.transpose(0, 2, 1, 3).reshape(B, T, C)

    def _L0_attn_b_ref(x, norm_w, w_q, w_k, w_v, w_out, scorer_w, scorer_b):
        import jax, jax.numpy as jnp
        import numpy as np
        H = 16
        HD = 64
        W = 128
        G = 32
        EPS = 1e-06
        NEG = -1e+30
        B, S, D = x.shape
        h = x * jax.lax.rsqrt(jnp.mean(x * x, axis=-1, keepdims=True) + EPS) * norm_w

        def proj(w):
            return jnp.einsum('bsd,de->bse', h, w).reshape(B, S, H, HD).transpose(0, 2, 1, 3)
        q, k, v = (proj(w_q), proj(w_k), proj(w_v))
        scale = HD ** (-0.5)
        nW = S // W
        qw = q.reshape(B, H, nW, W, HD)
        kw = k.reshape(B, H, nW, W, HD)
        vw = v.reshape(B, H, nW, W, HD)
        ll = jnp.einsum('bhnqd,bhnkd->bhnqk', qw, kw) * scale
        cm = jnp.tril(jnp.ones((W, W), bool))
        ll = jnp.where(cm, ll, NEG).reshape(B, H, S, W)
        scores = (jnp.einsum('bsd,do->bso', h, scorer_w) + scorer_b)[..., 0]
        _, idx = jax.lax.top_k(scores, G)
        kg = jnp.take_along_axis(k, idx[:, None, :, None], axis=2)
        vg = jnp.take_along_axis(v, idx[:, None, :, None], axis=2)
        lg = jnp.einsum('bhsd,bhgd->bhsg', q, kg) * scale
        pos = jnp.arange(S)
        gmask = idx[:, None, None, :] <= pos[None, None, :, None]
        lg = jnp.where(gmask, lg, NEG)
        attn = jax.nn.softmax(jnp.concatenate([ll, lg], axis=-1), axis=-1)
        a_loc = attn[..., :W].reshape(B, H, nW, W, W)
        o = jnp.einsum('bhnqk,bhnkd->bhnqd', a_loc, vw).reshape(B, H, S, HD)
        o = o + jnp.einsum('bhsg,bhgd->bhsd', attn[..., W:], vg)
        o = o.transpose(0, 2, 1, 3).reshape(B, S, H * HD)
        return x + jnp.einsum('bse,ed->bsd', o, w_out)

    def _L0_ffn_ref(x, weight_q, weight_scale, bias):
        import jax, jax.numpy as jnp
        import numpy as np
        B, S, IN, OUT = (4, 1024, 128, 128)
        EPS = 1e-06

        def _xla_quantized_matmul(x2d, weight_q, weight_scale):
            amax = jnp.max(jnp.abs(x2d), axis=-1, keepdims=True)
            x_scale = jnp.maximum(amax, EPS) / 127.0
            x_q = jnp.clip(jnp.round(x2d / x_scale), -128, 127).astype(jnp.int8)
            acc = jax.lax.dot_general(x_q, weight_q, (((1,), (1,)), ((), ())), preferred_element_type=jnp.int32)
            return acc.astype(jnp.float32) * x_scale * weight_scale[None, :]
        orig_shape = x.shape
        x2d = x.reshape(-1, orig_shape[-1])
        out = _xla_quantized_matmul(x2d, weight_q, weight_scale)
        out = out.reshape(*orig_shape[:-1], out.shape[-1])
        out = out + bias
        return out
    x = L0_attn_a_x
    x = x + _L0_attn_a_ref(_layernorm(x, axis=-1), L0_attn_a_W, L0_attn_a_b)
    x = x + _L0_ffn_ref(_layernorm(x, axis=-1), L0_ffn_weight_q, L0_ffn_weight_scale, L0_ffn_bias)
    x = x + _L0_attn_b_ref(_layernorm(x, axis=-1), L0_attn_b_norm_w, L0_attn_b_w_q, L0_attn_b_w_k, L0_attn_b_w_v, L0_attn_b_w_out, L0_attn_b_scorer_w, L0_attn_b_scorer_b)
    x = x + _L0_ffn_ref(_layernorm(x, axis=-1), L0_ffn_weight_q, L0_ffn_weight_scale, L0_ffn_bias)
    return x

_drawn_inputs = setup_inputs


def setup_inputs(seed=0):
    import zlib

    import numpy as np

    out = dict(_drawn_inputs(seed))
    spreads = {'L0_attn_b_norm_w': (1.0, 0.6)}
    factors = {'L0_attn_a_W': 4.906,
     'L0_attn_b_w_q': 8.0,
     'L0_attn_b_w_k': 8.0,
     'L0_attn_b_w_v': 8.0,
     'L0_attn_b_w_out': 8.0,
     'L0_attn_b_scorer_w': 8.0,
     'L0_ffn_bias': 8.0}
    for name, (base, spread) in spreads.items():
        noise = np.random.default_rng([zlib.crc32(name.encode()), seed]).standard_normal(out[name].shape)
        drawn = base * np.exp(spread * noise) if base else spread * noise
        out[name] = jnp.asarray(drawn.astype(out[name].dtype))
    for name, factor in factors.items():
        out[name] = (out[name] * factor).astype(out[name].dtype)
    return out
```

```python
from contextlib import ExitStack

import concourse.bass as bass
from concourse import mybir

F32 = mybir.dt.float32
BF16 = mybir.dt.bfloat16
I32 = mybir.dt.int32
U32 = mybir.dt.uint32
ALU = mybir.AluOpType
ACT = mybir.ActivationFunctionType
X = mybir.AxisListType.X

P = 128
BATCH, SEQ, DIM = 2, 1024, 128
TILES = SEQ // P
NT = BATCH * TILES
BANK = 512

HEADS_A, HD_A = 16, 8
QUAD = 4
GROUPS = HEADS_A // QUAD
PARTS = 3
ROWS = PARTS * PARTS * HD_A
MROWS = ROWS + PARTS
BIG = -1.0e30
MAGIC = 1.5 * 2.0 ** 23

HEADS_B, HD_B = 16, 64
PAIRS = HEADS_B // 2
PICKED = 32
KEYS = P + PICKED

MAX_UNITS = []
for _t in range(TILES):
    _n = QUAD if _t < 2 else (2 if _t < 4 else 1)
    MAX_UNITS += [(_t, h, _n) for h in range(0, QUAD, _n)]
MAX_SLOTS = len(MAX_UNITS) + 1

PROB_GROUPS = []
for _c in range(SEQ // BANK):
    for _j in range(4 * (_c + 1)):
        _lo = max(BANK * _c, P * _j)
        _w = BANK * (_c + 1) - _lo
        PROB_GROUPS.append((_c, _j, _lo, _w, max(1, min(QUAD, BANK // _w))))
PROB_UNITS = []
for _g, (_c, _j, _lo, _w, _n) in enumerate(PROB_GROUPS):
    PROB_UNITS += [(_g, h, _n) for h in range(0, QUAD, _n)]
NG, NU = len(PROB_GROUPS), len(PROB_UNITS)
DIAG = [_j * P >= BANK * _c for _c, _j, *_ in PROB_GROUPS]
UNITS_OF = [[u for u, x in enumerate(PROB_UNITS) if x[0] == g] for g in range(NG)]
MASKED = [u for u, x in enumerate(PROB_UNITS) if DIAG[x[0]]]


def order_of_step():
    cols = [(PROB_GROUPS[g][3]) * n for g, _, n in PROB_UNITS]
    total, at, items, done = sum(cols), 0, [], []
    for u, c in enumerate(cols):
        items.append((at / total + SCORE_LAG, 0, "score", u))
        at += c
        done.append(at / total)
    for g in range(NG):
        items.append((done[UNITS_OF[g][-1]] + SCORE_LAG + WEIGH_LAG, 1, "weigh", g))
    at = 0
    for k in range(MAX_SLOTS):
        items.append((MAX_SHARE * at / total + (TURN_LAG if k == len(MAX_UNITS) else 0), 2, "max", k))
        at += P * (MAX_UNITS[k][0] + 1) * MAX_UNITS[k][2] if k < len(MAX_UNITS) else 0
    return [(what, n) for _, _, what, n in sorted(items)]


SCORE_LAG = 0.04
WEIGH_LAG = 0.05
TURN_LAG = 0.08
MAX_SHARE = 0.82
STEP = order_of_step()
PROB_SLOTS = NU // 2
SCORE_BANKS = 3


def last_in_bank(u):
    bank = u % SCORE_BANKS
    if u >= SCORE_BANKS:
        return u - SCORE_BANKS
    return max(v for v in range(2 * NU) if v % SCORE_BANKS == bank) - 2 * NU


def make_identity(pool, tile, made):
    pool.memset(tile[:], 0.0).then_inc(made, 1)
    pool.wait_ge(made, 1)
    pool.affine_select(out=tile[:], in_=tile[:], compare_op=ALU.not_equal, fill=1.0, base=0,
                       pattern=[[-1, P]], channel_multiplier=1).then_inc(made, 1)


def over(ap, shape):
    return ap.to_broadcast(shape)


class Chain:

    def __init__(self, engine, sem):
        self.engine, self.sem, self.done = engine, sem, 0

    def __call__(self, instruction):
        instruction.then_inc(self.sem, 1)
        self.done += 1
        self.engine.wait_ge(self.sem, self.done)


def build(nc, x, w, b, norm_w, w_q, w_k, w_v, w_out, scorer_w, scorer_b, ffn_w, ffn_s, ffn_b, out):
    xv = x.rearrange("b (t p) c -> p b t c", p=P)
    q_dram = nc.dram_tensor("q_dram", [PARTS, P, BATCH, SEQ], BF16, kind="Internal").ap()
    k_dram = nc.dram_tensor("k_dram", [PARTS, PARTS, P, BATCH, SEQ], BF16, kind="Internal").ap()
    v_dram = nc.dram_tensor("v_dram", [BATCH, GROUPS, P, TILES * QUAD * 32], F32, kind="Internal").ap()
    o_dram = nc.dram_tensor("o_dram", [BATCH, GROUPS, P, SEQ], F32, kind="Internal").ap()

    with ExitStack() as whole:
        def keep(name, shape, dt):
            return whole.enter_context(nc.sbuf_tensor(name, shape, dt))

        PS = whole.enter_context(nc.psum_tensor("PS", [P, 8, BANK], F32))
        xs = keep("xs", [P, BATCH, TILES, DIM], F32)
        ident = keep("ident", [P, P], F32)
        identb = keep("identb", [P, P], BF16)
        causal = keep("causal", [P, P], BF16)

        project_a(nc, PS, xs, ident, identb, causal, xv, w, b, q_dram, k_dram, v_dram)
        attend_a(nc, PS, ident, identb, causal, q_dram, k_dram, v_dram, o_dram)
        gather_a(nc, PS, xs, ident, o_dram)
        ffn(nc, PS, xs, identb, ffn_w, ffn_s, ffn_b, None)
        attend_b(nc, PS, xs, ident, identb, causal, norm_w, w_q, w_k, w_v, w_out, scorer_w, scorer_b)
        ffn(nc, PS, xs, identb, ffn_w, ffn_s, ffn_b, out.rearrange("b (t p) c -> p b t c", p=P))


def project_a(nc, PS, xs, ident, identb, causal, xv, w, b, q_dram, k_dram, v_dram):
    with ExitStack() as ctx:
        def sb(name, shape, dt):
            return ctx.enter_context(nc.sbuf_tensor(name, shape, dt))

        def sem(name):
            return ctx.enter_context(nc.semaphore(name))

        wsb = sb("wsb", [P, 3, P], F32)
        wT = sb("wT", [P, 3, P], F32)
        bcol = sb("bcol", [P, 2], F32)
        bvrow = sb("bvrow", [P, P], F32)
        xc = sb("xc", [P, BATCH, TILES, DIM], F32)
        sq = sb("sq", [P, BATCH, TILES, DIM], F32)
        xn = sb("xn", [P, BATCH, TILES, DIM], F32)
        st = sb("st", [P, 4, BATCH, TILES], F32)
        hT = sb("hT", [P, BATCH, SEQ], F32)
        qk = sb("qk", [P, 2, BATCH, SEQ], F32)
        rest = sb("rest", [P, 2, BATCH, SEQ], F32)
        parts = sb("parts", [P, 2, PARTS, BATCH, SEQ], BF16)
        va = sb("va", [P, BATCH, GROUPS, TILES, QUAD, 32], F32)

        x_in = [sem(f"x_in{i}") for i in range(BATCH)]
        w_in = sem("w_in")
        id_made, idb_made, causal_made, va_made = sem("id_made"), sem("idb_made"), sem("causal_made"), sem("va_made")
        dve_chain = sem("dve_chain")
        centred, squared, varied, rooted, normed = (sem(n) for n in ("centred", "squared", "varied", "rooted", "normed"))
        wT_ready, wT_copied, hT_ready, hT_copied = (sem(n) for n in ("wT_ready", "wT_copied", "hT_ready", "hT_copied"))
        q_ready, q_taken, k_ready, k_taken, v_ready, v_taken = (
            sem(n) for n in ("q_ready", "q_taken", "k_ready", "k_taken", "v_ready", "v_taken"))
        hi_made = [sem("q_hi_made"), sem("k_hi_made")]
        rest_made = [sem("q_rest_made"), sem("k_rest_made")]
        lo_made = [sem("q_lo_made"), sem("k_lo_made")]
        parts_out, v_out = sem("parts_out"), sem("v_out")

        block = ctx.enter_context(nc.Block())

        @block.sync
        def _(sp):
            for i in range(BATCH):
                sp.dma_start(xs[:, i], xv[:, i]).then_inc(x_in[i], 16)
            sp.dma_start(wsb[:], w.rearrange("(r p) c -> p r c", p=P)).then_inc(w_in, 16)
            for r in range(2):
                sp.dma_start(bcol[:, r:r + 1], b[P * r:P * (r + 1)].rearrange("(h d) -> d h", d=HD_A)[:, :, None],
                             allow_slow_non_contiguous=True).then_inc(w_in, 16)
            sp.dma_start(bvrow[:], over(b[2 * P:3 * P][None], [P, P])).then_inc(w_in, 16)
            for i in range(BATCH):
                sp.wait_ge(hi_made[0], 2 * (i + 1))
                sp.wait_ge(lo_made[0], i + 1)
                sp.dma_start(q_dram[:, :, i].rearrange("c p t -> p c t"), parts[:, 0, :, i]).then_inc(parts_out, 16)
                sp.wait_ge(hi_made[1], 2 * (i + 1))
                sp.wait_ge(lo_made[1], i + 1)
                for a in range(PARTS):
                    sp.dma_start(k_dram[a, :, :, i].rearrange("c p t -> p c t"),
                                 over(parts[:, 1, a, i][:, None], [P, PARTS, SEQ])).then_inc(parts_out, 16)
                sp.wait_ge(v_taken, TILES * (i + 1))
                sp.dma_start(v_dram[i].rearrange("g p n -> p g n"),
                             va[:, i].rearrange("p g j h d -> p g (j h d)")).then_inc(v_out, 16)
            sp.wait_ge(parts_out, 16 * 8)
            sp.wait_ge(v_out, 32)

        @block.gpsimd
        def _(pool):
            make_identity(pool, ident, id_made)
            make_identity(pool, identb, idb_made)
            pool.memset(causal[:], 0.0).then_inc(causal_made, 1)
            pool.wait_ge(causal_made, 1)
            pool.affine_select(out=causal[:], in_=causal[:], compare_op=ALU.is_ge, fill=BIG, base=0,
                               pattern=[[-1, P]], channel_multiplier=1).then_inc(causal_made, 1)
            pool.memset(va[:], 0.0).then_inc(va_made, 1)
            pool.wait_ge(va_made, 1)
            pool.memset(va[:, :, :, :, :, HD_A:HD_A + 1], 1.0).then_inc(va_made, 1)
            for i in range(BATCH):
                pool.wait_ge(hi_made[1], 2 * i + 1)
                pool.tensor_tensor(rest[:, 1, i], qk[:, 1, i], parts[:, 1, 0, i], ALU.subtract).then_inc(rest_made[1], 1)
                pool.wait_ge(rest_made[1], i + 1)
                pool.wait_ge(hi_made[1], 2 * i + 2)
                pool.tensor_tensor(parts[:, 1, 2, i], rest[:, 1, i], parts[:, 1, 1, i], ALU.subtract).then_inc(lo_made[1], 1)

        @block.vector
        def _(dve):
            chain = Chain(dve, dve_chain)
            for i in range(BATCH):
                dve.wait_ge(x_in[i], 16)
                layer_norm(dve, chain, xs[:, i], xc[:, i], sq[:, i], xn[:, i], [st[:, k, i] for k in range(4)],
                           i, centred, squared, varied, rooted, normed)
            for i in range(BATCH):
                for k in range(2):
                    dve.wait_ge(q_ready, 2 * i + k + 1)
                    dve.tensor_scalar(qk[:, 0, i, BANK * k:BANK * (k + 1)], PS[:, 5, :], bcol[:, 0:1],
                                      float(HD_A) ** -0.5, ALU.add, ALU.mult).then_inc(q_taken, 1)
                dve.wait_ge(hi_made[0], 2 * i + 1)
                dve.tensor_tensor(rest[:, 0, i], qk[:, 0, i], parts[:, 0, 0, i], ALU.subtract).then_inc(rest_made[0], 1)
                if i == 0:
                    dve.wait_ge(va_made, 2)
                    dve.wait_ge(w_in, 64)
                for t in range(TILES):
                    if t % 4 == 0:
                        dve.wait_ge(v_ready, 2 * i + t // 4 + 1)
                    dve.tensor_tensor(va[:, i, :, t, :, 0:HD_A],
                                      PS[:, 7, P * (t % 4):P * (t % 4 + 1)].rearrange("p (g h d) -> p g h d", g=GROUPS, h=QUAD),
                                      bvrow[:].rearrange("p (g h d) -> p g h d", g=GROUPS, h=QUAD), ALU.add).then_inc(v_taken, 1)
                dve.wait_ge(rest_made[0], i + 1)
                dve.wait_ge(hi_made[0], 2 * i + 2)
                dve.tensor_tensor(parts[:, 0, 2, i], rest[:, 0, i], parts[:, 0, 1, i], ALU.subtract).then_inc(lo_made[0], 1)

        @block.scalar
        def _(act):
            act.wait_ge(wT_ready, 1)
            for r in range(2):
                act.activation(wT[:, r].rearrange("p (d h) -> p d h", d=HD_A),
                               PS[:, 0, P * r:P * (r + 1)].rearrange("p (h d) -> p d h", d=HD_A), ACT.Copy).then_inc(wT_copied, 1)
            act.activation(wT[:, 2], PS[:, 0, 2 * P:3 * P], ACT.Copy).then_inc(wT_copied, 1)
            act.wait_ge(w_in, 64)
            for i in range(BATCH):
                layer_norm_act(act, xc[:, i], sq[:, i], st[:, 2, i], i, centred, squared, varied, rooted)
            for i in range(BATCH):
                for k in range(2):
                    act.wait_ge(hT_ready, 2 * i + k + 1)
                    act.activation(hT[:, i, BANK * k:BANK * (k + 1)], PS[:, 1 + 2 * i + k, :], ACT.Copy).then_inc(hT_copied, 1)
            for i in range(BATCH):
                for k in range(2):
                    act.wait_ge(k_ready, 2 * i + k + 1)
                    act.activation(qk[:, 1, i, BANK * k:BANK * (k + 1)], PS[:, 6, :], ACT.Identity,
                                   bias=bcol[:, 1:2]).then_inc(k_taken, 1)
                for side, taken in ((1, k_taken), (0, q_taken)):
                    act.wait_ge(taken, 2 * (i + 1))
                    act.activation(parts[:, side, 0, i], qk[:, side, i], ACT.Copy).then_inc(hi_made[side], 1)
                for side in (1, 0):
                    act.wait_ge(rest_made[side], i + 1)
                    act.activation(parts[:, side, 1, i], rest[:, side, i], ACT.Copy).then_inc(hi_made[side], 1)

        @block.tensor
        def _(pe):
            pe.wait_ge(w_in, 64)
            pe.wait_ge(id_made, 2)
            for r in range(3):
                mm = pe.transpose(PS[:, 0, P * r:P * (r + 1)], wsb[:, r], ident[:])
            mm.then_inc(wT_ready, 1)
            for i in range(BATCH):
                pe.wait_ge(normed, i + 1)
                for t in range(TILES):
                    mm = pe.transpose(PS[:, 1 + 2 * i + t // 4, P * (t % 4):P * (t % 4 + 1)], xn[:, i, t], ident[:])
                    if t % 4 == 3:
                        mm.then_inc(hT_ready, 1)
            pe.wait_ge(wT_copied, 3)
            for i in range(BATCH):
                for k in range(2):
                    n = 2 * i + k
                    pe.wait_ge(hT_copied, n + 1)
                    pe.wait_ge(q_taken, n)
                    pe.matmul(PS[:, 5, :], wT[:, 0], hT[:, i, BANK * k:BANK * (k + 1)], start=True, stop=True).then_inc(q_ready, 1)
                    pe.wait_ge(k_taken, n)
                    pe.matmul(PS[:, 6, :], wT[:, 1], hT[:, i, BANK * k:BANK * (k + 1)], start=True, stop=True).then_inc(k_ready, 1)
                    pe.wait_ge(v_taken, 4 * n)
                    for t in range(4):
                        mm = pe.matmul(PS[:, 7, P * t:P * (t + 1)], hT[:, i, BANK * k + P * t:BANK * k + P * (t + 1)], wT[:, 2],
                                       start=True, stop=True)
                    mm.then_inc(v_ready, 1)


def layer_norm(dve, chain, src, xc, sq, dst, st, i, centred, squared, varied, rooted, normed):
    chain(dve.tensor_reduce(st[0], src, X, ALU.add))
    chain(dve.tensor_scalar(st[1], st[0], 1.0 / DIM, None, ALU.mult))
    dve.tensor_tensor(xc, src, over(st[1][:, :, None], [P, TILES, DIM]), ALU.subtract).then_inc(centred, 1)
    dve.wait_ge(squared, i + 1)
    chain(dve.tensor_reduce(st[3], sq, X, ALU.add))
    dve.tensor_scalar(st[2], st[3], 1.0 / DIM, 1e-5, ALU.mult, ALU.add).then_inc(varied, 1)
    dve.wait_ge(rooted, i + 1)
    chain(dve.reciprocal(st[0], st[2]))
    dve.tensor_tensor(dst, xc, over(st[0][:, :, None], [P, TILES, DIM]), ALU.mult).then_inc(normed, 1)


def layer_norm_act(act, xc, sq, var, i, centred, squared, varied, rooted):
    act.wait_ge(centred, i + 1)
    act.activation(sq, xc, ACT.Square).then_inc(squared, 1)
    act.wait_ge(varied, i + 1)
    act.activation(var, var, ACT.Sqrt).then_inc(rooted, 1)


def attend_a(nc, PS, ident, identb, causal, q_dram, k_dram, v_dram, o_dram):
    with ExitStack() as ctx:
        def sb(name, shape, dt):
            return ctx.enter_context(nc.sbuf_tensor(name, shape, dt))

        def sem(name):
            return ctx.enter_context(nc.semaphore(name))

        q1 = sb("q1", [P, 2, QUAD, SEQ], BF16)
        k1 = sb("k1", [P, 2, QUAD, SEQ], BF16)
        q2 = sb("q2", [P, 2, QUAD, SEQ], BF16)
        k2 = sb("k2", [P, 2, QUAD, SEQ], BF16)
        vb = sb("vb", [P, 2, TILES, QUAD, 32], F32)
        probs = sb("probs", [P, PROB_SLOTS, BANK], F32)
        ob = sb("ob", [P, 2, BANK], F32)
        neg = sb("neg", [P, 2, QUAD, TILES], F32)
        nrest = sb("nrest", [P, 2, QUAD, TILES], F32)
        nparts = sb("nparts", [P, 2, QUAD, PARTS, TILES], BF16)
        nT = sb("nT", [QUAD * PARTS * TILES, 2, P], BF16)

        ones_made = sem("ones_made")
        max_loaded = [sem(f"max_loaded{i}") for i in range(2)]
        prob_loaded = [sem(f"prob_loaded{i}") for i in range(2)]
        rows_loaded = [sem(f"rows_loaded{i}") for i in range(2)]
        max_scored, max_drained, neg_chain = sem("max_scored"), sem("max_drained"), sem("neg_chain")
        parts_ready = sem("parts_ready")
        scored, exped, masked, summed = sem("scored"), sem("exped"), sem("masked"), sem("summed")
        o_copied = sem("o_copied")
        sp_met, pool_met = sem("sp_met"), sem("pool_met")
        o_out = [sem(f"o_out{i}") for i in range(2)]

        block = ctx.enter_context(nc.Block())
        CREDIT = SCORE_BANKS
        MCREDIT = 2
        START = 1
        LOADS = (PARTS + 1) * 16

        q_rows = q_dram.rearrange("c (d h) b t -> (c d) h b t", h=HEADS_A)
        k_rows = k_dram.rearrange("a c (d h) b t -> (a c d) h b t", h=HEADS_A)

        def load_stacks(eng, i, par, qbuf, kbuf, done):
            for a in range(PARTS):
                n = PARTS * HD_A
                eng.dma_start(qbuf[n * a:n * (a + 1), par], q_rows[:, bass.ds(i * QUAD, QUAD), par]).then_inc(done, 16)
            eng.dma_start(kbuf[0:ROWS, par], k_rows[:, bass.ds(i * QUAD, QUAD), par]).then_inc(done, 16)

        def load_v(eng, i, par):
            eng.dma_start(vb[:, par].rearrange("p j h d -> p (j h d)"), v_dram[par, bass.ds(i, 1)].rearrange("g p n -> p (g n)")).then_inc(
                prob_loaded[par], 16)

        @block.sync
        def _(sp):
            for n in range(2):
                sp.sem_inc(o_out[n], 16 * START)
                sp.sem_inc(rows_loaded[n], 16 * START)
            sp.wait_ge(ones_made, 2)
            load_stacks(sp, 0, 0, q1, k1, max_loaded[0])
            sp.wait_ge(ones_made, 4)
            load_stacks(sp, 0, 0, q2, k2, prob_loaded[0])
            load_v(sp, 0, 0)
            load_stacks(sp, 0, 1, q1, k1, max_loaded[1])

            def load_rows(i, par):
                sp.wait_ge(parts_ready, i * 2 + par + 1)
                for h in range(QUAD):
                    n = PARTS * TILES
                    sp.dma_start(q2[ROWS:MROWS, par, h], nT[n * h:n * (h + 1), par]).then_inc(rows_loaded[par], 16)

            load_rows(0, 0)

            def step(i, par, more_max, more_prob):
                q = i * 2 + par
                if more_max:
                    sp.wait_ge(max_scored, q * MAX_SLOTS + MAX_SLOTS)
                    sp.sem_inc(sp_met, 1)
                    load_stacks(sp, i + 1, par, q1, k1, max_loaded[par])
                if more_prob:
                    sp.wait_ge(summed, q * NG + START)
                    sp.sem_inc(sp_met, 1)
                    load_stacks(sp, i + par, 1 - par, q2, k2, prob_loaded[1 - par])
                    load_v(sp, i + par, 1 - par)
                for c in range(2):
                    if c == 1 and more_prob:
                        load_rows(i + par, 1 - par)
                    sp.wait_ge(o_copied, q * 2 + c + 1 + START)
                    sp.sem_inc(sp_met, 1)
                    sp.dma_start(o_dram[par, bass.ds(i, 1), :, BANK * c:BANK * (c + 1)].rearrange("g p n -> p (g n)"),
                                 ob[:, c]).then_inc(o_out[c], 16)

            with sp.Fori(0, GROUPS - 1) as i:
                step(i, 0, True, True)
                step(i, 1, True, True)
            step(GROUPS - 1, 0, False, True)
            step(GROUPS - 1, 1, False, False)
            for c in range(2):
                sp.wait_ge(o_out[c], 16 * 2 * GROUPS + 16 * START)

        @block.gpsimd
        def _(pool):
            for n, (buf, value) in enumerate(((q1, 0.0), (k1, 0.0), (q2, 0.0), (k2, 1.0))):
                pool.memset(buf[64:P], value).then_inc(ones_made, 1)
                pool.wait_ge(ones_made, n + 1)
            zero = pool.to_reg(0.0)

            def step(i, par):
                for n, u in enumerate(MASKED):
                    g, h0, nh = PROB_UNITS[u]
                    w = PROB_GROUPS[g][3]
                    s = (NU * par + u) % PROB_SLOTS
                    pool.wait_ge(exped, i * (2 * NU) + NU * par + u + 1 + CREDIT)
                    pool.sem_inc(pool_met, 1)
                    v = probs[:, s, 0:nh * w].rearrange("p (h w) -> p h w", h=nh)[:, :, 0:P]
                    pool.affine_select(out=v, in_=v, compare_op=ALU.is_ge, fill=zero, base=0,
                                       pattern=[[0, nh], [1, P]], channel_multiplier=-1).then_inc(masked, 1)

            with pool.Fori(0, GROUPS - 1) as i:
                step(i, 0)
                step(i, 1)
            step(GROUPS - 1, 0)
            step(GROUPS - 1, 1)

        @block.vector
        def _(dve):
            dve.sem_inc(max_drained, MCREDIT)

            def maxima(i, par):
                q = i * 2 + par
                for k, (t, h0, nh) in enumerate(MAX_UNITS):
                    s = (MAX_SLOTS * par + k) % 2
                    w = P * (t + 1)
                    if w <= BANK:
                        per = min(nh, BANK // w) if t < 2 else 1
                        src = PS[:, 2 * s:2 * s + nh // per, 0:per * w]
                        src = src.rearrange("p b (h w) -> p (b h) w", w=w) if nh // per == 1 or per * w == BANK else src
                    else:
                        src = PS[:, 2 * s:2 * s + 2, :].rearrange("p b n -> p (b n)")[:, 0:w][:, None]
                    dve.wait_ge(max_scored, q * MAX_SLOTS + k + 1)
                    dve.tensor_reduce(neg[:, par, h0:h0 + nh, t], src, X, ALU.max, negate=True).then_inc(max_drained, 1)
                dve.wait_ge(max_drained, q * MAX_SLOTS + MAX_SLOTS - 1 + MCREDIT)
                np_ = nparts[:, par]
                dve.tensor_copy(np_[:, :, 0], neg[:, par]).then_inc(neg_chain, 1)
                dve.wait_ge(neg_chain, q * 4 + 1)
                dve.tensor_tensor(nrest[:, par], neg[:, par], np_[:, :, 0], ALU.subtract).then_inc(neg_chain, 1)
                dve.wait_ge(neg_chain, q * 4 + 2)
                dve.tensor_copy(np_[:, :, 1], nrest[:, par]).then_inc(neg_chain, 1)
                dve.wait_ge(neg_chain, q * 4 + 3)
                dve.tensor_tensor(np_[:, :, 2], nrest[:, par], np_[:, :, 1], ALU.subtract).then_inc(neg_chain, 1)
                s = (MAX_SLOTS * par + MAX_SLOTS - 1) % 2
                dve.wait_ge(max_scored, q * MAX_SLOTS + MAX_SLOTS)
                dve.wait_ge(rows_loaded[par], i * 64 + 16 * START)
                dve.tensor_copy(nT[:, par], PS[0:96, 2 * s, 0:P // 2].bitcast(BF16)).then_inc(parts_ready, 1)
                dve.wait_ge(parts_ready, q + 1)
                dve.sem_inc(max_drained, 1)

            maxima(0, 0)
            with dve.Fori(0, GROUPS - 1) as i:
                maxima(i, 1)
                maxima(i + 1, 0)
            maxima(GROUPS - 1, 1)

        @block.scalar
        def _(act):
            act.sem_inc(exped, CREDIT)
            act.sem_inc(o_copied, START)

            def step(i, par):
                q = i * 2 + par
                for u, (g, h0, nh) in enumerate(PROB_UNITS):
                    w = PROB_GROUPS[g][3]
                    at = NU * par + u
                    if at >= PROB_SLOTS:
                        act.wait_ge(summed, i * (2 * NG) + NG * ((at - PROB_SLOTS) // NU) + PROB_UNITS[(at - PROB_SLOTS) % NU][0] + 1 + START)
                    else:
                        act.wait_ge(summed, i * (2 * NG) + START)
                    act.wait_ge(scored, i * (2 * NU) + at + 1)
                    act.activation(probs[:, at % PROB_SLOTS, 0:nh * w], PS[:, 4 + at % SCORE_BANKS, 0:nh * w],
                                   ACT.Exp).then_inc(exped, 1)
                    if u == UNITS_OF[4][3]:
                        copy_out(i, par, 0)
                copy_out(i, par, 1)

            def copy_out(i, par, c):
                q = i * 2 + par
                act.wait_ge(o_out[c], q * 16 + 16 * START)
                act.wait_ge(summed, q * NG + (4 if c == 0 else NG) + START)
                act.activation(ob[:, c], PS[:, 7, :], ACT.Copy).then_inc(o_copied, 1)

            with act.Fori(0, GROUPS - 1) as i:
                step(i, 0)
                step(i, 1)
            step(GROUPS - 1, 0)
            step(GROUPS - 1, 1)

        @block.tensor
        def _(pe):
            pe.sem_inc(summed, START)

            def maximum(i, par, k):
                q = i * 2 + par
                s = (MAX_SLOTS * par + k) % 2
                if k == 0:
                    pe.wait_ge(max_loaded[par], (i + 1) * LOADS)
                pe.wait_ge(max_drained, q * MAX_SLOTS + k - 1 + MCREDIT)
                if k == MAX_SLOTS - 1:
                    pe.wait_ge(neg_chain, q * 4 + 4)
                    pe.transpose(PS[0:96, 2 * s, 0:P // 2].bitcast(BF16),
                                 nparts[:, par].rearrange("p h c t -> p (h c t)"), identb[:]).then_inc(max_scored, 1)
                    return
                t, h0, nh = MAX_UNITS[k]
                w = P * (t + 1)
                for n in range(nh):
                    h = h0 + n
                    if w <= BANK:
                        per = BANK // w if t < 2 else 1
                        pieces = [(2 * s + n // per, (n % per) * w, 0, w)]
                    else:
                        pieces = [(2 * s, 0, 0, BANK), (2 * s + 1, 0, BANK, w - BANK)]
                    for bank, at, s0, ws in pieces:
                        last = s0 + ws == w
                        mm = pe.matmul(PS[:, bank, at:at + ws], q1[:, par, h, P * t:P * (t + 1)],
                                       k1[:, par, h, s0:s0 + ws], start=True, stop=not last)
                        if last:
                            mm = pe.matmul(PS[:, bank, at + ws - P:at + ws], identb[:], causal[:], start=False, stop=True)
                mm.then_inc(max_scored, 1)

            def score(i, par, u):
                g, h0, nh = PROB_UNITS[u]
                c, j, lo, w, _ = PROB_GROUPS[g]
                at = NU * par + u
                if u == 0:
                    pe.wait_ge(prob_loaded[par], (i + 1) * (LOADS + 16))
                    pe.wait_ge(rows_loaded[par], (i + 1) * 64 + 16 * START)
                pe.wait_ge(exped, i * (2 * NU) + last_in_bank(at) + 1 + CREDIT)
                for n in range(nh):
                    mm = pe.matmul(PS[:, 4 + at % SCORE_BANKS, n * w:(n + 1) * w], k2[:, par, h0 + n, P * j:P * (j + 1)],
                                   q2[:, par, h0 + n, lo:lo + w], start=True, stop=True)
                mm.then_inc(scored, 1)

            def weigh(i, par, g):
                q = i * 2 + par
                c, j, lo, w, per = PROB_GROUPS[g]
                last = UNITS_OF[g][-1]
                if DIAG[g]:
                    pe.wait_ge(masked, q * len(MASKED) + MASKED.index(last) + 1)
                else:
                    pe.wait_ge(exped, q * NU + last + 1 + CREDIT)
                if j == 0:
                    pe.wait_ge(o_copied, q * 2 + c + START)
                for h in range(QUAD):
                    u = UNITS_OF[g][h // per]
                    s = (NU * par + u) % PROB_SLOTS
                    mm = pe.matmul(PS[32 * h:32 * (h + 1), 7, lo - BANK * c:BANK], vb[:, par, j, h],
                                   probs[:, s, (h % per) * w:(h % per + 1) * w], start=j == 0, stop=j == 4 * c + 3)
                mm.then_inc(summed, 1)

            def step(i, par, ahead):
                i1, par1 = (i, 1) if par == 0 else (i + 1, 0)
                for what, n in STEP:
                    if what == "score":
                        score(i, par, n)
                    elif what == "weigh":
                        weigh(i, par, n)
                    elif ahead:
                        maximum(i1, par1, n)

            for k in range(MAX_SLOTS):
                maximum(0, 0, k)
            with pe.Fori(0, GROUPS - 1) as i:
                step(i, 0, True)
                step(i, 1, True)
            step(GROUPS - 1, 0, True)
            step(GROUPS - 1, 1, False)


def gather_a(nc, PS, xs, ident, o_dram):
    with ExitStack() as ctx:
        def sb(name, shape, dt):
            return ctx.enter_context(nc.sbuf_tensor(name, shape, dt))

        def sem(name):
            return ctx.enter_context(nc.semaphore(name))

        oT = sb("oT", [P, BATCH, GROUPS, SEQ], F32)
        y = sb("y", [P, BATCH, TILES, DIM], F32)
        inv = sb("inv", [P, NT, HEADS_A], F32)
        o_in = [sem(f"o_in{i}") for i in range(BATCH)]
        turned, inverted, scaled, added = sem("turned"), sem("inverted"), sem("scaled"), sem("added")
        block = ctx.enter_context(nc.Block())

        @block.sync
        def _(sp):
            for i in range(BATCH):
                sp.dma_start(oT[:, i], o_dram[i].rearrange("g p n -> p g n")).then_inc(o_in[i], 16)

        @block.tensor
        def _(pe):
            for i in range(BATCH):
                pe.wait_ge(o_in[i], 16)
                for t in range(TILES):
                    n = i * TILES + t
                    if n >= 8:
                        pe.wait_ge(scaled, n - 7)
                    for g in range(GROUPS):
                        mm = pe.transpose(PS[:, n % 8, P * g:P * (g + 1)], oT[:, i, g, P * t:P * (t + 1)], ident[:])
                    mm.then_inc(turned, 1)

        @block.vector
        def _(dve):
            for n in range(NT):
                bank = PS[:, n % 8, :].rearrange("p (h d) -> p h d", d=32)
                dve.wait_ge(turned, n + 1)
                dve.reciprocal(inv[:, n], bank[:, :, HD_A]).then_inc(inverted, 1)
                dve.wait_ge(inverted, n + 1)
                dve.tensor_tensor(y[:, n // TILES, n % TILES].rearrange("p (h d) -> p h d", d=HD_A), bank[:, :, 0:HD_A],
                                  over(inv[:, n, :, None], [P, HEADS_A, HD_A]), ALU.mult).then_inc(scaled, 1)

        @block.gpsimd
        def _(pool):
            for n in range(NT):
                pool.wait_ge(scaled, n + 1)
                i, t = n // TILES, n % TILES
                pool.tensor_tensor(xs[:, i, t], xs[:, i, t], y[:, i, t], ALU.add).then_inc(added, 1)


def ffn(nc, PS, xs, identb, wq, ws, wb, out):
    with ExitStack() as ctx:
        def sb(name, shape, dt):
            return ctx.enter_context(nc.sbuf_tensor(name + ("_2" if out is not None else "_1"), shape, dt))

        def sem(name):
            return ctx.enter_context(nc.semaphore(name + ("_2" if out is not None else "_1")))

        shape = [P, BATCH, TILES, DIM]
        w64 = sb("w64", [P, P, 2], I32)
        wbf = sb("wbf", [P, P], BF16)
        wqT = sb("wqT", [P, P], BF16)
        wsrow = sb("wsrow", [P, P], F32)
        brow = sb("brow", [P, P], F32)
        xc, sq, xn = sb("fxc", shape, F32), sb("fsq", shape, F32), sb("fxn", shape, F32)
        st = sb("fst", [P, 4, BATCH, TILES], F32)
        amax = sb("amax", [P, 4, BATCH, TILES], F32)
        xq = sb("xq", shape, BF16)
        xqT = sb("xqT", [P, BATCH, SEQ], BF16)
        acc = sb("acc", shape, F32)

        w_in = sem("fw_in")
        dve_chain = sem("fdve_chain")
        centred, squared, varied, rooted, normed = (sem(n) for n in ("fcentred", "fsquared", "fvaried", "frooted", "fnormed"))
        w_cast, w_turned, w_copied = sem("w_cast"), sem("w_turned"), sem("w_copied")
        divided, clipped, rounded = sem("divided"), sem("clipped"), sem("rounded")
        turned, copied, multiplied, rescaled = sem("fturned"), sem("fcopied"), sem("multiplied"), sem("rescaled")
        biased, weighted, added, stored = sem("biased"), sem("weighted"), sem("fadded"), sem("fstored")
        block = ctx.enter_context(nc.Block())

        @block.sync
        def _(sp):
            sp.dma_start(w64[:].rearrange("p c w -> p (c w)"), wq.bitcast(I32)).then_inc(w_in, 16)
            sp.dma_start(wsrow[:], over(ws[None], [P, P])).then_inc(w_in, 16)
            sp.dma_start(brow[:], over(wb[None], [P, P])).then_inc(w_in, 16)
            if out is not None:
                for i in range(BATCH):
                    sp.wait_ge(added, i + 1)
                    sp.dma_start(out[:, i], xs[:, i]).then_inc(stored, 16)
                sp.wait_ge(stored, 16 * BATCH)

        @block.vector
        def _(dve):
            chain = Chain(dve, dve_chain)
            for i in range(BATCH):
                layer_norm(dve, chain, xs[:, i], xc[:, i], sq[:, i], xn[:, i], [st[:, k, i] for k in range(4)],
                           i, centred, squared, varied, rooted, normed)
                dve.wait_ge(normed, i + 1)
                chain(dve.tensor_reduce(amax[:, 0, i], xn[:, i], X, ALU.max, apply_absolute_value=True))
                chain(dve.tensor_scalar(amax[:, 2, i], amax[:, 0, i], 1e-6, 1.0 / 127.0, ALU.max, ALU.mult))
                chain(dve.reciprocal(amax[:, 3, i], amax[:, 2, i]))
                dve.tensor_tensor(xc[:, i], xn[:, i], over(amax[:, 3, i, :, None], [P, TILES, DIM]), ALU.mult).then_inc(divided, 1)
                dve.wait_ge(clipped, i + 1)
                dve.tensor_scalar(xq[:, i], xc[:, i], MAGIC, MAGIC, ALU.add, ALU.subtract).then_inc(rounded, 1)
            for i in range(BATCH):
                dve.wait_ge(w_in, 48)
                dve.wait_ge(rescaled, TILES * (i + 1))
                dve.tensor_tensor(xn[:, i], acc[:, i], over(wsrow[:, None], [P, TILES, P]), ALU.mult).then_inc(weighted, 1)
                dve.wait_ge(weighted, i + 1)
                dve.wait_ge(biased, i + 1)
                dve.tensor_tensor(xs[:, i], xs[:, i], xn[:, i], ALU.add).then_inc(added, 1)

        @block.gpsimd
        def _(pool):
            for i in range(BATCH):
                pool.wait_ge(divided, i + 1)
                pool.tensor_scalar(xc[:, i], xc[:, i], 127.0, -128.0, ALU.min, ALU.max).then_inc(clipped, 1)
            for i in range(BATCH):
                pool.wait_ge(w_in, 48)
                pool.tensor_tensor(xs[:, i], xs[:, i], over(brow[:, None], [P, TILES, P]), ALU.add).then_inc(biased, 1)

        @block.scalar
        def _(act):
            act.wait_ge(w_in, 48)
            act.activation(wbf[:], w64[:, :, 0], ACT.Copy).then_inc(w_cast, 1)
            for i in range(BATCH):
                layer_norm_act(act, xc[:, i], sq[:, i], st[:, 2, i], i, centred, squared, varied, rooted)
                if i == 0:
                    act.wait_ge(w_turned, 1)
                    act.activation(wqT[:], PS[:, 6, 0:P // 2].bitcast(BF16), ACT.Copy).then_inc(w_copied, 1)
            for i in range(BATCH):
                act.wait_ge(turned, i + 1)
                act.activation(xqT[:, i], PS[:, i].bitcast(BF16), ACT.Copy).then_inc(copied, 1)
                for t in range(TILES):
                    if t % 4 == 0:
                        act.wait_ge(multiplied, 2 * i + t // 4 + 1)
                    act.activation(acc[:, i, t], PS[:, 2 + 2 * i + t // 4, P * (t % 4):P * (t % 4 + 1)], ACT.Copy,
                                   scale=amax[:, 2, i, t:t + 1]).then_inc(rescaled, 1)

        @block.tensor
        def _(pe):
            pe.wait_ge(w_cast, 1)
            pe.transpose(PS[:, 6, 0:P // 2].bitcast(BF16), wbf[:], identb[:]).then_inc(w_turned, 1)
            for i in range(BATCH):
                pe.wait_ge(rounded, i + 1)
                for t in range(TILES):
                    mm = pe.transpose(PS[:, i, P // 2 * t:P // 2 * (t + 1)].bitcast(BF16), xq[:, i, t], identb[:])
                mm.then_inc(turned, 1)
            pe.wait_ge(w_copied, 1)
            for i in range(BATCH):
                pe.wait_ge(copied, i + 1)
                for t in range(TILES):
                    mm = pe.matmul(PS[:, 2 + 2 * i + t // 4, P * (t % 4):P * (t % 4 + 1)], xqT[:, i, P * t:P * (t + 1)], wqT[:],
                                   start=True, stop=True)
                    if t % 4 == 3:
                        mm.then_inc(multiplied, 1)


def attend_b(nc, PS, xs, ident, identb, causal, norm_w, w_q, w_k, w_v, w_out, scorer_w, scorer_b):
    with ExitStack() as ctx:
        def sb(name, shape, dt):
            return ctx.enter_context(nc.sbuf_tensor(name, shape, dt))

        wq = sb("wq", [P, HEADS_B * HD_B], F32)
        wk = sb("wk", [P, HEADS_B * HD_B], F32)
        wv = sb("wv", [P, HEADS_B * HD_B], F32)
        wo = sb("wo", [P, PAIRS, DIM], F32)
        hT = sb("bhT", [P, BATCH, SEQ], F32)
        masks = sb("masks", [P, BATCH, TILES, KEYS], BF16)
        kT = sb("kT", [P, 2, PAIRS, KEYS], F32)
        vg = sb("vg", [P, BATCH, HEADS_B // 4, 4, HD_B + 1], F32)
        pick_b(nc, PS, xs, ident, causal, norm_w, w_q, w_k, w_v, w_out, scorer_w, scorer_b, wq, wk, wv, wo, hT, masks, kT, vg)
        windows_b(nc, PS, xs, ident, identb, wq, wk, wv, wo, hT, masks, kT, vg)


def pick_b(nc, PS, xs, ident, causal, norm_w, w_q, w_k, w_v, w_out, scorer_w, scorer_b, wq, wk, wv, wo, hT, masks, kT, vg):
    with ExitStack() as ctx:
        def sb(name, shape, dt):
            return ctx.enter_context(nc.sbuf_tensor(name, shape, dt))

        def sem(name):
            return ctx.enter_context(nc.semaphore(name))

        shape = [P, BATCH, TILES, DIM]
        xc, sq, xn, hn = sb("bxc", shape, F32), sb("bsq", shape, F32), sb("bxn", shape, F32), sb("bhn", shape, F32)
        st = sb("bst", [P, 4, BATCH, TILES], F32)
        st2 = sb("bst2", [P, 4, BATCH, TILES], F32)
        nw = sb("nw", [P, 1], F32)
        scw = sb("scw", [P, BATCH, BATCH], F32)
        scb = sb("scb", [BATCH, 1], F32)
        scores = sb("scores", [BATCH, SEQ], F32)
        left = sb("left", [BATCH, 2, SEQ], F32)
        top = sb("top", [BATCH, PICKED], F32)
        index = sb("index", [BATCH, PICKED], U32)
        indexf = sb("indexf", [BATCH, PICKED], F32)
        rows = sb("rows", [BATCH, BATCH, P], F32)
        picked = sb("picked", [P, BATCH, PICKED], F32)
        token = sb("token", [P, TILES], F32)
        onehot = sb("onehot", [P, BATCH, TILES, PICKED], F32)
        later = sb("later", [P, BATCH, TILES, PICKED], F32)
        hg = sb("hg", [P, BATCH, 4, PICKED], F32)

        w_in, s_in = sem("bw_in"), sem("bs_in")
        dve_chain, dve_chain2 = sem("bdve_chain"), sem("bdve_chain2")
        centred, squared, varied, rooted, normed = (sem(n) for n in ("bcentred", "bsquared", "bvaried", "brooted", "bnormed"))
        squared2, varied2, rooted2, rmsed = (sem(n) for n in ("bsquared2", "bvaried2", "brooted2", "rmsed"))
        summed, turned, copied = sem("bsummed"), sem("bturned"), sem("bcopied")
        scored, biased, indexed, spread, spread_copied = sem("bscored"), sem("bbiased"), sem("indexed"), sem("spread"), sem("spread_copied")
        consts, onehots, masked = sem("consts"), sem("onehots"), sem("bmasked")
        gathered, hg_copied, kg_ready, kg_copied, vg_ready, vg_copied = (
            sem(n) for n in ("gathered", "hg_copied", "kg_ready", "kg_copied", "vg_ready", "vg_copied"))
        causal_copied, vg_zeroed, scw_zeroed = sem("causal_copied"), sem("vg_zeroed"), sem("scw_zeroed")
        block = ctx.enter_context(nc.Block())

        @block.sync
        def _(sp):
            sp.dma_start(nw[:], norm_w[:, None], allow_slow_non_contiguous=True).then_inc(s_in, 16)
            sp.dma_start(scb[:], over(scorer_b[None], [BATCH, 1]), allow_slow_non_contiguous=True).then_inc(s_in, 16)
            sp.wait_ge(scw_zeroed, 1)
            for i in range(BATCH):
                sp.dma_start(scw[:, i, i:i + 1], scorer_w, allow_slow_non_contiguous=True).then_inc(s_in, 16)
            for dst, src in ((wk, w_k), (wv, w_v), (wq, w_q)):
                sp.dma_start(dst[:], src).then_inc(w_in, 16)
            sp.dma_start(wo[:], w_out.rearrange("(r p) n -> p r n", p=P)).then_inc(w_in, 16)
            sp.wait_ge(w_in, 64)

        @block.gpsimd
        def _(pool):
            pool.memset(scw[:], 0.0).then_inc(scw_zeroed, 1)
            pool.memset(vg[:], 0.0).then_inc(vg_zeroed, 1)
            pool.iota(token[:], [[P, TILES]], base=0, channel_multiplier=1, allow_small_or_imprecise_dtypes=True).then_inc(consts, 1)
            pool.memset(rows[:], 0.0).then_inc(consts, 1)
            pool.wait_ge(consts, 2)
            pool.affine_select(out=rows[:], in_=rows[:], compare_op=ALU.not_equal, fill=1.0, base=0,
                               pattern=[[-1, BATCH], [0, P]], channel_multiplier=1).then_inc(consts, 1)
            for i in range(BATCH):
                pool.tensor_copy(masks[:, i, :, 0:P], over(causal[:, None], [P, TILES, P])).then_inc(causal_copied, 1)
            for i in range(BATCH):
                pool.wait_ge(normed, i + 1)
                pool.tensor_tensor(xs[:, i], xs[:, i], xn[:, i], ALU.add).then_inc(summed, 1)

        @block.vector
        def _(dve):
            chain = Chain(dve, dve_chain)
            for i in range(BATCH):
                layer_norm(dve, chain, xs[:, i], xc[:, i], sq[:, i], xn[:, i], [st[:, k, i] for k in range(4)],
                           i, centred, squared, varied, rooted, normed)
                dve.wait_ge(squared2, i + 1)
                chain(dve.tensor_reduce(st2[:, 3, i], sq[:, i], X, ALU.add))
                dve.tensor_scalar(st2[:, 2, i], st2[:, 3, i], 1.0 / DIM, 1e-6, ALU.mult, ALU.add).then_inc(varied2, 1)
                dve.wait_ge(rooted2, i + 1)
                chain(dve.reciprocal(st2[:, 0, i], st2[:, 2, i]))
                dve.tensor_tensor(hn[:, i], xn[:, i], over(st2[:, 0, i, :, None], [P, TILES, DIM]), ALU.mult).then_inc(rmsed, 1)
            dve.wait_ge(s_in, 64)
            dve.wait_ge(scored, 1)
            chain(dve.tensor_scalar(scores[:], PS[0:BATCH, 4:6, :].rearrange("p b n -> p (b n)"), scb[:, 0:1], None, ALU.add))
            src = scores[:]
            for r in range(PICKED // 8):
                chain(dve.max(top[:, 8 * r:8 * r + 8], src))
                chain(dve.max_index(index[:, 8 * r:8 * r + 8], top[:, 8 * r:8 * r + 8], src))
                if r < PICKED // 8 - 1:
                    chain(dve.match_replace(left[:, r % 2], top[:, 8 * r:8 * r + 8], src, -3.0e38))
                    src = left[:, r % 2]
            dve.tensor_copy(indexf[:], index[:]).then_inc(indexed, 1)
            dve.wait_ge(spread, 1)
            dve.tensor_copy(picked[:], PS[:, 6, 0:BATCH * PICKED].rearrange("p (b g) -> p b g", b=BATCH)).then_inc(spread_copied, 1)
            dve.wait_ge(spread_copied, 1)
            dve.wait_ge(consts, 3)
            for i in range(BATCH):
                at = over(picked[:, i][:, None], [P, TILES, PICKED])
                own = over(token[:, :, None], [P, TILES, PICKED])
                dve.tensor_tensor(onehot[:, i], at, own, ALU.is_equal).then_inc(onehots, 1)
                chain(dve.tensor_tensor(later[:, i], at, own, ALU.is_gt))
                dve.tensor_scalar(masks[:, i, :, P:KEYS], later[:, i], BIG, None, ALU.mult).then_inc(masked, 1)
            dve.wait_ge(kg_ready, 1)
            for i in range(BATCH):
                dve.tensor_copy(kT[:, i, :, P:KEYS], PS[:, 0].rearrange("p (r b g) -> p r b g", r=PAIRS, b=BATCH)[:, :, i]).then_inc(kg_copied, 1)
            dve.wait_ge(vg_zeroed, 1)
            for r in range(4):
                dve.memset(vg[32 * r:32 * (r + 1), :, :, r, HD_B:HD_B + 1], 1.0).then_inc(vg_copied, 1)
            for i in range(BATCH):
                dve.wait_ge(vg_ready, i + 1)
                for r in range(4):
                    src = PS[32 * r:32 * (r + 1), 2 + 2 * i:4 + 2 * i, :].rearrange("p b n -> p (b n)").rearrange(
                        "p (g r d) -> p g r d", g=HEADS_B // 4, r=4)[:, :, r]
                    dve.tensor_copy(vg[32 * r:32 * (r + 1), i, :, r, 0:HD_B], src).then_inc(vg_copied, 1)

        @block.scalar
        def _(act):
            for i in range(BATCH):
                layer_norm_act(act, xc[:, i], sq[:, i], st[:, 2, i], i, centred, squared, varied, rooted)
                act.wait_ge(normed, i + 1)
                act.activation(sq[:, i], xn[:, i], ACT.Square).then_inc(squared2, 1)
                act.wait_ge(varied2, i + 1)
                act.activation(st2[:, 2, i], st2[:, 2, i], ACT.Sqrt).then_inc(rooted2, 1)
            act.wait_ge(s_in, 64)
            for i in range(BATCH):
                for k in range(2):
                    act.wait_ge(turned, 2 * i + k + 1)
                    act.activation(hT[:, i, BANK * k:BANK * (k + 1)], PS[:, 2 * i + k, :], ACT.Copy, scale=nw[:, 0:1]).then_inc(copied, 1)
            for i in range(BATCH):
                act.wait_ge(gathered, i + 1)
                act.activation(hg[:, i], over(PS[:, 7, PICKED * i:PICKED * (i + 1)][:, None], [P, 4, PICKED]), ACT.Copy,
                               scale=nw[:, 0:1]).then_inc(hg_copied, 1)

        @block.tensor
        def _(pe):
            for i in range(BATCH):
                pe.wait_ge(rmsed, i + 1)
                for t in range(TILES):
                    mm = pe.transpose(PS[:, 2 * i + t // 4, P * (t % 4):P * (t % 4 + 1)], hn[:, i, t], ident[:])
                    if t % 4 == 3:
                        mm.then_inc(turned, 1)
            pe.wait_ge(copied, 4)
            for k in range(2):
                for i in range(BATCH):
                    mm = pe.matmul(PS[0:BATCH, 4 + k, :], scw[:, i], hT[:, i, BANK * k:BANK * (k + 1)], start=i == 0, stop=i == BATCH - 1)
            mm.then_inc(scored, 1)
            pe.wait_ge(indexed, 1)
            pe.wait_ge(consts, 3)
            for i in range(BATCH):
                mm = pe.matmul(PS[:, 6, PICKED * i:PICKED * (i + 1)], rows[:, i], indexf[:], start=True, stop=True)
            mm.then_inc(spread, 1)
            for i in range(BATCH):
                pe.wait_ge(onehots, i + 1)
                if i:
                    pe.wait_ge(hg_copied, i)
                for t in range(TILES):
                    mm = pe.matmul(PS[:, 7, PICKED * i:PICKED * (i + 1)], hn[:, i, t], onehot[:, i, t], start=t == 0, stop=t == TILES - 1)
                mm.then_inc(gathered, 1)
            pe.wait_ge(hg_copied, BATCH)
            pe.wait_ge(w_in, 64)
            for r in range(PAIRS):
                mm = pe.matmul(PS[:, 0, BATCH * PICKED * r:BATCH * PICKED * (r + 1)], wk[:, P * r:P * (r + 1)], hg[:, :, 0], start=True, stop=True)
            mm.then_inc(kg_ready, 1)
            for i in range(BATCH):
                if i == 1:
                    pe.wait_ge(spread_copied, 1)
                for k in range(2):
                    mm = pe.matmul(PS[:, 2 + 2 * i + k, :], hg[:, i].rearrange("p r g -> p (r g)"), wv[:, BANK * k:BANK * (k + 1)],
                                   start=True, stop=True)
                mm.then_inc(vg_ready, 1)


def windows_b(nc, PS, xs, ident, identb, wq, wk, wv, wo, hT, masks, kT, vg):
    with ExitStack() as ctx:
        def sb(name, shape, dt):
            return ctx.enter_context(nc.sbuf_tensor(name, shape, dt))

        def sem(name):
            return ctx.enter_context(nc.semaphore(name))

        hw = sb("hw", [P, 2, P], F32)
        mw = sb("mw", [P, 2, KEYS], BF16)
        qT = sb("qT", [P, 2, PAIRS, P], F32)
        vw = sb("vw", [P, 2, HEADS_B, HD_B + 1], F32)
        nmax = sb("nmax", [P, 2, HEADS_B], F32)
        pr = sb("pr", [P, 2, HEADS_B, KEYS], F32)
        prg = sb("prg", [P, 2, HEADS_B, PICKED], F32)
        pT = sb("pT", [P, HEADS_B, P], F32)
        pgT = sb("pgT", [P, 4, P], F32)
        inv = sb("binv", [P, 2, HEADS_B], F32)
        o = sb("o", [P, HEADS_B, HD_B], F32)
        oT = sb("boT", [P, PAIRS, P], F32)

        h_in = [sem(f"h_in{i}") for i in range(2)]
        m_in = [sem(f"m_in{i}") for i in range(2)]
        v_ones = sem("v_ones")
        t_ready, t_taken = sem("t_ready"), sem("t_taken")
        s_ready, s_maxed, s_taken, exped = sem("s_ready"), sem("s_maxed"), sem("s_taken"), sem("bexped")
        o_ready, o_inv, o_taken = sem("o_ready"), sem("o_inv"), sem("o_taken")
        sp_met = sem("bsp_met")
        block = ctx.enter_context(nc.Block())

        UNITS = [(0, 6), (6, 6), (12, 4)]
        STEP = ["pg", "p0", "s0", "p1", "w0", "s1", "p2", "w1", "p3", "s2", "w2", "w3",
                "q0", "q1", "o0", "k0", "k1", "o1", "v0", "v1", "out"]
        PROJECTIONS = ["q0", "q1", "k0", "k1", "v0", "v1"]
        ITEMS = [name for name in STEP if name[0] in "pqkv" or name in ("o0", "o1")]
        LAST_ITEMS = [name for name in ITEMS if name not in PROJECTIONS]
        NTI, T0 = len(ITEMS), 2 * len(PROJECTIONS)
        NO = 5
        OC = 2

        def last(i):
            return isinstance(i, int) and i == TILES - 1

        def t_index(i, par, name):
            if last(i):
                return T0 + (i * 2) * NTI + par * len(LAST_ITEMS) + LAST_ITEMS.index(name)
            return T0 + (i * 2 + par) * NTI + ITEMS.index(name)

        def bank_of(par, name, first):
            return (t_index(0, par, name) if first is None else first) % 2

        @block.sync
        def _(sp):
            def load(i, par):
                sp.dma_start(hw[:, par], hT[:, par, bass.ds(i * P, P)]).then_inc(h_in[par], 16)
                sp.dma_start(mw[:, par], masks[:, par, bass.ds(i, 1)].rearrange("p o k -> p (o k)")).then_inc(m_in[par], 16)

            load(0, 0)
            load(0, 1)

            def step(i):
                for par in range(2):
                    sp.wait_ge(t_ready, t_index(i, par, "pg") + 1)
                    sp.sem_inc(sp_met, 1)
                    sp.wait_ge(s_ready, (i * 2 + par) * 3 + 3)
                    sp.sem_inc(sp_met, 1)
                    load(i + 1, par)

            with sp.Fori(0, TILES - 1) as i:
                step(i)

        @block.gpsimd
        def _(pool):
            pool.memset(vw[:, :, :, HD_B:HD_B + 1], 1.0).then_inc(v_ones, 1)

        @block.vector
        def _(dve):
            dve.sem_inc(o_taken, OC)

            def softmax(i, par, u, first=False):
                n = (i * 2 + par) * 3 + u
                h0, nh = UNITS[u]
                s = 2 * ((3 * par + u) % 2)
                per = nh // 2
                full = PS[:, s:s + 2, 0:KEYS * per].rearrange("p b (h k) -> p b h k", h=per)
                mx = nmax[:, par, h0:h0 + nh].rearrange("p (h b) -> p b h", b=2)
                dve.wait_ge(s_ready, n + 1)
                dve.tensor_reduce(mx, full, X, ALU.max).then_inc(s_maxed, 1)
                if u == 0 and not first:
                    dve.wait_ge(t_ready, T0 + (i * 2 + par - 1) * NTI)
                dve.wait_ge(s_maxed, n + 1)
                for b in range(2):
                    ins = dve.tensor_tensor(pr[:, par, h0 + b:h0 + nh:2], full[:, b], over(mx[:, b][:, :, None], [P, per, KEYS]),
                                            ALU.subtract)
                ins.then_inc(s_taken, 1)

            def values(i, par, g):
                n = i * 2 + par
                bank = PS[:, 6 + (NO * par + g) % 2, 0:4 * (HD_B + 1)].rearrange("p (h d) -> p h d", h=4)
                dve.wait_ge(o_ready, n * NO + g + 1 + OC)
                dve.reciprocal(inv[:, par, 4 * g:4 * g + 4], bank[:, :, HD_B]).then_inc(o_inv, 1)
                if g == 0:
                    dve.wait_ge(t_ready, t_index(i, par, "pg"))
                dve.wait_ge(o_inv, n * 4 + g + 1)
                dve.tensor_tensor(o[:, 4 * g:4 * g + 4], bank[:, :, 0:HD_B], over(inv[:, par, 4 * g:4 * g + 4, None], [P, 4, HD_B]),
                                  ALU.mult).then_inc(o_taken, 1)

            def output(i, par):
                n = i * 2 + par
                tile = xs[:, par, bass.ds(i, 1)].rearrange("p o c -> p (o c)")
                dve.wait_ge(o_ready, n * NO + NO + OC)
                dve.tensor_tensor(tile, tile, PS[:, 6 + (NO * par + 4) % 2, 0:DIM], ALU.add).then_inc(o_taken, 1)

            def step(i, par, ahead=True):
                i1, par1 = (i, 1) if par == 0 else (i + 1, 0)
                for name in ("s0", "w0", "s1", "w1", "s2", "w2", "w3"):
                    if name[0] == "w":
                        values(i, par, int(name[1]))
                    elif ahead:
                        softmax(i1, par1, int(name[1]))
                output(i, par)

            for u in range(3):
                softmax(0, 0, u, first=True)
            with dve.Fori(0, TILES - 1) as i:
                step(i, 0)
                step(i, 1)
            step(TILES - 1, 0)
            step(TILES - 1, 1, ahead=False)

        @block.scalar
        def _(act):
            def take(i, par, name, first=None):
                n = i * 2 + par
                index = t_index(i, par, name) if first is None else first
                bank = PS[:, 4 + bank_of(par, name, first), :]
                four = bank.rearrange("p (r t) -> p r t", r=4)
                act.wait_ge(t_ready, index + 1)
                k = int(name[-1]) if name != "pg" else 0
                if name == "q0" and first is None:
                    act.wait_ge(s_ready, n * 3 + 3)
                if name == "v0" and first is None:
                    act.wait_ge(o_ready, n * NO + 4 + OC)
                if name[0] == "q":
                    ins = act.activation(qT[:, par, 4 * k:4 * k + 4], four, ACT.Copy, scale=float(HD_B) ** -0.5)
                elif name[0] == "k":
                    ins = act.activation(kT[:, par, 4 * k:4 * k + 4, 0:P], four, ACT.Copy)
                elif name[0] == "v":
                    ins = act.activation(vw[:, par, 8 * k:8 * k + 8, 0:HD_B], bank.rearrange("p (h d) -> p h d", d=HD_B), ACT.Copy)
                elif name == "pg":
                    act.wait_ge(o_ready, n * NO + OC)
                    ins = act.activation(pgT[:], four, ACT.Copy)
                elif name[0] == "p":
                    ins = act.activation(pT[:, 4 * k:4 * k + 4], four, ACT.Copy)
                else:
                    ins = act.activation(oT[:, 4 * k:4 * k + 4], four, ACT.Copy)
                ins.then_inc(t_taken, 1)

            def exponential(i, par, name):
                u = 2 if name == "eg" else int(name[1])
                h0, nh = UNITS[u]
                act.wait_ge(s_taken, (i * 2 + par) * 3 + u + 1)
                if name == "eg":
                    act.activation(prg[:, par], pr[:, par, :, P:KEYS], ACT.Exp).then_inc(exped, 1)
                else:
                    v = pr[:, par, h0:h0 + nh, 0:P]
                    act.activation(v, v, ACT.Exp).then_inc(exped, 1)

            ORDER = ["pg", "p0", "p1", "e0", "p2", "p3", "e1", "q0", "e2", "q1", "o0", "k0", "eg", "k1", "o1", "v0", "v1"]

            def step(i, par, ahead=True):
                i1, par1 = (i, 1) if par == 0 else (i + 1, 0)
                for name in ORDER:
                    if name[0] == "e":
                        if ahead:
                            exponential(i1, par1, name)
                    elif name not in PROJECTIONS or not last(i):
                        take(i, par, name)

            for k, name in enumerate(PROJECTIONS):
                take(0, 0, name, first=k)
            exponential(0, 0, "e0")
            exponential(0, 0, "e1")
            for k, name in enumerate(PROJECTIONS):
                take(0, 1, name, first=len(PROJECTIONS) + k)
            exponential(0, 0, "e2")
            exponential(0, 0, "eg")
            with act.Fori(0, TILES - 1) as i:
                step(i, 0)
                step(i, 1)
            step(TILES - 1, 0)
            step(TILES - 1, 1, ahead=False)

        @block.tensor
        def _(pe):
            pe.sem_inc(o_ready, OC)

            def item(i, par, name, first=None):
                if first is None or first >= 2:
                    pe.wait_ge(t_taken, (t_index(i, par, name) if first is None else first) - 1)
                return PS[:, 4 + bank_of(par, name, first), :]

            def project(i, par, name, first=None):
                bank, k = item(i, par, name, first), int(name[1])
                if name[0] == "v":
                    mm = pe.matmul(bank, hw[:, par], wv[:, BANK * k:BANK * (k + 1)], start=True, stop=True)
                else:
                    for r in range(4):
                        c = P * (4 * k + r)
                        mm = pe.matmul(bank[:, P * r:P * (r + 1)], (wq if name[0] == "q" else wk)[:, c:c + P], hw[:, par],
                                       start=True, stop=True)
                mm.then_inc(t_ready, 1)

            def scores(i, par, u, first=False):
                n = (i * 2 + par) * 3 + u
                h0, nh = UNITS[u]
                s = 2 * ((3 * par + u) % 2)
                if u == 0:
                    pe.wait_ge(t_taken, len(PROJECTIONS) if first else T0 + (i * 2 + par - 1) * NTI)
                    pe.wait_ge(m_in[par], (i + 1) * 16)
                if not (first and u < 2):
                    pe.wait_ge(s_taken, n - 1)
                per = nh // 2
                for k in range(per):
                    for b in range(2):
                        lo = HD_B * b
                        pe.matmul(PS[:, s + b, KEYS * k:KEYS * (k + 1)], qT[lo:lo + HD_B, par, h0 // 2 + k],
                                  kT[lo:lo + HD_B, par, h0 // 2 + k], start=k == 0, stop=False, skip_group_check=True)
                for b in range(2):
                    mm = pe.matmul(PS[:, s + b, 0:KEYS * per], identb[:], over(mw[:, par][:, None], [P, per, KEYS]),
                                   start=False, stop=True, skip_group_check=True)
                mm.then_inc(s_ready, 1)

            def turn_probs(i, par, name):
                bank = item(i, par, name)
                if name == "pg":
                    pe.wait_ge(exped, (i * 2 + par) * 4 + 4)
                for r in range(4):
                    if name == "pg":
                        src = prg[:, par, 4 * r:4 * r + 4].rearrange("p h g -> p (h g)")
                    else:
                        src = pr[:, par, 4 * int(name[1]) + r, 0:P]
                    mm = pe.transpose(bank[:, P * r:P * (r + 1)], src, ident[:])
                mm.then_inc(t_ready, 1)

            def weigh(i, par, g):
                n = i * 2 + par
                bank = PS[:, 6 + (NO * par + g) % 2, 0:4 * (HD_B + 1)]
                pe.wait_ge(o_taken, n * NO + g - 1 + OC)
                pe.wait_ge(t_taken, t_index(i, par, f"p{g}") + 1)
                pe.matmul(bank, pgT[:, g], vg[:, par, g].rearrange("p h d -> p (h d)"), start=True, stop=False, skip_group_check=True)
                for r in range(4):
                    h = 4 * g + r
                    mm = pe.matmul(bank[:, (HD_B + 1) * r:(HD_B + 1) * (r + 1)], pT[:, h], vw[:, par, h], start=False, stop=r == 3,
                                   skip_group_check=True)
                mm.then_inc(o_ready, 1)

            def turn_values(i, par, k):
                n = i * 2 + par
                bank = item(i, par, f"o{k}")
                pe.wait_ge(o_taken, n * NO + 2 * k + 2 + OC)
                for r in range(4):
                    e = 2 * (4 * k + r)
                    mm = pe.transpose(bank[:, P * r:P * (r + 1)], o[:, e:e + 2].rearrange("p h d -> p (h d)"), ident[:])
                mm.then_inc(t_ready, 1)

            def output(i, par):
                n = i * 2 + par
                pe.wait_ge(t_taken, t_index(i, par, "o1") + 1)
                bank = PS[:, 6 + (NO * par + 4) % 2, 0:DIM]
                pe.wait_ge(o_taken, n * NO + 4 - 1 + OC)
                for r in range(PAIRS):
                    mm = pe.matmul(bank, oT[:, r], wo[:, r], start=r == 0, stop=r == PAIRS - 1)
                mm.then_inc(o_ready, 1)

            def step(i, par, ahead=True):
                i1, par1 = (i, 1) if par == 0 else (i + 1, 0)
                for name in STEP:
                    if name[0] == "s":
                        if ahead:
                            scores(i1, par1, int(name[1]))
                    elif name[0] == "w":
                        weigh(i, par, int(name[1]))
                    elif name[0] == "p":
                        turn_probs(i, par, name)
                    elif name == "out":
                        output(i, par)
                    elif name[0] == "o":
                        turn_values(i, par, int(name[1]))
                    elif not last(i):
                        if name == "q0":
                            pe.wait_ge(h_in[par], (i + 2) * 16)
                        project(i, par, name)

            pe.wait_ge(v_ones, 1)
            pe.wait_ge(h_in[0], 16)
            for k, name in enumerate(PROJECTIONS):
                project(0, 0, name, first=k)
            scores(0, 0, 0, first=True)
            scores(0, 0, 1, first=True)
            pe.wait_ge(h_in[1], 16)
            for k, name in enumerate(PROJECTIONS):
                project(0, 1, name, first=len(PROJECTIONS) + k)
            scores(0, 0, 2, first=True)
            with pe.Fori(0, TILES - 1) as i:
                step(i, 0)
                step(i, 1)
            step(TILES - 1, 0)
            step(TILES - 1, 1, ahead=False)


_INS = ["L0_attn_a_x", "L0_attn_a_W", "L0_attn_a_b", "L0_attn_b_norm_w", "L0_attn_b_w_q", "L0_attn_b_w_k", "L0_attn_b_w_v",
        "L0_attn_b_w_out", "L0_attn_b_scorer_w", "L0_attn_b_scorer_b", "L0_ffn_weight_q", "L0_ffn_weight_scale",
        "L0_ffn_bias"]


def kernel(**inputs):
    import numpy as _np
    import concourse.bacc as _bacc
    from concourse import mybir as _mybir
    from concourse.bass_utils import run_bass_kernel_spmd as _run

    nc = _bacc.Bacc("TRN2", target_bir_lowering=False, num_devices=1)
    arrays, args = {}, []
    for name in _INS:
        a = _np.ascontiguousarray(inputs[name])
        if a.dtype.kind in "iu":
            a = a.astype(_np.int64)
        arrays[f"in_{name}_dram"] = a
        args.append(nc.dram_tensor(f"in_{name}_dram", a.shape, _mybir.dt.from_np(a.dtype), kind="ExternalInput").ap())
    args.append(nc.dram_tensor("out_dram", (BATCH, SEQ, DIM), F32, kind="ExternalOutput").ap())
    build(nc, *args)
    return _run(nc, [arrays], core_ids=[0]).results[0]["out_dram"]
```

```python
from contextlib import ExitStack

import concourse.bass as bass
from concourse import mybir

F32 = mybir.dt.float32
BF16 = mybir.dt.bfloat16
I32 = mybir.dt.int32
U32 = mybir.dt.uint32
ALU = mybir.AluOpType
ACT = mybir.ActivationFunctionType
X = mybir.AxisListType.X

P = 128
BATCH, SEQ, DIM = 2, 1024, 128
TILES = SEQ // P
NT = BATCH * TILES
BANK = 512

HEADS_A, HD_A = 16, 8
QUAD = 4
GROUPS = HEADS_A // QUAD
PARTS = 3
ROWS = PARTS * PARTS * HD_A
MROWS = ROWS + PARTS
BIG = -1.0e30
MAGIC = 1.5 * 2.0 ** 23

HEADS_B, HD_B = 16, 64
PAIRS = HEADS_B // 2
PICKED = 32
KEYS = P + PICKED

MAX_UNITS = []
for _t in range(TILES):
    _n = QUAD if _t < 2 else (2 if _t < 4 else 1)
    MAX_UNITS += [(_t, h, _n) for h in range(0, QUAD, _n)]
MAX_SLOTS = len(MAX_UNITS) + 1

PROB_GROUPS = []
for _c in range(SEQ // BANK):
    for _j in range(4 * (_c + 1)):
        _lo = max(BANK * _c, P * _j)
        _w = BANK * (_c + 1) - _lo
        PROB_GROUPS.append((_c, _j, _lo, _w, max(1, min(QUAD, BANK // _w))))
PROB_UNITS = []
for _g, (_c, _j, _lo, _w, _n) in enumerate(PROB_GROUPS):
    PROB_UNITS += [(_g, h, _n) for h in range(0, QUAD, _n)]
NG, NU = len(PROB_GROUPS), len(PROB_UNITS)
DIAG = [_j * P >= BANK * _c for _c, _j, *_ in PROB_GROUPS]
UNITS_OF = [[u for u, x in enumerate(PROB_UNITS) if x[0] == g] for g in range(NG)]
MASKED = [u for u, x in enumerate(PROB_UNITS) if DIAG[x[0]]]


def order_of_step():
    cols = [(PROB_GROUPS[g][3]) * n for g, _, n in PROB_UNITS]
    total, at, items, done = sum(cols), 0, [], []
    for u, c in enumerate(cols):
        items.append((at / total + SCORE_LAG, 0, "score", u))
        at += c
        done.append(at / total)
    for g in range(NG):
        items.append((done[UNITS_OF[g][-1]] + SCORE_LAG + WEIGH_LAG, 1, "weigh", g))
    widths = [P * (t + 1) * n for t, _, n in MAX_UNITS]
    for k in range(MAX_SLOTS):
        at = (sum(widths[:k]) - sum(widths[:MAX_AHEAD])) / sum(widths) + (1 if k < MAX_AHEAD else 0)
        at = at * MAX_SHARE + (TURN_LAG if k == len(MAX_UNITS) or k < MAX_AHEAD else 0)
        items.append((at, 2 if k == len(MAX_UNITS) else 3, "max", k))
    return [(what, n) for _, _, what, n in sorted(items)]


SCORE_LAG = 0.04
WEIGH_LAG = 0.1
TURN_LAG = 0.08
MAX_AHEAD = 3
MAX_SHARE = 1 - TURN_LAG
STEP = order_of_step()
PROB_SLOTS = NU // 2
SCORE_BANKS = 3


def last_in_bank(u):
    bank = u % SCORE_BANKS
    if u >= SCORE_BANKS:
        return u - SCORE_BANKS
    return max(v for v in range(2 * NU) if v % SCORE_BANKS == bank) - 2 * NU


def make_identity(pool, tile, made):
    pool.memset(tile[:], 0.0).then_inc(made, 1)
    pool.wait_ge(made, 1)
    pool.affine_select(out=tile[:], in_=tile[:], compare_op=ALU.not_equal, fill=1.0, base=0,
                       pattern=[[-1, P]], channel_multiplier=1).then_inc(made, 1)


def over(ap, shape):
    return ap.to_broadcast(shape)


class Chain:

    def __init__(self, engine, sem):
        self.engine, self.sem, self.done = engine, sem, 0

    def __call__(self, *instructions):
        for instruction in instructions:
            instruction.then_inc(self.sem, 1)
            self.done += 1
        self.engine.wait_ge(self.sem, self.done)


def build(nc, x, w, b, norm_w, w_q, w_k, w_v, w_out, scorer_w, scorer_b, ffn_w, ffn_s, ffn_b, out):
    xv = x.rearrange("b (t p) c -> p b t c", p=P)
    q_dram = nc.dram_tensor("q_dram", [PARTS, P, BATCH, SEQ], BF16, kind="Internal").ap()
    k_dram = nc.dram_tensor("k_dram", [PARTS, PARTS, P, BATCH, SEQ], BF16, kind="Internal").ap()
    o_dram = nc.dram_tensor("o_dram", [BATCH, GROUPS, P, SEQ], F32, kind="Internal").ap()

    with ExitStack() as whole:
        def keep(name, shape, dt):
            return whole.enter_context(nc.sbuf_tensor(name, shape, dt))

        PS = whole.enter_context(nc.psum_tensor("PS", [P, 8, BANK], F32))
        xs = keep("xs", [P, BATCH, TILES, DIM], F32)
        ident = keep("ident", [P, P], F32)
        identb = keep("identb", [P, P], BF16)
        causal = keep("causal", [P, P], BF16)

        with ExitStack() as ctx:
            def sb(name, shape, dt):
                return ctx.enter_context(nc.sbuf_tensor(name, shape, dt))

            stacks = [sb(name, [P, 2, QUAD, SEQ], BF16) for name in ("q1", "k1", "q2", "k2")]
            parts = sb("parts", [P, 2, PARTS, BATCH, SEQ], BF16)
            va = sb("va", [P, BATCH, GROUPS, TILES, QUAD, 32], F32)
            parts_out = [ctx.enter_context(nc.semaphore(f"parts_out{i}")) for i in range(BATCH)]
            max_loaded = [ctx.enter_context(nc.semaphore(f"max_loaded{i}")) for i in range(2)]
            project_a(nc, PS, xs, ident, identb, causal, xv, w, b, q_dram, k_dram, stacks, parts, va, parts_out, max_loaded)
            attend_a(nc, PS, ident, identb, causal, q_dram, k_dram, o_dram, stacks, va, parts_out, max_loaded)
        gather_a(nc, PS, xs, ident, o_dram)
        ffn(nc, PS, xs, identb, ffn_w, ffn_s, ffn_b, None)
        attend_b(nc, PS, xs, ident, identb, causal, norm_w, w_q, w_k, w_v, w_out, scorer_w, scorer_b)
        ffn(nc, PS, xs, identb, ffn_w, ffn_s, ffn_b, out.rearrange("b (t p) c -> p b t c", p=P))


def load_stacks(eng, i, par, q_dram, k_dram, qbuf, kbuf, done):
    q_rows = q_dram.rearrange("c (d h) b t -> (c d) h b t", h=HEADS_A)
    k_rows = k_dram.rearrange("a c (d h) b t -> (a c d) h b t", h=HEADS_A)
    for a in range(PARTS):
        n = PARTS * HD_A
        eng.dma_start(qbuf[n * a:n * (a + 1), par], q_rows[:, bass.ds(i * QUAD, QUAD), par]).then_inc(done, 16)
    eng.dma_start(kbuf[0:ROWS, par], k_rows[:, bass.ds(i * QUAD, QUAD), par]).then_inc(done, 16)


def project_a(nc, PS, xs, ident, identb, causal, xv, w, b, q_dram, k_dram, stacks, parts, va, parts_out, max_loaded):
    with ExitStack() as ctx:
        def sb(name, shape, dt):
            return ctx.enter_context(nc.sbuf_tensor(name, shape, dt))

        def sem(name):
            return ctx.enter_context(nc.semaphore(name))

        wsb = sb("wsb", [P, 3, P], F32)
        wT = sb("wT", [P, 3, P], F32)
        bcol = sb("bcol", [P, 2], F32)
        bvrow = sb("bvrow", [P, P], F32)
        xc = sb("xc", [P, BATCH, TILES, DIM], F32)
        xn = sb("xn", [P, BATCH, TILES, DIM], F32)
        raw = sb("raw", [P, BATCH, TILES, 6], F32)
        mv = sb("mv", [P, BATCH, TILES, 2], F32)
        root = sb("root", [P, BATCH, TILES], F32)
        rstd = sb("rstd", [P, BATCH, TILES], F32)
        hT = sb("hT", [P, BATCH, SEQ], F32)
        qk = sb("qk", [P, 2, BATCH, SEQ], F32)
        rest = sb("rest", [P, 2, BATCH, SEQ], F32)

        x_in = [sem(f"x_in{i}") for i in range(BATCH)]
        w_in = sem("w_in")
        id_made, idb_made, causal_made, va_made = sem("id_made"), sem("idb_made"), sem("causal_made"), sem("va_made")
        dve_chain = sem("dve_chain")
        varied, rooted, normed = sem("varied"), sem("rooted"), sem("normed")
        wT_ready, wT_copied, hT_ready, hT_copied = (sem(n) for n in ("wT_ready", "wT_copied", "hT_ready", "hT_copied"))
        q_ready, q_taken, k_ready, k_taken, v_ready, v_taken = (
            sem(n) for n in ("q_ready", "q_taken", "k_ready", "k_taken", "v_ready", "v_taken"))
        hi_made = [sem("q_hi_made"), sem("k_hi_made")]
        rest_made = [sem("q_rest_made"), sem("k_rest_made")]
        lo_made = [sem("q_lo_made"), sem("k_lo_made")]
        ones_made, filled = sem("ones_made"), sem("filled")
        q_banks, k_banks, v_banks = (5, 1), (6, 2), (7, 3)

        block = ctx.enter_context(nc.Block())

        @block.sync
        def _(sp):
            for i in range(BATCH):
                sp.dma_start(xs[:, i], xv[:, i]).then_inc(x_in[i], 16)
            sp.dma_start(wsb[:], w.rearrange("(r p) c -> p r c", p=P)).then_inc(w_in, 16)
            for r in range(2):
                sp.dma_start(bcol[:, r:r + 1], b[P * r:P * (r + 1)].rearrange("(h d) -> d h", d=HD_A)[:, :, None],
                             allow_slow_non_contiguous=True).then_inc(w_in, 16)
            sp.dma_start(bvrow[:], over(b[2 * P:3 * P][None], [P, P])).then_inc(w_in, 16)
            for i in range(BATCH):
                sp.wait_ge(hi_made[0], 2 * (i + 1))
                sp.wait_ge(lo_made[0], i + 1)
                sp.dma_start(q_dram[:, :, i].rearrange("c p t -> p c t"), parts[:, 0, :, i]).then_inc(parts_out[i], 16)
                sp.wait_ge(hi_made[1], 2 * (i + 1))
                sp.wait_ge(lo_made[1], i + 1)
                for a in range(PARTS):
                    sp.dma_start(k_dram[a, :, :, i].rearrange("c p t -> p c t"),
                                 over(parts[:, 1, a, i][:, None], [P, PARTS, SEQ])).then_inc(parts_out[i], 16)
                if i == 0:
                    sp.wait_ge(parts_out[0], 64)
                    sp.wait_ge(ones_made, 2)
                    load_stacks(sp, 0, 0, q_dram, k_dram, stacks[0], stacks[1], max_loaded[0])

        @block.gpsimd
        def _(pool):
            make_identity(pool, ident, id_made)
            make_identity(pool, identb, idb_made)
            pool.memset(causal[:], 0.0).then_inc(causal_made, 1)
            pool.wait_ge(causal_made, 1)
            pool.affine_select(out=causal[:], in_=causal[:], compare_op=ALU.is_ge, fill=BIG, base=0,
                               pattern=[[-1, P]], channel_multiplier=1).then_inc(causal_made, 1)
            pool.memset(va[:], 0.0).then_inc(va_made, 1)
            pool.wait_ge(va_made, 1)
            pool.memset(va[:, :, :, :, :, HD_A:HD_A + 1], 1.0).then_inc(va_made, 1)
            pool.wait_ge(va_made, 2)

            for n in range(2):
                pool.memset(stacks[n][64:P], 0.0).then_inc(ones_made, 1)
                pool.wait_ge(ones_made, n + 1)
            for i in range(BATCH):
                pool.wait_ge(hi_made[1], 2 * i + 1)
                pool.tensor_tensor(rest[:, 1, i], qk[:, 1, i], parts[:, 1, 0, i], ALU.subtract).then_inc(rest_made[1], 1)
                pool.wait_ge(rest_made[1], i + 1)
                pool.wait_ge(hi_made[1], 2 * i + 2)
                pool.tensor_tensor(parts[:, 1, 2, i], rest[:, 1, i], parts[:, 1, 1, i], ALU.subtract).then_inc(lo_made[1], 1)

        @block.vector
        def _(dve):
            chain = Chain(dve, dve_chain)
            dve.memset(stacks[2][64:P], 0.0).then_inc(filled, 1)
            for i in range(BATCH):
                dve.wait_ge(x_in[i], 16)
                moments(dve, chain, xs[:, i], raw[:, i], mv[:, i])
                dve.tensor_scalar(root[:, i], mv[:, i, :, 1], 1e-5, None, ALU.add).then_inc(varied, 1)
                centre = dve.tensor_tensor(xc[:, i], xs[:, i], per_row(mv[:, i, :, 0]), ALU.subtract)
                chain(centre)
                dve.wait_ge(rooted, i + 1)
                chain(dve.reciprocal(rstd[:, i], root[:, i]))
                dve.tensor_tensor(xn[:, i], xc[:, i], per_row(rstd[:, i]), ALU.mult).then_inc(normed, 1)
            for i in range(BATCH):
                for k in range(2):
                    dve.wait_ge(q_ready, 2 * i + k + 1)
                    dve.tensor_scalar(qk[:, 0, i, BANK * k:BANK * (k + 1)], PS[:, q_banks[k], :], bcol[:, 0:1],
                                      float(HD_A) ** -0.5, ALU.add, ALU.mult).then_inc(q_taken, 1)
                dve.wait_ge(hi_made[0], 2 * i + 1)
                dve.tensor_tensor(rest[:, 0, i], qk[:, 0, i], parts[:, 0, 0, i], ALU.subtract).then_inc(rest_made[0], 1)
                if i == 0:
                    dve.wait_ge(va_made, 2)
                    dve.wait_ge(w_in, 64)
                for t in range(TILES):
                    if t % 4 == 0:
                        dve.wait_ge(v_ready, 2 * i + t // 4 + 1)
                    dve.tensor_tensor(va[:, i, :, t, :, 0:HD_A],
                                      PS[:, v_banks[t // 4], P * (t % 4):P * (t % 4 + 1)].rearrange("p (g h d) -> p g h d", g=GROUPS, h=QUAD),
                                      bvrow[:].rearrange("p (g h d) -> p g h d", g=GROUPS, h=QUAD), ALU.add).then_inc(v_taken, 1)
                dve.wait_ge(rest_made[0], i + 1)
                dve.wait_ge(hi_made[0], 2 * i + 2)
                dve.tensor_tensor(parts[:, 0, 2, i], rest[:, 0, i], parts[:, 0, 1, i], ALU.subtract).then_inc(lo_made[0], 1)
            dve.memset(stacks[3][64:P], 1.0).then_inc(filled, 1)

        @block.scalar
        def _(act):
            act.wait_ge(wT_ready, 1)
            for r in range(2):
                act.activation(wT[:, r].rearrange("p (d h) -> p d h", d=HD_A),
                               PS[:, 0, P * r:P * (r + 1)].rearrange("p (h d) -> p d h", d=HD_A), ACT.Copy).then_inc(wT_copied, 1)
            act.activation(wT[:, 2], PS[:, 0, 2 * P:3 * P], ACT.Copy).then_inc(wT_copied, 1)
            act.wait_ge(w_in, 64)
            for i in range(BATCH):
                act.wait_ge(varied, i + 1)
                act.activation(root[:, i], root[:, i], ACT.Sqrt).then_inc(rooted, 1)
            for i in range(BATCH):
                for k in range(2):
                    act.wait_ge(hT_ready, 2 * i + k + 1)
                    act.activation(hT[:, i, BANK * k:BANK * (k + 1)], PS[:, 1 + 2 * i + k, :], ACT.Copy).then_inc(hT_copied, 1)
            for i in range(BATCH):
                for k in range(2):
                    act.wait_ge(k_ready, 2 * i + k + 1)
                    act.activation(qk[:, 1, i, BANK * k:BANK * (k + 1)], PS[:, k_banks[k], :], ACT.Identity,
                                   bias=bcol[:, 1:2]).then_inc(k_taken, 1)
                for side, taken in ((1, k_taken), (0, q_taken)):
                    act.wait_ge(taken, 2 * (i + 1))
                    act.activation(parts[:, side, 0, i], qk[:, side, i], ACT.Copy).then_inc(hi_made[side], 1)
                for side in (1, 0):
                    act.wait_ge(rest_made[side], i + 1)
                    act.activation(parts[:, side, 1, i], rest[:, side, i], ACT.Copy).then_inc(hi_made[side], 1)

        @block.tensor
        def _(pe):
            pe.wait_ge(w_in, 64)
            pe.wait_ge(id_made, 2)
            for r in range(3):
                mm = pe.transpose(PS[:, 0, P * r:P * (r + 1)], wsb[:, r], ident[:])
            mm.then_inc(wT_ready, 1)
            for i in range(BATCH):
                pe.wait_ge(normed, i + 1)
                for t in range(TILES):
                    mm = pe.transpose(PS[:, 1 + 2 * i + t // 4, P * (t % 4):P * (t % 4 + 1)], xn[:, i, t], ident[:])
                    if t % 4 == 3:
                        mm.then_inc(hT_ready, 1)
            pe.wait_ge(wT_copied, 3)
            for i in range(BATCH):
                for k in range(2):
                    n = 2 * i + k
                    pe.wait_ge(hT_copied, 1 if n == 0 else 4)
                    if n >= 2:
                        pe.wait_ge(q_taken, n - 1)
                    pe.matmul(PS[:, q_banks[k], :], wT[:, 0], hT[:, i, BANK * k:BANK * (k + 1)], start=True, stop=True).then_inc(q_ready, 1)
                    if n >= 2:
                        pe.wait_ge(k_taken, n - 1)
                    pe.matmul(PS[:, k_banks[k], :], wT[:, 1], hT[:, i, BANK * k:BANK * (k + 1)], start=True, stop=True).then_inc(k_ready, 1)
                    if n >= 2:
                        pe.wait_ge(v_taken, 4 * (n - 1))
                    for t in range(4):
                        mm = pe.matmul(PS[:, v_banks[k], P * t:P * (t + 1)], hT[:, i, BANK * k + P * t:BANK * k + P * (t + 1)], wT[:, 2],
                                       start=True, stop=True)
                    mm.then_inc(v_ready, 1)


def moments(dve, chain, src, raw, mv):
    chain(*[dve.bn_stats(raw[:, t], src[:, t]) for t in range(TILES)])
    chain(*[dve.bn_aggr(mv[:, t], raw[:, t]) for t in range(TILES)])


def per_row(values):
    return over(values[:, :, None], [P, TILES, DIM])


def attend_a(nc, PS, ident, identb, causal, q_dram, k_dram, o_dram, stacks, va, parts_out, max_loaded):
    with ExitStack() as ctx:
        def sb(name, shape, dt):
            return ctx.enter_context(nc.sbuf_tensor(name, shape, dt))

        def sem(name):
            return ctx.enter_context(nc.semaphore(name))

        q1, k1, q2, k2 = stacks
        vb = sb("vb", [P, 2, TILES, QUAD, 32], F32)
        probs = sb("probs", [P, PROB_SLOTS, BANK], F32)
        ob = sb("ob", [P, 2, BANK], F32)
        neg = sb("neg", [P, 2, QUAD, TILES], F32)
        nrest = sb("nrest", [P, 2, QUAD, TILES], F32)
        nparts = sb("nparts", [P, 2, QUAD, PARTS, TILES], BF16)
        nT = sb("nT", [QUAD * PARTS * TILES, 2, P], BF16)

        prob_loaded = [sem(f"prob_loaded{i}") for i in range(2)]
        rows_loaded = [sem(f"rows_loaded{i}") for i in range(2)]
        max_scored, max_drained, neg_chain = sem("max_scored"), sem("max_drained"), sem("neg_chain")
        parts_ready = sem("parts_ready")
        scored, exped, masked, summed = sem("scored"), sem("exped"), sem("masked"), sem("summed")
        o_copied = sem("o_copied")
        sp_met, pool_met = sem("sp_met"), sem("pool_met")
        o_out = [sem(f"o_out{i}") for i in range(2)]

        block = ctx.enter_context(nc.Block())
        CREDIT = SCORE_BANKS
        MCREDIT = 2
        START = 1
        LOADS = (PARTS + 1) * 16

        def load_v(eng, i, par):
            eng.dma_start(vb[:, par].rearrange("p j h d -> p (j h d)"),
                          va[:, par, bass.ds(i, 1)].rearrange("p g j h d -> p (g j h d)")).then_inc(prob_loaded[par], 16)

        @block.sync
        def _(sp):
            for n in range(2):
                sp.sem_inc(o_out[n], 16 * START)
                sp.sem_inc(rows_loaded[n], 16 * START)
            load_stacks(sp, 0, 0, q_dram, k_dram, q2, k2, prob_loaded[0])
            load_v(sp, 0, 0)
            sp.wait_ge(parts_out[1], 64)
            load_stacks(sp, 0, 1, q_dram, k_dram, q1, k1, max_loaded[1])

            def load_rows(i, par):
                sp.wait_ge(parts_ready, i * 2 + par + 1)
                for h in range(QUAD):
                    n = PARTS * TILES
                    sp.dma_start(q2[ROWS:MROWS, par, h], nT[n * h:n * (h + 1), par]).then_inc(rows_loaded[par], 16)

            load_rows(0, 0)

            def step(i, par, more_max, more_prob):
                q = i * 2 + par
                if more_max:
                    sp.wait_ge(max_scored, q * MAX_SLOTS + MAX_SLOTS)
                    sp.sem_inc(sp_met, 1)
                    load_stacks(sp, i + 1, par, q_dram, k_dram, q1, k1, max_loaded[par])
                if more_prob:
                    sp.wait_ge(summed, q * NG + START)
                    sp.sem_inc(sp_met, 1)
                    load_stacks(sp, i + par, 1 - par, q_dram, k_dram, q2, k2, prob_loaded[1 - par])
                    load_v(sp, i + par, 1 - par)
                for c in range(2):
                    if c == 1 and more_prob:
                        load_rows(i + par, 1 - par)
                    sp.wait_ge(o_copied, q * 2 + c + 1 + START)
                    sp.sem_inc(sp_met, 1)
                    sp.dma_start(o_dram[par, bass.ds(i, 1), :, BANK * c:BANK * (c + 1)].rearrange("g p n -> p (g n)"),
                                 ob[:, c]).then_inc(o_out[c], 16)

            with sp.Fori(0, GROUPS - 1) as i:
                step(i, 0, True, True)
                step(i, 1, True, True)
            step(GROUPS - 1, 0, False, True)
            step(GROUPS - 1, 1, False, False)
            for c in range(2):
                sp.wait_ge(o_out[c], 16 * 2 * GROUPS + 16 * START)

        @block.gpsimd
        def _(pool):
            zero = pool.to_reg(0.0)

            def step(i, par):
                for n, u in enumerate(MASKED):
                    g, h0, nh = PROB_UNITS[u]
                    w = PROB_GROUPS[g][3]
                    s = (NU * par + u) % PROB_SLOTS
                    pool.wait_ge(exped, i * (2 * NU) + NU * par + u + 1 + CREDIT)
                    pool.sem_inc(pool_met, 1)
                    v = probs[:, s, 0:nh * w].rearrange("p (h w) -> p h w", h=nh)[:, :, 0:P]
                    pool.affine_select(out=v, in_=v, compare_op=ALU.is_ge, fill=zero, base=0,
                                       pattern=[[0, nh], [1, P]], channel_multiplier=-1).then_inc(masked, 1)

            with pool.Fori(0, GROUPS - 1) as i:
                step(i, 0)
                step(i, 1)
            step(GROUPS - 1, 0)
            step(GROUPS - 1, 1)

        @block.vector
        def _(dve):
            dve.sem_inc(max_drained, MCREDIT)

            def maxima(i, par):
                q = i * 2 + par
                for k, (t, h0, nh) in enumerate(MAX_UNITS):
                    s = (MAX_SLOTS * par + k) % 2
                    w = P * (t + 1)
                    if w <= BANK:
                        per = min(nh, BANK // w) if t < 2 else 1
                        src = PS[:, 2 * s:2 * s + nh // per, 0:per * w]
                        src = src.rearrange("p b (h w) -> p (b h) w", w=w) if nh // per == 1 or per * w == BANK else src
                    else:
                        src = PS[:, 2 * s:2 * s + 2, :].rearrange("p b n -> p (b n)")[:, 0:w][:, None]
                    dve.wait_ge(max_scored, q * MAX_SLOTS + k + 1)
                    dve.tensor_reduce(neg[:, par, h0:h0 + nh, t], src, X, ALU.max, negate=True).then_inc(max_drained, 1)
                dve.wait_ge(max_drained, q * MAX_SLOTS + MAX_SLOTS - 1 + MCREDIT)
                np_ = nparts[:, par]
                dve.tensor_copy(np_[:, :, 0], neg[:, par]).then_inc(neg_chain, 1)
                dve.wait_ge(neg_chain, q * 4 + 1)
                dve.tensor_tensor(nrest[:, par], neg[:, par], np_[:, :, 0], ALU.subtract).then_inc(neg_chain, 1)
                dve.wait_ge(neg_chain, q * 4 + 2)
                dve.tensor_copy(np_[:, :, 1], nrest[:, par]).then_inc(neg_chain, 1)
                dve.wait_ge(neg_chain, q * 4 + 3)
                dve.tensor_tensor(np_[:, :, 2], nrest[:, par], np_[:, :, 1], ALU.subtract).then_inc(neg_chain, 1)
                s = (MAX_SLOTS * par + MAX_SLOTS - 1) % 2
                dve.wait_ge(max_scored, q * MAX_SLOTS + MAX_SLOTS)
                dve.wait_ge(rows_loaded[par], i * 64 + 16 * START)
                dve.tensor_copy(nT[:, par], PS[0:96, 2 * s, 0:P // 2].bitcast(BF16)).then_inc(parts_ready, 1)
                dve.wait_ge(parts_ready, q + 1)
                dve.sem_inc(max_drained, 1)

            maxima(0, 0)
            with dve.Fori(0, GROUPS - 1) as i:
                maxima(i, 1)
                maxima(i + 1, 0)
            maxima(GROUPS - 1, 1)

        @block.scalar
        def _(act):
            act.sem_inc(exped, CREDIT)
            act.sem_inc(o_copied, START)

            def step(i, par):
                q = i * 2 + par
                for u, (g, h0, nh) in enumerate(PROB_UNITS):
                    w = PROB_GROUPS[g][3]
                    at = NU * par + u
                    if at >= PROB_SLOTS:
                        act.wait_ge(summed, i * (2 * NG) + NG * ((at - PROB_SLOTS) // NU) + PROB_UNITS[(at - PROB_SLOTS) % NU][0] + 1 + START)
                    else:
                        act.wait_ge(summed, i * (2 * NG) + START)
                    act.wait_ge(scored, i * (2 * NU) + at + 1)
                    act.activation(probs[:, at % PROB_SLOTS, 0:nh * w], PS[:, 4 + at % SCORE_BANKS, 0:nh * w],
                                   ACT.Exp).then_inc(exped, 1)
                    if u == UNITS_OF[4][3]:
                        copy_out(i, par, 0)
                copy_out(i, par, 1)

            def copy_out(i, par, c):
                q = i * 2 + par
                act.wait_ge(o_out[c], q * 16 + 16 * START)
                act.wait_ge(summed, q * NG + (4 if c == 0 else NG) + START)
                act.activation(ob[:, c], PS[:, 7, :], ACT.Copy).then_inc(o_copied, 1)

            with act.Fori(0, GROUPS - 1) as i:
                step(i, 0)
                step(i, 1)
            step(GROUPS - 1, 0)
            step(GROUPS - 1, 1)

        @block.tensor
        def _(pe):
            pe.sem_inc(summed, START)

            def maximum(i, par, k):
                q = i * 2 + par
                s = (MAX_SLOTS * par + k) % 2
                if k == 0:
                    pe.wait_ge(max_loaded[par], (i + 1) * LOADS)
                pe.wait_ge(max_drained, q * MAX_SLOTS + k - 1 + MCREDIT)
                if k == MAX_SLOTS - 1:
                    pe.wait_ge(neg_chain, q * 4 + 4)
                    pe.transpose(PS[0:96, 2 * s, 0:P // 2].bitcast(BF16),
                                 nparts[:, par].rearrange("p h c t -> p (h c t)"), identb[:]).then_inc(max_scored, 1)
                    return
                t, h0, nh = MAX_UNITS[k]
                w = P * (t + 1)
                for n in range(nh):
                    h = h0 + n
                    if w <= BANK:
                        per = BANK // w if t < 2 else 1
                        pieces = [(2 * s + n // per, (n % per) * w, 0, w)]
                    else:
                        pieces = [(2 * s, 0, 0, BANK), (2 * s + 1, 0, BANK, w - BANK)]
                    for bank, at, s0, ws in pieces:
                        last = s0 + ws == w
                        mm = pe.matmul(PS[:, bank, at:at + ws], q1[:, par, h, P * t:P * (t + 1)],
                                       k1[:, par, h, s0:s0 + ws], start=True, stop=not last)
                        if last:
                            mm = pe.matmul(PS[:, bank, at + ws - P:at + ws], identb[:], causal[:], start=False, stop=True)
                mm.then_inc(max_scored, 1)

            def score(i, par, u):
                g, h0, nh = PROB_UNITS[u]
                c, j, lo, w, _ = PROB_GROUPS[g]
                at = NU * par + u
                if u == 0:
                    pe.wait_ge(prob_loaded[par], (i + 1) * (LOADS + 16))
                    pe.wait_ge(rows_loaded[par], (i + 1) * 64 + 16 * START)
                pe.wait_ge(exped, i * (2 * NU) + last_in_bank(at) + 1 + CREDIT)
                for n in range(nh):
                    mm = pe.matmul(PS[:, 4 + at % SCORE_BANKS, n * w:(n + 1) * w], k2[:, par, h0 + n, P * j:P * (j + 1)],
                                   q2[:, par, h0 + n, lo:lo + w], start=True, stop=True)
                mm.then_inc(scored, 1)

            def weigh(i, par, g):
                q = i * 2 + par
                c, j, lo, w, per = PROB_GROUPS[g]
                last = UNITS_OF[g][-1]
                if DIAG[g]:
                    pe.wait_ge(masked, q * len(MASKED) + MASKED.index(last) + 1)
                else:
                    pe.wait_ge(exped, q * NU + last + 1 + CREDIT)
                if j == 0:
                    pe.wait_ge(o_copied, q * 2 + c + START)
                for h in range(QUAD):
                    u = UNITS_OF[g][h // per]
                    s = (NU * par + u) % PROB_SLOTS
                    mm = pe.matmul(PS[32 * h:32 * (h + 1), 7, lo - BANK * c:BANK], vb[:, par, j, h],
                                   probs[:, s, (h % per) * w:(h % per + 1) * w], start=j == 0, stop=j == 4 * c + 3)
                mm.then_inc(summed, 1)

            def step(i, par, ahead):
                i1, par1 = (i, 1) if par == 0 else (i + 1, 0)
                for what, n in STEP:
                    if what == "score":
                        score(i, par, n)
                    elif what == "weigh":
                        weigh(i, par, n)
                    elif n >= MAX_AHEAD and ahead >= 1:
                        maximum(i1, par1, n)
                    elif n < MAX_AHEAD and ahead >= 2:
                        maximum(i + 1, par, n)

            for k in range(MAX_SLOTS):
                maximum(0, 0, k)
            for k in range(MAX_AHEAD):
                maximum(0, 1, k)
            with pe.Fori(0, GROUPS - 1) as i:
                step(i, 0, ahead=2)
                step(i, 1, ahead=2)
            step(GROUPS - 1, 0, ahead=1)
            step(GROUPS - 1, 1, ahead=0)


def gather_a(nc, PS, xs, ident, o_dram):
    with ExitStack() as ctx:
        def sb(name, shape, dt):
            return ctx.enter_context(nc.sbuf_tensor(name, shape, dt))

        def sem(name):
            return ctx.enter_context(nc.semaphore(name))

        oT = sb("oT", [P, BATCH, GROUPS, SEQ], F32)
        y = sb("y", [P, BATCH, TILES, DIM], F32)
        inv = sb("inv", [P, NT, HEADS_A], F32)
        o_in = [sem(f"o_in{i}") for i in range(BATCH)]
        turned, inverted, scaled, added = sem("turned"), sem("inverted"), sem("scaled"), sem("added")
        block = ctx.enter_context(nc.Block())

        @block.sync
        def _(sp):
            for i in range(BATCH):
                sp.dma_start(oT[:, i], o_dram[i].rearrange("g p n -> p g n")).then_inc(o_in[i], 16)

        PAIR = 2

        @block.tensor
        def _(pe):
            for n in range(NT):
                i, t = n // TILES, n % TILES
                if t == 0:
                    pe.wait_ge(o_in[i], 16)
                if n >= 8 and n % PAIR == 0:
                    pe.wait_ge(scaled, (n - 8) // PAIR + 1)
                for g in range(GROUPS):
                    mm = pe.transpose(PS[:, n % 8, P * g:P * (g + 1)], oT[:, i, g, P * t:P * (t + 1)], ident[:])
                if n % PAIR == PAIR - 1:
                    mm.then_inc(turned, 1)

        @block.vector
        def _(dve):
            for u in range(NT // PAIR):
                i, t = u * PAIR // TILES, u * PAIR % TILES
                banks = PS[:, u * PAIR % 8:u * PAIR % 8 + PAIR, :].rearrange("p b (h d) -> p b h d", d=32)
                dve.wait_ge(turned, u + 1)
                dve.reciprocal(inv[:, u * PAIR:(u + 1) * PAIR], banks[:, :, :, HD_A]).then_inc(inverted, 1)
                dve.wait_ge(inverted, u + 1)
                dve.tensor_tensor(y[:, i, t:t + PAIR].rearrange("p b (h d) -> p b h d", d=HD_A), banks[:, :, :, 0:HD_A],
                                  over(inv[:, u * PAIR:(u + 1) * PAIR, :, None], [P, PAIR, HEADS_A, HD_A]),
                                  ALU.mult).then_inc(scaled, 1)

        @block.gpsimd
        def _(pool):
            for u in range(NT // PAIR):
                i, t = u * PAIR // TILES, u * PAIR % TILES
                pool.wait_ge(scaled, u + 1)
                pool.tensor_tensor(xs[:, i, t:t + PAIR], xs[:, i, t:t + PAIR], y[:, i, t:t + PAIR], ALU.add).then_inc(added, 1)


def ffn(nc, PS, xs, identb, wq, ws, wb, out):
    with ExitStack() as ctx:
        def sb(name, shape, dt):
            return ctx.enter_context(nc.sbuf_tensor(name + ("_2" if out is not None else "_1"), shape, dt))

        def sem(name):
            return ctx.enter_context(nc.semaphore(name + ("_2" if out is not None else "_1")))

        shape = [P, BATCH, TILES, DIM]
        w64 = sb("w64", [P, P, 2], I32)
        wbf = sb("wbf", [P, P], BF16)
        wqT = sb("wqT", [P, P], BF16)
        wsrow = sb("wsrow", [P, P], F32)
        brow = sb("brow", [P, P], F32)
        xc, z, acc = sb("fxc", shape, F32), sb("fz", shape, F32), sb("acc", shape, F32)
        raw = sb("fraw", [P, BATCH, TILES, 6], F32)
        mv = sb("fmv", [P, BATCH, TILES, 2], F32)
        root = sb("froot", [P, BATCH, TILES], F32)
        rstd = sb("frstd", [P, BATCH, TILES], F32)
        amax = sb("amax", [P, 2, BATCH, TILES], F32)
        scale = sb("fscale", [P, BATCH, TILES], F32)
        inv = sb("finv", [P, 2, BATCH, TILES], F32)
        xq = sb("xq", shape, BF16)
        xqT = sb("xqT", [P, BATCH, SEQ], BF16)

        w_in = sem("fw_in")
        dve_chain = sem("fdve_chain")
        varied, centred, rooted, sized = sem("fvaried"), sem("fcentred"), sem("frooted"), sem("sized")
        w_cast, w_turned, w_copied = sem("w_cast"), sem("w_turned"), sem("w_copied")
        divided, rounded = sem("divided"), sem("rounded")
        turned, copied, multiplied = sem("fturned"), sem("fcopied"), sem("multiplied")
        biased, added, stored = sem("biased"), sem("fadded"), sem("fstored")
        block = ctx.enter_context(nc.Block())
        HALF = TILES // 2

        @block.sync
        def _(sp):
            sp.dma_start(w64[:].rearrange("p c w -> p (c w)"), wq.bitcast(I32)).then_inc(w_in, 16)
            sp.dma_start(wsrow[:], over(ws[None], [P, P])).then_inc(w_in, 16)
            sp.dma_start(brow[:], over(wb[None], [P, P])).then_inc(w_in, 16)
            if out is not None:
                for n in range(2 * BATCH):
                    i, half = n // 2, slice(HALF * (n % 2), HALF * (n % 2 + 1))
                    sp.wait_ge(added, n + 1)
                    sp.dma_start(out[:, i, half], xs[:, i, half]).then_inc(stored, 16)
                sp.wait_ge(stored, 16 * 2 * BATCH)

        @block.vector
        def _(dve):
            chain = Chain(dve, dve_chain)

            def statistics(i):
                moments(dve, chain, xs[:, i], raw[:, i], mv[:, i])
                dve.tensor_scalar(root[:, i], mv[:, i, :, 1], 1e-5, None, ALU.add).then_inc(varied, 1)

            def centre(i):
                dve.tensor_tensor(xc[:, i], xs[:, i], per_row(mv[:, i, :, 0]), ALU.subtract).then_inc(centred, 1)

            def steps(i):
                dve.wait_ge(centred, i + 1)
                dve.wait_ge(rooted, i + 1)
                chain(dve.tensor_reduce(amax[:, 0, i], xc[:, i], X, ALU.max, apply_absolute_value=True),
                      dve.reciprocal(rstd[:, i], root[:, i]))
                chain(dve.tensor_tensor(amax[:, 1, i], amax[:, 0, i], rstd[:, i], ALU.mult))
                chain(dve.tensor_scalar(scale[:, i], amax[:, 1, i], 1e-6, 1.0 / 127.0, ALU.max, ALU.mult))
                chain(dve.reciprocal(inv[:, 0, i], scale[:, i]))
                dve.tensor_tensor(inv[:, 1, i], inv[:, 0, i], rstd[:, i], ALU.mult).then_inc(sized, 1)

            def quantise(i):
                dve.wait_ge(divided, TILES * (i + 1))
                chain(dve.tensor_scalar(z[:, i], z[:, i], 127.0, -128.0, ALU.min, ALU.max))
                dve.tensor_scalar(xq[:, i], z[:, i], MAGIC, MAGIC, ALU.add, ALU.subtract).then_inc(rounded, 1)

            statistics(0)
            centre(0)
            statistics(1)
            steps(0)
            centre(1)
            steps(1)
            quantise(0)
            quantise(1)
            dve.wait_ge(w_in, 48)
            for n in range(2 * BATCH):
                i, half = n // 2, slice(HALF * (n % 2), HALF * (n % 2 + 1))
                dve.wait_ge(multiplied, n + 1)
                chain(*[dve.scalar_tensor_tensor(acc[:, i, t], PS[:, 4 + n, P * (t % HALF):P * (t % HALF + 1)],
                                                 scale[:, i, t:t + 1], wsrow[:], ALU.mult, ALU.mult)
                        for t in range(TILES)[half]])
                dve.wait_ge(biased, i + 1)
                dve.tensor_tensor(xs[:, i, half], xs[:, i, half], acc[:, i, half], ALU.add).then_inc(added, 1)

        @block.gpsimd
        def _(pool):
            pool.wait_ge(w_in, 48)
            for i in range(BATCH):
                pool.wait_ge(centred, i + 1)
                pool.tensor_tensor(xs[:, i], xs[:, i], over(brow[:, None], [P, TILES, P]), ALU.add).then_inc(biased, 1)

        @block.scalar
        def _(act):
            for i in range(BATCH):
                act.wait_ge(varied, i + 1)
                act.activation(root[:, i], root[:, i], ACT.Sqrt).then_inc(rooted, 1)
                if i == 0:
                    act.wait_ge(w_in, 48)
                    act.activation(wbf[:], w64[:, :, 0], ACT.Copy).then_inc(w_cast, 1)
            for i in range(BATCH):
                act.wait_ge(sized, i + 1)
                for t in range(TILES):
                    act.activation(z[:, i, t], xc[:, i, t], ACT.Copy, scale=inv[:, 1, i, t:t + 1]).then_inc(divided, 1)
            act.wait_ge(w_turned, 1)
            act.activation(wqT[:], PS[:, 6, 0:P // 2].bitcast(BF16), ACT.Copy).then_inc(w_copied, 1)
            for n in range(2 * BATCH):
                act.wait_ge(turned, n + 1)
                act.activation(xqT[:, n // 2, BANK * (n % 2):BANK * (n % 2 + 1)], PS[:, n, 0:BANK // 2].bitcast(BF16),
                               ACT.Copy).then_inc(copied, 1)

        @block.tensor
        def _(pe):
            pe.wait_ge(w_cast, 1)
            pe.transpose(PS[:, 6, 0:P // 2].bitcast(BF16), wbf[:], identb[:]).then_inc(w_turned, 1)

            def turn(n):
                i = n // 2
                pe.wait_ge(rounded, i + 1)
                for k in range(HALF):
                    mm = pe.transpose(PS[:, n, P // 2 * k:P // 2 * (k + 1)].bitcast(BF16), xq[:, i, HALF * (n % 2) + k], identb[:])
                mm.then_inc(turned, 1)

            def multiply(n):
                i = n // 2
                pe.wait_ge(copied, n + 1)
                for k in range(HALF):
                    t = HALF * (n % 2) + k
                    mm = pe.matmul(PS[:, 4 + n, P * k:P * (k + 1)], xqT[:, i, P * t:P * (t + 1)], wqT[:], start=True, stop=True)
                mm.then_inc(multiplied, 1)

            turn(0)
            turn(1)
            pe.wait_ge(w_copied, 1)
            multiply(0)
            multiply(1)
            turn(2)
            turn(3)
            multiply(2)
            multiply(3)


def attend_b(nc, PS, xs, ident, identb, causal, norm_w, w_q, w_k, w_v, w_out, scorer_w, scorer_b):
    with ExitStack() as ctx:
        def sb(name, shape, dt):
            return ctx.enter_context(nc.sbuf_tensor(name, shape, dt))

        wq = sb("wq", [P, HEADS_B * HD_B], F32)
        wk = sb("wk", [P, HEADS_B * HD_B], F32)
        wv = sb("wv", [P, HEADS_B * HD_B], F32)
        wo = sb("wo", [P, PAIRS, DIM], F32)
        hT = sb("bhT", [P, BATCH, SEQ], F32)
        masks = sb("masks", [P, BATCH, TILES, KEYS], BF16)
        kT = sb("kT", [P, 2, PAIRS, KEYS], F32)
        vg = sb("vg", [P, BATCH, HEADS_B // 4, 4, HD_B], F32)
        qT = sb("qT", [P, 2, PAIRS, P], F32)
        vw = sb("vw", [P, 2, HEADS_B, HD_B], F32)
        pick_b(nc, PS, xs, ident, causal, norm_w, w_q, w_k, w_v, w_out, scorer_w, scorer_b, wq, wk, wv, wo, hT, masks, kT, vg, qT, vw)
        windows_b(nc, PS, xs, ident, identb, wq, wk, wv, wo, hT, masks, kT, vg, qT, vw)


PROJECTIONS = ["q0", "q1", "k0", "k1", "v0", "v1"]


def project_half(pe, name, bank, h, wq, wk, wv):
    k = int(name[1])
    if name[0] == "v":
        return pe.matmul(bank, h, wv[:, BANK * k:BANK * (k + 1)], start=True, stop=True)
    for r in range(4):
        c = P * (4 * k + r)
        mm = pe.matmul(bank[:, P * r:P * (r + 1)], (wq if name[0] == "q" else wk)[:, c:c + P], h, start=True, stop=True)
    return mm


def take_half(act, name, bank, par, qT, kT, vw):
    k = int(name[1])
    four = bank.rearrange("p (r t) -> p r t", r=4)
    if name[0] == "q":
        return act.activation(qT[:, par, 4 * k:4 * k + 4], four, ACT.Copy, scale=float(HD_B) ** -0.5)
    if name[0] == "k":
        return act.activation(kT[:, par, 4 * k:4 * k + 4, 0:P], four, ACT.Copy)
    return act.activation(vw[:, par, 8 * k:8 * k + 8], bank.rearrange("p (h d) -> p h d", d=HD_B), ACT.Copy)


def pick_b(nc, PS, xs, ident, causal, norm_w, w_q, w_k, w_v, w_out, scorer_w, scorer_b, wq, wk, wv, wo, hT, masks, kT, vg, qT, vw):
    with ExitStack() as ctx:
        def sb(name, shape, dt):
            return ctx.enter_context(nc.sbuf_tensor(name, shape, dt))

        def sem(name):
            return ctx.enter_context(nc.semaphore(name))

        shape = [P, BATCH, TILES, DIM]
        xc, xn, hn = sb("bxc", shape, F32), sb("bxn", shape, F32), sb("bhn", shape, F32)
        raw = sb("braw", [P, BATCH, TILES, 6], F32)
        mv = sb("bmv", [P, BATCH, TILES, 2], F32)
        root = sb("broot", [P, BATCH, TILES], F32)
        rstd = sb("brstd", [P, BATCH, TILES], F32)
        power = sb("bpower", [P, 3, BATCH, TILES], F32)
        rrms = sb("brrms", [P, 2, BATCH, TILES], F32)
        nw = sb("nw", [P, 1], F32)
        scw = sb("scw", [P, BATCH, BATCH], F32)
        scb = sb("scb", [BATCH, 1], F32)
        scores = sb("scores", [BATCH, SEQ], F32)
        left = sb("left", [BATCH, 2, SEQ], F32)
        top = sb("top", [BATCH, PICKED], F32)
        index = sb("index", [BATCH, PICKED], U32)
        indexf = sb("indexf", [BATCH, PICKED], F32)
        rows = sb("rows", [BATCH, BATCH, P], F32)
        picked = sb("picked", [P, BATCH, PICKED], F32)
        token = sb("token", [P, TILES], F32)
        onehot = sb("onehot", [P, BATCH, TILES, PICKED], F32)
        later = sb("later", [P, BATCH, TILES, PICKED], F32)
        hg = sb("hg", [P, BATCH, 4, PICKED], F32)

        w_in, s_in = sem("bw_in"), sem("bs_in")
        dve_chain, dve_chain2 = sem("bdve_chain"), sem("bdve_chain2")
        varied, rooted, inverted, normed = (sem(n) for n in ("bvaried", "brooted", "binverted", "bnormed"))
        varied2, rooted2, rmsed = (sem(n) for n in ("bvaried2", "brooted2", "rmsed"))
        summed, turned, copied = sem("bsummed"), sem("bturned"), sem("bcopied")
        scored, biased, indexed, spread, spread_copied = sem("bscored"), sem("bbiased"), sem("indexed"), sem("spread"), sem("spread_copied")
        consts, onehots, masked = sem("consts"), sem("onehots"), sem("bmasked")
        gathered, hg_copied, kg_ready, kg_copied, vg_ready, vg_copied = (
            sem(n) for n in ("gathered", "hg_copied", "kg_ready", "kg_copied", "vg_ready", "vg_copied"))
        first_ready, first_taken = sem("first_ready"), sem("first_taken")
        causal_copied, vg_zeroed, scw_zeroed = sem("causal_copied"), sem("vg_zeroed"), sem("scw_zeroed")
        block = ctx.enter_context(nc.Block())

        @block.sync
        def _(sp):
            sp.dma_start(nw[:], norm_w[:, None], allow_slow_non_contiguous=True).then_inc(s_in, 16)
            sp.dma_start(scb[:], over(scorer_b[None], [BATCH, 1]), allow_slow_non_contiguous=True).then_inc(s_in, 16)
            sp.wait_ge(scw_zeroed, 1)
            for i in range(BATCH):
                sp.dma_start(scw[:, i, i:i + 1], scorer_w, allow_slow_non_contiguous=True).then_inc(s_in, 16)
            for dst, src in ((wk, w_k), (wv, w_v), (wq, w_q)):
                sp.dma_start(dst[:], src).then_inc(w_in, 16)
            sp.dma_start(wo[:], w_out.rearrange("(r p) n -> p r n", p=P)).then_inc(w_in, 16)
            sp.wait_ge(w_in, 64)

        @block.gpsimd
        def _(pool):
            pool.memset(scw[:], 0.0).then_inc(scw_zeroed, 1)
            pool.memset(vg[:], 0.0).then_inc(vg_zeroed, 1)
            pool.iota(token[:], [[P, TILES]], base=0, channel_multiplier=1, allow_small_or_imprecise_dtypes=True).then_inc(consts, 1)
            pool.memset(rows[:], 0.0).then_inc(consts, 1)
            pool.wait_ge(consts, 2)
            pool.affine_select(out=rows[:], in_=rows[:], compare_op=ALU.not_equal, fill=1.0, base=0,
                               pattern=[[-1, BATCH], [0, P]], channel_multiplier=1).then_inc(consts, 1)
            for i in range(BATCH):
                pool.tensor_copy(masks[:, i, :, 0:P], over(causal[:, None], [P, TILES, P])).then_inc(causal_copied, 1)
            pool.wait_ge(inverted, 1)
            for i in range(BATCH):
                pool.tensor_tensor(xn[:, i], xc[:, i], per_row(rstd[:, i]), ALU.mult).then_inc(normed, 1)
                pool.wait_ge(normed, i + 1)
                pool.tensor_tensor(xs[:, i], xs[:, i], xn[:, i], ALU.add).then_inc(summed, 1)

        @block.vector
        def _(dve):
            chain = Chain(dve, dve_chain)
            for i in range(BATCH):
                moments(dve, chain, xs[:, i], raw[:, i], mv[:, i])
            dve.tensor_scalar(root[:], mv[:, :, :, 1], 1e-5, None, ALU.add).then_inc(varied, 1)
            centres = [dve.tensor_tensor(xc[:, i], xs[:, i], per_row(mv[:, i, :, 0]), ALU.subtract) for i in range(BATCH)]
            dve.wait_ge(rooted, 1)
            chain(*centres, dve.reciprocal(rstd[:], root[:]))
            dve.tensor_tensor(power[:, 0], rstd[:], rstd[:], ALU.mult).then_inc(inverted, 1)
            dve.wait_ge(inverted, 1)
            chain(dve.tensor_tensor(power[:, 1], power[:, 0], mv[:, :, :, 1], ALU.mult))
            dve.tensor_scalar(power[:, 2], power[:, 1], 1e-6, None, ALU.add).then_inc(varied2, 1)
            dve.wait_ge(rooted2, 1)
            chain(dve.reciprocal(rrms[:, 0], power[:, 2]))
            chain(dve.tensor_tensor(rrms[:, 1], rrms[:, 0], rstd[:], ALU.mult))
            for i in range(BATCH):
                dve.tensor_tensor(hn[:, i], xc[:, i], per_row(rrms[:, 1, i]), ALU.mult).then_inc(rmsed, 1)
            dve.wait_ge(s_in, 64)
            dve.wait_ge(scored, 1)
            chain(dve.tensor_scalar(scores[:], PS[0:BATCH, 4:6, :].rearrange("p b n -> p (b n)"), scb[:, 0:1], None, ALU.add))
            src = scores[:]
            for r in range(PICKED // 8):
                chain(dve.max(top[:, 8 * r:8 * r + 8], src))
                chain(dve.max_index(index[:, 8 * r:8 * r + 8], top[:, 8 * r:8 * r + 8], src))
                if r < PICKED // 8 - 1:
                    chain(dve.match_replace(left[:, r % 2], top[:, 8 * r:8 * r + 8], src, -3.0e38))
                    src = left[:, r % 2]
            dve.tensor_copy(indexf[:], index[:]).then_inc(indexed, 1)
            dve.wait_ge(spread, 1)
            dve.tensor_copy(picked[:], PS[:, 6, 0:BATCH * PICKED].rearrange("p (b g) -> p b g", b=BATCH)).then_inc(spread_copied, 1)
            dve.wait_ge(spread_copied, 1)
            dve.wait_ge(consts, 3)
            for i in range(BATCH):
                at = over(picked[:, i][:, None], [P, TILES, PICKED])
                own = over(token[:, :, None], [P, TILES, PICKED])
                dve.tensor_tensor(onehot[:, i], at, own, ALU.is_equal).then_inc(onehots, 1)
                chain(dve.tensor_tensor(later[:, i], at, own, ALU.is_gt))
                dve.tensor_scalar(masks[:, i, :, P:KEYS], later[:, i], BIG, None, ALU.mult).then_inc(masked, 1)
            dve.wait_ge(kg_ready, 1)
            for i in range(BATCH):
                dve.tensor_copy(kT[:, i, :, P:KEYS], PS[:, 0].rearrange("p (r b g) -> p r b g", r=PAIRS, b=BATCH)[:, :, i]).then_inc(kg_copied, 1)
            dve.wait_ge(vg_zeroed, 1)
            for i in range(BATCH):
                dve.wait_ge(vg_ready, i + 1)
                for r in range(4):
                    src = PS[32 * r:32 * (r + 1), 2 + 2 * i:4 + 2 * i, :].rearrange("p b n -> p (b n)").rearrange(
                        "p (g r d) -> p g r d", g=HEADS_B // 4, r=4)[:, :, r]
                    dve.tensor_copy(vg[32 * r:32 * (r + 1), i, :, r], src).then_inc(vg_copied, 1)

        @block.scalar
        def _(act):
            act.wait_ge(varied, 1)
            act.activation(root[:], root[:], ACT.Sqrt).then_inc(rooted, 1)
            act.wait_ge(varied2, 1)
            act.activation(power[:, 2], power[:, 2], ACT.Sqrt).then_inc(rooted2, 1)
            act.wait_ge(s_in, 64)
            for i in range(BATCH):
                for k in range(2):
                    act.wait_ge(turned, 2 * i + k + 1)
                    act.activation(hT[:, i, BANK * k:BANK * (k + 1)], PS[:, 2 * i + k, :], ACT.Copy, scale=nw[:, 0:1]).then_inc(copied, 1)
            for n in range(len(PROJECTIONS) * BATCH):
                act.wait_ge(first_ready, n + 1)
                take_half(act, PROJECTIONS[n % len(PROJECTIONS)], PS[:, n % 4, :], n // len(PROJECTIONS), qT, kT, vw).then_inc(first_taken, 1)
            for i in range(BATCH):
                act.wait_ge(gathered, i + 1)
                act.activation(hg[:, i], over(PS[:, 7, PICKED * i:PICKED * (i + 1)][:, None], [P, 4, PICKED]), ACT.Copy,
                               scale=nw[:, 0:1]).then_inc(hg_copied, 1)

        @block.tensor
        def _(pe):
            for i in range(BATCH):
                pe.wait_ge(rmsed, i + 1)
                for t in range(TILES):
                    mm = pe.transpose(PS[:, 2 * i + t // 4, P * (t % 4):P * (t % 4 + 1)], hn[:, i, t], ident[:])
                    if t % 4 == 3:
                        mm.then_inc(turned, 1)
            pe.wait_ge(copied, 4)
            for k in range(2):
                for i in range(BATCH):
                    mm = pe.matmul(PS[0:BATCH, 4 + k, :], scw[:, i], hT[:, i, BANK * k:BANK * (k + 1)], start=i == 0, stop=i == BATCH - 1)
            mm.then_inc(scored, 1)
            pe.wait_ge(w_in, 64)
            for n in range(len(PROJECTIONS) * BATCH):
                if n >= 4:
                    pe.wait_ge(first_taken, n - 3)
                project_half(pe, PROJECTIONS[n % len(PROJECTIONS)], PS[:, n % 4, :], hT[:, n // len(PROJECTIONS), 0:P],
                             wq, wk, wv).then_inc(first_ready, 1)
            pe.wait_ge(indexed, 1)
            pe.wait_ge(consts, 3)
            for i in range(BATCH):
                mm = pe.matmul(PS[:, 6, PICKED * i:PICKED * (i + 1)], rows[:, i], indexf[:], start=True, stop=True)
            mm.then_inc(spread, 1)
            for i in range(BATCH):
                pe.wait_ge(onehots, i + 1)
                if i:
                    pe.wait_ge(hg_copied, i)
                for t in range(TILES):
                    mm = pe.matmul(PS[:, 7, PICKED * i:PICKED * (i + 1)], hn[:, i, t], onehot[:, i, t], start=t == 0, stop=t == TILES - 1)
                mm.then_inc(gathered, 1)
            pe.wait_ge(hg_copied, BATCH)
            pe.wait_ge(first_taken, len(PROJECTIONS) * BATCH)
            for r in range(PAIRS):
                mm = pe.matmul(PS[:, 0, BATCH * PICKED * r:BATCH * PICKED * (r + 1)], wk[:, P * r:P * (r + 1)], hg[:, :, 0], start=True, stop=True)
            mm.then_inc(kg_ready, 1)
            for i in range(BATCH):
                if i == 1:
                    pe.wait_ge(spread_copied, 1)
                for k in range(2):
                    mm = pe.matmul(PS[:, 2 + 2 * i + k, :], hg[:, i].rearrange("p r g -> p (r g)"), wv[:, BANK * k:BANK * (k + 1)],
                                   start=True, stop=True)
                mm.then_inc(vg_ready, 1)


def windows_b(nc, PS, xs, ident, identb, wq, wk, wv, wo, hT, masks, kT, vg, qT, vw):
    with ExitStack() as ctx:
        def sb(name, shape, dt):
            return ctx.enter_context(nc.sbuf_tensor(name, shape, dt))

        def sem(name):
            return ctx.enter_context(nc.semaphore(name))

        hw = sb("hw", [P, 2, P], F32)
        mw = sb("mw", [P, 2, KEYS], BF16)
        nmax = sb("nmax", [P, 2, HEADS_B], F32)
        pr = sb("pr", [P, 2, HEADS_B, KEYS], F32)
        prg = sb("prg", [P, 2, HEADS_B, PICKED], F32)
        pT = sb("pT", [P, HEADS_B, P], F32)
        pgT = sb("pgT", [P, 4, P], F32)
        sums = sb("bsums", [P, 2, HEADS_B], F32)
        inv = sb("binv", [P, 2, HEADS_B], F32)
        oT = sb("boT", [P, PAIRS, P], F32)

        h_in = [sem(f"h_in{i}") for i in range(2)]
        m_in = [sem(f"m_in{i}") for i in range(2)]
        t_ready, t_taken = sem("t_ready"), sem("t_taken")
        s_ready, s_maxed, s_taken, exped = sem("s_ready"), sem("s_maxed"), sem("s_taken"), sem("bexped")
        p_summed, p_inverted, p_picked, p_scaled = sem("p_summed"), sem("p_inverted"), sem("p_picked"), sem("p_scaled")
        o_ready, o_taken = sem("o_ready"), sem("o_taken")
        out_ready, out_taken = sem("out_ready"), sem("out_taken")
        sp_met = sem("bsp_met")
        block = ctx.enter_context(nc.Block())

        UNITS = [(0, 6), (6, 6), (12, 4)]
        STEP = ["pg", "p0", "s0", "p1", "w0", "s1", "p2", "w1", "p3", "s2", "w2", "w3",
                "q0", "q1", "k0", "k1", "v0", "v1", "out"]
        ITEMS = [name for name in STEP if name[0] in "pqkv"]
        LAST_ITEMS = [name for name in ITEMS if name not in PROJECTIONS]
        NTI = len(ITEMS)
        T0 = NTI
        CREDIT = 2

        def last(i):
            return isinstance(i, int) and i == TILES - 1

        def t_index(i, par, name):
            if last(i):
                return T0 + (i * 2) * NTI + par * len(LAST_ITEMS) + LAST_ITEMS.index(name)
            return T0 + (i * 2 + par) * NTI + ITEMS.index(name)

        def bank_of(par, name):
            return PS[:, 4 + t_index(0, par, name) % 2, :]

        @block.sync
        def _(sp):
            def load(i, par):
                sp.dma_start(hw[:, par], hT[:, par, bass.ds(i * P, P)]).then_inc(h_in[par], 16)
                sp.dma_start(mw[:, par], masks[:, par, bass.ds(i, 1)].rearrange("p o k -> p (o k)")).then_inc(m_in[par], 16)

            sp.dma_start(mw[:, 1], masks[:, 1, 0]).then_inc(m_in[1], 16)

            def step(i):
                for par in range(2):
                    sp.wait_ge(t_ready, t_index(i, par, "pg") + 1)
                    sp.sem_inc(sp_met, 1)
                    sp.wait_ge(s_ready, (i * 2 + par) * 3 + 3)
                    sp.sem_inc(sp_met, 1)
                    load(i + 1, par)

            with sp.Fori(0, TILES - 1) as i:
                step(i)

        @block.vector
        def _(dve):
            dve.sem_inc(out_taken, CREDIT)

            def softmax(i, par, u, first=False):
                n = (i * 2 + par) * 3 + u
                h0, nh = UNITS[u]
                s = 2 * ((3 * par + u) % 2)
                per = nh // 2
                full = PS[:, s:s + 2, 0:KEYS * per].rearrange("p b (h k) -> p b h k", h=per)
                mx = nmax[:, par, h0:h0 + nh].rearrange("p (h b) -> p b h", b=2)
                dve.wait_ge(s_ready, n + 1)
                dve.tensor_reduce(mx, full, X, ALU.max).then_inc(s_maxed, 1)
                if u == 0 and not first:
                    dve.wait_ge(t_ready, T0 + (i * 2 + par - 1) * NTI)
                dve.wait_ge(s_maxed, n + 1)
                for b in range(2):
                    ins = dve.tensor_tensor(pr[:, par, h0 + b:h0 + nh:2], full[:, b], over(mx[:, b][:, :, None], [P, per, KEYS]),
                                            ALU.subtract)
                ins.then_inc(s_taken, 1)

            def normalise(i, par, u):
                n = (i * 2 + par) * 3 + u
                h0, nh = UNITS[u]
                unit = slice(h0, h0 + nh)
                dve.wait_ge(exped, n + 1)
                dve.tensor_reduce(sums[:, par, unit], pr[:, par, unit], X, ALU.add).then_inc(p_summed, 1)
                dve.wait_ge(p_summed, n + 1)
                dve.reciprocal(inv[:, par, unit], sums[:, par, unit]).then_inc(p_inverted, 1)
                dve.wait_ge(p_inverted, n + 1)
                dve.tensor_tensor(prg[:, par, unit], pr[:, par, unit, P:KEYS], over(inv[:, par, unit, None], [P, nh, PICKED]),
                                  ALU.mult).then_inc(p_picked, 1)
                dve.tensor_tensor(pr[:, par, unit, 0:P], pr[:, par, unit, 0:P], over(inv[:, par, unit, None], [P, nh, P]),
                                  ALU.mult).then_inc(p_scaled, 1)

            def output(i, par):
                n = i * 2 + par
                tile = xs[:, par, bass.ds(i, 1)].rearrange("p o c -> p (o c)")
                dve.wait_ge(out_ready, n + 1 + CREDIT)
                dve.tensor_tensor(tile, tile, PS[:, 6 + par, 0:DIM], ALU.add).then_inc(out_taken, 1)

            def step(i, par, ahead=True):
                i1, par1 = (i, 1) if par == 0 else (i + 1, 0)
                for name in ("s0", "s1", "n0", "s2", "n1", "n2", "out"):
                    if name == "out":
                        output(i, par)
                    elif ahead:
                        (softmax if name[0] == "s" else normalise)(i1, par1, int(name[1]))

            for u in range(3):
                softmax(0, 0, u, first=True)
            for u in range(3):
                normalise(0, 0, u)
            with dve.Fori(0, TILES - 1) as i:
                step(i, 0)
                step(i, 1)
            step(TILES - 1, 0)
            step(TILES - 1, 1, ahead=False)

        @block.scalar
        def _(act):
            act.sem_inc(o_taken, CREDIT)
            act.sem_inc(t_taken, T0)

            def take(i, par, name):
                n = i * 2 + par
                bank = bank_of(par, name)
                four = bank.rearrange("p (r t) -> p r t", r=4)
                act.wait_ge(t_ready, t_index(i, par, name) + 1)
                if name == "q0":
                    act.wait_ge(s_ready, n * 3 + 3)
                if name == "v0":
                    act.wait_ge(o_ready, n * 4 + 4 + CREDIT)
                if name in PROJECTIONS:
                    ins = take_half(act, name, bank, par, qT, kT, vw)
                elif name == "pg":
                    act.wait_ge(o_ready, n * 4 + CREDIT)
                    ins = act.activation(pgT[:], four, ACT.Copy)
                else:
                    k = int(name[1])
                    ins = act.activation(pT[:, 4 * k:4 * k + 4], four, ACT.Copy)
                ins.then_inc(t_taken, 1)

            def take_output(i, par, k):
                n = i * 2 + par
                act.wait_ge(o_ready, n * 4 + 2 * k + 2 + CREDIT)
                act.wait_ge(out_ready, n + CREDIT)
                act.activation(oT[:, 4 * k:4 * k + 4], PS[:, 6 + (par + k) % 2, :].rearrange("p (r t) -> p r t", r=4),
                               ACT.Copy).then_inc(o_taken, 1)

            def exponential(i, par, u):
                n = (i * 2 + par) * 3 + u
                h0, nh = UNITS[u]
                act.wait_ge(s_taken, n + 1)
                v = pr[:, par, h0:h0 + nh]
                act.activation(v, v, ACT.Exp).then_inc(exped, 1)

            ORDER = ["pg", "p0", "p1", "e0", "p2", "p3", "o0", "e1", "o1", "q0", "e2", "q1", "k0", "k1", "v0", "v1"]

            def step(i, par, ahead=True):
                i1, par1 = (i, 1) if par == 0 else (i + 1, 0)
                for name in ORDER:
                    if name[0] == "e":
                        if ahead:
                            exponential(i1, par1, int(name[1]))
                    elif name[0] == "o":
                        take_output(i, par, int(name[1]))
                    elif name not in PROJECTIONS or not last(i):
                        take(i, par, name)

            for u in range(3):
                exponential(0, 0, u)
            with act.Fori(0, TILES - 1) as i:
                step(i, 0)
                step(i, 1)
            step(TILES - 1, 0)
            step(TILES - 1, 1, ahead=False)

        @block.tensor
        def _(pe):
            pe.sem_inc(o_ready, CREDIT)
            pe.sem_inc(out_ready, CREDIT)
            pe.sem_inc(t_ready, T0)

            def item(i, par, name):
                pe.wait_ge(t_taken, t_index(i, par, name) - 1)
                return bank_of(par, name)

            def scores(i, par, u, first=False):
                n = (i * 2 + par) * 3 + u
                h0, nh = UNITS[u]
                s = 2 * ((3 * par + u) % 2)
                if u == 0:
                    if not first:
                        pe.wait_ge(t_taken, T0 + (i * 2 + par - 1) * NTI)
                        pe.wait_ge(m_in[par], (i + par) * 16)
                if not (first and u < 2):
                    pe.wait_ge(s_taken, n - 1)
                per = nh // 2
                for k in range(per):
                    for b in range(2):
                        lo = HD_B * b
                        pe.matmul(PS[:, s + b, KEYS * k:KEYS * (k + 1)], qT[lo:lo + HD_B, par, h0 // 2 + k],
                                  kT[lo:lo + HD_B, par, h0 // 2 + k], start=k == 0, stop=False, skip_group_check=True)
                mask = masks[:, par, 0] if first else mw[:, par]
                for b in range(2):
                    mm = pe.matmul(PS[:, s + b, 0:KEYS * per], identb[:], over(mask[:, None], [P, per, KEYS]),
                                   start=False, stop=True, skip_group_check=True)
                mm.then_inc(s_ready, 1)

            def turn_probs(i, par, name):
                bank = item(i, par, name)
                if name == "pg":
                    pe.wait_ge(p_scaled, (i * 2 + par) * 3 + 3)
                for r in range(4):
                    if name == "pg":
                        src = prg[:, par, 4 * r:4 * r + 4].rearrange("p h g -> p (h g)")
                    else:
                        src = pr[:, par, 4 * int(name[1]) + r, 0:P]
                    mm = pe.transpose(bank[:, P * r:P * (r + 1)], src, ident[:])
                mm.then_inc(t_ready, 1)

            def weigh(i, par, g):
                n = i * 2 + par
                if g == 0:
                    pe.wait_ge(o_taken, n * 2 + CREDIT)
                if g == 2:
                    pe.wait_ge(out_taken, n + CREDIT)
                pe.wait_ge(t_taken, t_index(i, par, f"p{g}") + 1)
                for k in range(2):
                    block = PS[:, 6 + (par + g // 2) % 2, P * (2 * (g % 2) + k):P * (2 * (g % 2) + k + 1)]
                    pe.matmul(block, vg[:, par, g, 2 * k:2 * k + 2].rearrange("p h d -> p (h d)"), pgT[:, g],
                              start=True, stop=False, skip_group_check=True)
                    for b in range(2):
                        h = 4 * g + 2 * k + b
                        mm = pe.matmul(block[HD_B * b:HD_B * (b + 1)], vw[:, par, h], pT[:, h], start=False, stop=True,
                                       skip_group_check=True)
                mm.then_inc(o_ready, 1)

            def output(i, par):
                n = i * 2 + par
                pe.wait_ge(o_taken, n * 2 + 2 + CREDIT)
                for r in range(PAIRS):
                    mm = pe.matmul(PS[:, 6 + par, 0:DIM], oT[:, r], wo[:, r], start=r == 0, stop=r == PAIRS - 1)
                mm.then_inc(out_ready, 1)

            def step(i, par, ahead=True):
                i1, par1 = (i, 1) if par == 0 else (i + 1, 0)
                for name in STEP:
                    if name[0] == "s":
                        if ahead:
                            scores(i1, par1, int(name[1]))
                    elif name[0] == "w":
                        weigh(i, par, int(name[1]))
                    elif name[0] == "p":
                        turn_probs(i, par, name)
                    elif name == "out":
                        output(i, par)
                    elif not last(i):
                        if name == "q0":
                            pe.wait_ge(h_in[par], (i + 1) * 16)
                        project_half(pe, name, item(i, par, name), hw[:, par], wq, wk, wv).then_inc(t_ready, 1)

            for u in range(3):
                scores(0, 0, u, first=True)
            with pe.Fori(0, TILES - 1) as i:
                step(i, 0)
                step(i, 1)
            step(TILES - 1, 0)
            step(TILES - 1, 1, ahead=False)


_INS = ["L0_attn_a_x", "L0_attn_a_W", "L0_attn_a_b", "L0_attn_b_norm_w", "L0_attn_b_w_q", "L0_attn_b_w_k", "L0_attn_b_w_v",
        "L0_attn_b_w_out", "L0_attn_b_scorer_w", "L0_attn_b_scorer_b", "L0_ffn_weight_q", "L0_ffn_weight_scale",
        "L0_ffn_bias"]


def kernel(**inputs):
    import numpy as _np
    import concourse.bacc as _bacc
    from concourse import mybir as _mybir
    from concourse.bass_utils import run_bass_kernel_spmd as _run

    nc = _bacc.Bacc("TRN2", target_bir_lowering=False, num_devices=1)
    arrays, args = {}, []
    for name in _INS:
        a = _np.ascontiguousarray(inputs[name])
        if a.dtype.kind in "iu":
            a = a.astype(_np.int64)
        arrays[f"in_{name}_dram"] = a
        args.append(nc.dram_tensor(f"in_{name}_dram", a.shape, _mybir.dt.from_np(a.dtype), kind="ExternalInput").ap())
    args.append(nc.dram_tensor("out_dram", (BATCH, SEQ, DIM), F32, kind="ExternalOutput").ap())
    build(nc, *args)
    return _run(nc, [arrays], core_ids=[0]).results[0]["out_dram"]
```

```python
from contextlib import ExitStack

import concourse.bass as bass
from concourse import mybir

F32 = mybir.dt.float32
BF16 = mybir.dt.bfloat16
I32 = mybir.dt.int32
U32 = mybir.dt.uint32
ALU = mybir.AluOpType
ACT = mybir.ActivationFunctionType
X = mybir.AxisListType.X

P = 128
BATCH, SEQ, DIM = 2, 1024, 128
TILES = SEQ // P
BANK = 512

HEADS_A, HD_A = 16, 8
QUAD = 4
GROUPS = HEADS_A // QUAD
PARTS = 3
ROWS = PARTS * PARTS * HD_A
MROWS = ROWS + PARTS
BIG = -1.0e30
MAGIC = 1.5 * 2.0 ** 23

HEADS_B, HD_B = 16, 64
PAIRS = HEADS_B // 2
PICKED = 32
KEYS = P + PICKED

MAX_UNITS = []
for _t in range(TILES):
    _n = QUAD if _t < 2 else (2 if _t < 4 else 1)
    MAX_UNITS += [(_t, h, _n) for h in range(0, QUAD, _n)]
MAX_SLOTS = len(MAX_UNITS) + 1

PROB_GROUPS = []
for _c in range(SEQ // BANK):
    for _j in range(4 * (_c + 1)):
        _lo = max(BANK * _c, P * _j)
        _w = BANK * (_c + 1) - _lo
        PROB_GROUPS.append((_c, _j, _lo, _w, max(1, min(QUAD, BANK // _w))))
PROB_UNITS = []
for _g, (_c, _j, _lo, _w, _n) in enumerate(PROB_GROUPS):
    PROB_UNITS += [(_g, h, _n) for h in range(0, QUAD, _n)]
NG, NU = len(PROB_GROUPS), len(PROB_UNITS)
DIAG = [_j * P >= BANK * _c for _c, _j, *_ in PROB_GROUPS]
UNITS_OF = [[u for u, x in enumerate(PROB_UNITS) if x[0] == g] for g in range(NG)]
MASKED = [u for u, x in enumerate(PROB_UNITS) if DIAG[x[0]]]


def order_of_step():
    cols = [(PROB_GROUPS[g][3]) * n for g, _, n in PROB_UNITS]
    total, at, items, done = sum(cols), 0, [], []
    for u, c in enumerate(cols):
        items.append((at / total + SCORE_LAG, 0, "score", u))
        at += c
        done.append(at / total)
    for g in range(NG):
        items.append((done[UNITS_OF[g][-1]] + SCORE_LAG + WEIGH_LAG, 1, "weigh", g))
    widths = [P * (t + 1) * n for t, _, n in MAX_UNITS]
    for k in range(MAX_SLOTS):
        at = (sum(widths[:k]) - sum(widths[:MAX_AHEAD])) / sum(widths) + (1 if k < MAX_AHEAD else 0)
        at = at * MAX_SHARE + (TURN_LAG if k == len(MAX_UNITS) or k < MAX_AHEAD else 0)
        items.append((at, 2 if k == len(MAX_UNITS) else 3, "max", k))
    return [(what, n) for _, _, what, n in sorted(items)]


SCORE_LAG = 0.04
WEIGH_LAG = 0.07
TURN_LAG = 0.08
MAX_AHEAD = 3
MAX_SHARE = 1 - TURN_LAG
STEP = order_of_step()
PROB_SLOTS = NU // 2
SCORE_BANKS = 3


def last_in_bank(u):
    bank = u % SCORE_BANKS
    if u >= SCORE_BANKS:
        return u - SCORE_BANKS
    return max(v for v in range(2 * NU) if v % SCORE_BANKS == bank) - 2 * NU


def make_identity(pool, tile, made):
    pool.memset(tile[:], 0.0).then_inc(made, 1)
    pool.wait_ge(made, 1)
    pool.affine_select(out=tile[:], in_=tile[:], compare_op=ALU.not_equal, fill=1.0, base=0,
                       pattern=[[-1, P]], channel_multiplier=1).then_inc(made, 1)


def over(ap, shape):
    return ap.to_broadcast(shape)


class Chain:

    def __init__(self, engine, sem):
        self.engine, self.sem, self.done = engine, sem, 0

    def __call__(self, *instructions):
        for instruction in instructions:
            instruction.then_inc(self.sem, 1)
            self.done += 1
        self.engine.wait_ge(self.sem, self.done)


def build(nc, x, w, b, norm_w, w_q, w_k, w_v, w_out, scorer_w, scorer_b, ffn_w, ffn_s, ffn_b, out):
    xv = x.rearrange("b (t p) c -> p b t c", p=P)
    q_dram = nc.dram_tensor("q_dram", [PARTS, P, BATCH, SEQ], BF16, kind="Internal").ap()
    k_dram = nc.dram_tensor("k_dram", [PARTS, PARTS, P, BATCH, SEQ], BF16, kind="Internal").ap()

    with ExitStack() as whole:
        def keep(name, shape, dt):
            return whole.enter_context(nc.sbuf_tensor(name, shape, dt))

        PS = whole.enter_context(nc.psum_tensor("PS", [P, 8, BANK], F32))
        xs = keep("xs", [P, BATCH, TILES, DIM], F32)
        ident = keep("ident", [P, P], F32)
        identb = keep("identb", [P, P], BF16)
        causal = keep("causal", [P, P], BF16)

        rows = Rows(whole, nc, "rows")
        weights = Weights(whole, nc)
        with ExitStack() as ctx:
            def sb(name, shape, dt):
                return ctx.enter_context(nc.sbuf_tensor(name, shape, dt))

            stacks = [sb(name, [P, 2, QUAD, SEQ], BF16) for name in ("q1", "k1", "q2", "k2")]
            va = sb("va", [P, BATCH, GROUPS, TILES, QUAD, 32], F32)
            parts_out = [ctx.enter_context(nc.semaphore(f"parts_out{i}")) for i in range(BATCH)]
            max_loaded = [ctx.enter_context(nc.semaphore(f"max_loaded{i}")) for i in range(2)]
            with nc.sbuf_tensor("parts", [P, 2, PARTS, BATCH, SEQ], BF16) as parts:
                project_a(nc, PS, xs, ident, identb, causal, xv, w, b, q_dram, k_dram, stacks, parts, va, parts_out, max_loaded)
            oT = sb("oT", [P, BATCH, GROUPS, SEQ], F32)
            attend_a(nc, PS, xs, ident, identb, causal, q_dram, k_dram, oT, stacks, va, parts_out, max_loaded, rows)
            gather_a(nc, PS, xs, ident, oT, rows)
        ffn(nc, PS, xs, identb, ffn_w, ffn_s, ffn_b, weights, rows, [0], None)
        attend_b(nc, PS, xs, ident, identb, causal, norm_w, w_q, w_k, w_v, w_out, scorer_w, scorer_b, rows)
        ffn(nc, PS, xs, identb, ffn_w, ffn_s, ffn_b, weights, rows, [0, 1], out.rearrange("b (t p) c -> p b t c", p=P))


def load_stacks(eng, i, par, q_dram, k_dram, qbuf, kbuf, done):
    q_rows = q_dram.rearrange("c (d h) b t -> (c d) h b t", h=HEADS_A)
    k_rows = k_dram.rearrange("a c (d h) b t -> (a c d) h b t", h=HEADS_A)
    for a in range(PARTS):
        n = PARTS * HD_A
        eng.dma_start(qbuf[n * a:n * (a + 1), par], q_rows[:, bass.ds(i * QUAD, QUAD), par]).then_inc(done, 16)
    eng.dma_start(kbuf[0:ROWS, par], k_rows[:, bass.ds(i * QUAD, QUAD), par]).then_inc(done, 16)


def project_a(nc, PS, xs, ident, identb, causal, xv, w, b, q_dram, k_dram, stacks, parts, va, parts_out, max_loaded):
    with ExitStack() as ctx:
        def sb(name, shape, dt):
            return ctx.enter_context(nc.sbuf_tensor(name, shape, dt))

        def sem(name):
            return ctx.enter_context(nc.semaphore(name))

        wsb = sb("wsb", [P, 3, P], F32)
        wT = sb("wT", [P, 3, P], F32)
        bcol = sb("bcol", [P, 2], F32)
        bvrow = sb("bvrow", [P, P], F32)
        xc = sb("xc", [P, BATCH, TILES, DIM], F32)
        xn = sb("xn", [P, BATCH, TILES, DIM], F32)
        raw = sb("raw", [P, BATCH, TILES, 6], F32)
        mv = sb("mv", [P, BATCH, TILES, 2], F32)
        root = sb("root", [P, BATCH, TILES], F32)
        rstd = sb("rstd", [P, BATCH, TILES], F32)
        hT = sb("hT", [P, BATCH, SEQ], F32)
        qk = sb("qk", [P, 2, BATCH, SEQ], F32)
        rest = sb("rest", [P, 2, BATCH, SEQ], F32)

        x_in = [sem(f"x_in{i}") for i in range(BATCH)]
        w_in = sem("w_in")
        id_made, idb_made, causal_made, va_made = sem("id_made"), sem("idb_made"), sem("causal_made"), sem("va_made")
        dve_chain = sem("dve_chain")
        varied, rooted, normed = sem("varied"), sem("rooted"), sem("normed")
        wT_ready, wT_copied, hT_ready, hT_copied = (sem(n) for n in ("wT_ready", "wT_copied", "hT_ready", "hT_copied"))
        q_ready, q_taken, k_ready, k_taken, v_ready, v_taken = (
            sem(n) for n in ("q_ready", "q_taken", "k_ready", "k_taken", "v_ready", "v_taken"))
        hi_made = [sem("q_hi_made"), sem("k_hi_made")]
        rest_made = [sem("q_rest_made"), sem("k_rest_made")]
        lo_made = [sem("q_lo_made"), sem("k_lo_made")]
        ones_made, filled = sem("ones_made"), sem("filled")
        q_banks, k_banks, v_banks = (5, 1), (6, 2), (7, 3)

        block = ctx.enter_context(nc.Block())

        @block.sync
        def _(sp):
            for i in range(BATCH):
                sp.dma_start(xs[:, i], xv[:, i]).then_inc(x_in[i], 16)
            sp.dma_start(wsb[:], w.rearrange("(r p) c -> p r c", p=P)).then_inc(w_in, 16)
            for r in range(2):
                sp.dma_start(bcol[:, r:r + 1], b[P * r:P * (r + 1)].rearrange("(h d) -> d h", d=HD_A)[:, :, None],
                             allow_slow_non_contiguous=True).then_inc(w_in, 16)
            sp.dma_start(bvrow[:], over(b[2 * P:3 * P][None], [P, P])).then_inc(w_in, 16)
            for i in range(BATCH):
                sp.wait_ge(hi_made[0], 2 * (i + 1))
                sp.wait_ge(lo_made[0], i + 1)
                sp.dma_start(q_dram[:, :, i].rearrange("c p t -> p c t"), parts[:, 0, :, i]).then_inc(parts_out[i], 16)
                sp.wait_ge(hi_made[1], 2 * (i + 1))
                sp.wait_ge(lo_made[1], i + 1)
                for a in range(PARTS):
                    sp.dma_start(k_dram[a, :, :, i].rearrange("c p t -> p c t"),
                                 over(parts[:, 1, a, i][:, None], [P, PARTS, SEQ])).then_inc(parts_out[i], 16)
                if i == 0:
                    sp.wait_ge(parts_out[0], 64)
                    sp.wait_ge(ones_made, 2)
                    load_stacks(sp, 0, 0, q_dram, k_dram, stacks[0], stacks[1], max_loaded[0])

        @block.gpsimd
        def _(pool):
            make_identity(pool, ident, id_made)
            make_identity(pool, identb, idb_made)
            pool.memset(causal[:], 0.0).then_inc(causal_made, 1)
            pool.wait_ge(causal_made, 1)
            pool.affine_select(out=causal[:], in_=causal[:], compare_op=ALU.is_ge, fill=BIG, base=0,
                               pattern=[[-1, P]], channel_multiplier=1).then_inc(causal_made, 1)
            pool.memset(va[:], 0.0).then_inc(va_made, 1)
            pool.wait_ge(va_made, 1)
            pool.memset(va[:, :, :, :, :, HD_A:HD_A + 1], 1.0).then_inc(va_made, 1)
            pool.wait_ge(va_made, 2)

            for n in range(2):
                pool.memset(stacks[n][64:P], 0.0).then_inc(ones_made, 1)
                pool.wait_ge(ones_made, n + 1)
            for i in range(BATCH):
                pool.wait_ge(hi_made[1], 2 * i + 1)
                pool.tensor_tensor(rest[:, 1, i], qk[:, 1, i], parts[:, 1, 0, i], ALU.subtract).then_inc(rest_made[1], 1)
                pool.wait_ge(rest_made[1], i + 1)
                pool.wait_ge(hi_made[1], 2 * i + 2)
                pool.tensor_tensor(parts[:, 1, 2, i], rest[:, 1, i], parts[:, 1, 1, i], ALU.subtract).then_inc(lo_made[1], 1)

        @block.vector
        def _(dve):
            chain = Chain(dve, dve_chain)
            dve.memset(stacks[2][64:P], 0.0).then_inc(filled, 1)
            for i in range(BATCH):
                dve.wait_ge(x_in[i], 16)
                moments(dve, chain, xs[:, i], raw[:, i], mv[:, i])
                dve.tensor_scalar(root[:, i], mv[:, i, :, 1], 1e-5, None, ALU.add).then_inc(varied, 1)
                centre = dve.tensor_tensor(xc[:, i], xs[:, i], per_row(mv[:, i, :, 0]), ALU.subtract)
                chain(centre)
                dve.wait_ge(rooted, i + 1)
                chain(dve.reciprocal(rstd[:, i], root[:, i]))
                dve.tensor_tensor(xn[:, i], xc[:, i], per_row(rstd[:, i]), ALU.mult).then_inc(normed, 1)
            for i in range(BATCH):
                for k in range(2):
                    dve.wait_ge(q_ready, 2 * i + k + 1)
                    dve.tensor_scalar(qk[:, 0, i, BANK * k:BANK * (k + 1)], PS[:, q_banks[k], :], bcol[:, 0:1],
                                      float(HD_A) ** -0.5, ALU.add, ALU.mult).then_inc(q_taken, 1)
                dve.wait_ge(hi_made[0], 2 * i + 1)
                dve.tensor_tensor(rest[:, 0, i], qk[:, 0, i], parts[:, 0, 0, i], ALU.subtract).then_inc(rest_made[0], 1)
                if i == 0:
                    dve.wait_ge(va_made, 2)
                    dve.wait_ge(w_in, 64)
                for t in range(TILES):
                    if t % 4 == 0:
                        dve.wait_ge(v_ready, 2 * i + t // 4 + 1)
                    dve.tensor_tensor(va[:, i, :, t, :, 0:HD_A],
                                      PS[:, v_banks[t // 4], P * (t % 4):P * (t % 4 + 1)].rearrange("p (g h d) -> p g h d", g=GROUPS, h=QUAD),
                                      bvrow[:].rearrange("p (g h d) -> p g h d", g=GROUPS, h=QUAD), ALU.add).then_inc(v_taken, 1)
                dve.wait_ge(rest_made[0], i + 1)
                dve.wait_ge(hi_made[0], 2 * i + 2)
                dve.tensor_tensor(parts[:, 0, 2, i], rest[:, 0, i], parts[:, 0, 1, i], ALU.subtract).then_inc(lo_made[0], 1)
            dve.memset(stacks[3][64:P], 1.0).then_inc(filled, 1)

        @block.scalar
        def _(act):
            act.wait_ge(wT_ready, 1)
            for r in range(2):
                act.activation(wT[:, r].rearrange("p (d h) -> p d h", d=HD_A),
                               PS[:, 0, P * r:P * (r + 1)].rearrange("p (h d) -> p d h", d=HD_A), ACT.Copy).then_inc(wT_copied, 1)
            act.activation(wT[:, 2], PS[:, 0, 2 * P:3 * P], ACT.Copy).then_inc(wT_copied, 1)
            act.wait_ge(w_in, 64)
            for i in range(BATCH):
                act.wait_ge(varied, i + 1)
                act.activation(root[:, i], root[:, i], ACT.Sqrt).then_inc(rooted, 1)
            for i in range(BATCH):
                for k in range(2):
                    act.wait_ge(hT_ready, 2 * i + k + 1)
                    act.activation(hT[:, i, BANK * k:BANK * (k + 1)], PS[:, 1 + 2 * i + k, :], ACT.Copy).then_inc(hT_copied, 1)
            for i in range(BATCH):
                for k in range(2):
                    act.wait_ge(k_ready, 2 * i + k + 1)
                    act.activation(qk[:, 1, i, BANK * k:BANK * (k + 1)], PS[:, k_banks[k], :], ACT.Identity,
                                   bias=bcol[:, 1:2]).then_inc(k_taken, 1)
                for side, taken in ((1, k_taken), (0, q_taken)):
                    act.wait_ge(taken, 2 * (i + 1))
                    act.activation(parts[:, side, 0, i], qk[:, side, i], ACT.Copy).then_inc(hi_made[side], 1)
                for side in (1, 0):
                    act.wait_ge(rest_made[side], i + 1)
                    act.activation(parts[:, side, 1, i], rest[:, side, i], ACT.Copy).then_inc(hi_made[side], 1)

        @block.tensor
        def _(pe):
            pe.wait_ge(w_in, 64)
            pe.wait_ge(id_made, 2)
            for r in range(3):
                mm = pe.transpose(PS[:, 0, P * r:P * (r + 1)], wsb[:, r], ident[:])
            mm.then_inc(wT_ready, 1)
            for i in range(BATCH):
                pe.wait_ge(normed, i + 1)
                for t in range(TILES):
                    mm = pe.transpose(PS[:, 1 + 2 * i + t // 4, P * (t % 4):P * (t % 4 + 1)], xn[:, i, t], ident[:])
                    if t % 4 == 3:
                        mm.then_inc(hT_ready, 1)
            pe.wait_ge(wT_copied, 3)
            for i in range(BATCH):
                for k in range(2):
                    n = 2 * i + k
                    pe.wait_ge(hT_copied, 1 if n == 0 else 4)
                    if n >= 2:
                        pe.wait_ge(q_taken, n - 1)
                    pe.matmul(PS[:, q_banks[k], :], wT[:, 0], hT[:, i, BANK * k:BANK * (k + 1)], start=True, stop=True).then_inc(q_ready, 1)
                    if n >= 2:
                        pe.wait_ge(k_taken, n - 1)
                    pe.matmul(PS[:, k_banks[k], :], wT[:, 1], hT[:, i, BANK * k:BANK * (k + 1)], start=True, stop=True).then_inc(k_ready, 1)
                    if n >= 2:
                        pe.wait_ge(v_taken, 4 * (n - 1))
                    for t in range(4):
                        mm = pe.matmul(PS[:, v_banks[k], P * t:P * (t + 1)], hT[:, i, BANK * k + P * t:BANK * k + P * (t + 1)], wT[:, 2],
                                       start=True, stop=True)
                    mm.then_inc(v_ready, 1)


class Rows:

    def __init__(self, ctx, nc, name):
        def sb(what, shape):
            return ctx.enter_context(nc.sbuf_tensor(name + what, shape, F32))

        self.xc = sb("_xc", [P, BATCH, TILES, DIM])
        self.raw = sb("_raw", [P, BATCH, TILES, 6])
        self.mv = sb("_mv", [P, BATCH, TILES, 2])
        self.amax = sb("_amax", [P, BATCH, TILES])

    def batch(self, dve, chain, xs, i):
        moments(dve, chain, xs[:, i], self.raw[:, i], self.mv[:, i])
        chain(dve.tensor_tensor(self.xc[:, i], xs[:, i], per_row(self.mv[:, i, :, 0]), ALU.subtract))
        chain(dve.tensor_reduce(self.amax[:, i], self.xc[:, i], X, ALU.max, apply_absolute_value=True))


def moments(dve, chain, src, raw, mv):
    chain(*[dve.bn_stats(raw[:, t], src[:, t]) for t in range(TILES)])
    chain(*[dve.bn_aggr(mv[:, t], raw[:, t]) for t in range(TILES)])


def per_row(values):
    return over(values[:, :, None], [P, TILES, DIM])


def attend_a(nc, PS, xs, ident, identb, causal, q_dram, k_dram, oT, stacks, va, parts_out, max_loaded, rows):
    with ExitStack() as ctx:
        def sb(name, shape, dt):
            return ctx.enter_context(nc.sbuf_tensor(name, shape, dt))

        def sem(name):
            return ctx.enter_context(nc.semaphore(name))

        q1, k1, q2, k2 = stacks
        vb = sb("vb", [P, 2, TILES, QUAD, 32], F32)
        probs = sb("probs", [P, PROB_SLOTS, BANK], F32)
        y = rows.xc[:, 0]
        inv = sb("ainv", [P, TILES, HEADS_A], F32)
        neg = sb("neg", [P, 2, QUAD, TILES], F32)
        nrest = sb("nrest", [P, 2, QUAD, TILES], F32)
        nparts = sb("nparts", [P, 2, QUAD, PARTS, TILES], BF16)
        nT = sb("nT", [QUAD * PARTS * TILES, 2, P], BF16)

        prob_loaded = [sem(f"prob_loaded{i}") for i in range(2)]
        rows_loaded = [sem(f"rows_loaded{i}") for i in range(2)]
        max_scored, max_drained, neg_chain = sem("max_scored"), sem("max_drained"), sem("neg_chain")
        parts_ready = sem("parts_ready")
        scored, exped, masked, summed = sem("scored"), sem("exped"), sem("masked"), sem("summed")
        o_copied = sem("o_copied")
        sp_met, pool_met = sem("sp_met"), sem("pool_met")
        turned, inverted, scaled, row_chain = sem("aturned"), sem("ainverted"), sem("ascaled"), sem("row_chain")

        block = ctx.enter_context(nc.Block())
        CREDIT = SCORE_BANKS
        MCREDIT = 2
        START = 1
        LOADS = (PARTS + 1) * 16

        def load_v(eng, i, par):
            eng.dma_start(vb[:, par].rearrange("p j h d -> p (j h d)"),
                          va[:, par, bass.ds(i, 1)].rearrange("p g j h d -> p (g j h d)")).then_inc(prob_loaded[par], 16)

        @block.sync
        def _(sp):
            for n in range(2):
                sp.sem_inc(rows_loaded[n], 16 * START)
            load_stacks(sp, 0, 0, q_dram, k_dram, q2, k2, prob_loaded[0])
            load_v(sp, 0, 0)
            sp.wait_ge(parts_out[1], 64)
            load_stacks(sp, 0, 1, q_dram, k_dram, q1, k1, max_loaded[1])

            def load_rows(i, par):
                sp.wait_ge(parts_ready, i * 2 + par + 1)
                for h in range(QUAD):
                    n = PARTS * TILES
                    sp.dma_start(q2[ROWS:MROWS, par, h], nT[n * h:n * (h + 1), par]).then_inc(rows_loaded[par], 16)

            load_rows(0, 0)

            def step(i, par, more_max, more_prob):
                q = i * 2 + par
                if more_max:
                    sp.wait_ge(max_scored, q * MAX_SLOTS + MAX_SLOTS)
                    sp.sem_inc(sp_met, 1)
                    load_stacks(sp, i + 1, par, q_dram, k_dram, q1, k1, max_loaded[par])
                if more_prob:
                    sp.wait_ge(summed, q * NG + START)
                    sp.sem_inc(sp_met, 1)
                    load_stacks(sp, i + par, 1 - par, q_dram, k_dram, q2, k2, prob_loaded[1 - par])
                    load_v(sp, i + par, 1 - par)
                    load_rows(i + par, 1 - par)

            with sp.Fori(0, GROUPS - 1) as i:
                step(i, 0, True, True)
                step(i, 1, True, True)
            step(GROUPS - 1, 0, False, True)

        @block.gpsimd
        def _(pool):
            zero = pool.to_reg(0.0)

            def step(i, par):
                for n, u in enumerate(MASKED):
                    g, h0, nh = PROB_UNITS[u]
                    w = PROB_GROUPS[g][3]
                    s = (NU * par + u) % PROB_SLOTS
                    pool.wait_ge(exped, i * (2 * NU) + NU * par + u + 1 + CREDIT)
                    pool.sem_inc(pool_met, 1)
                    v = probs[:, s, 0:nh * w].rearrange("p (h w) -> p h w", h=nh)[:, :, 0:P]
                    pool.affine_select(out=v, in_=v, compare_op=ALU.is_ge, fill=zero, base=0,
                                       pattern=[[0, nh], [1, P]], channel_multiplier=-1).then_inc(masked, 1)

            with pool.Fori(0, GROUPS - 1) as i:
                step(i, 0)
                step(i, 1)
            step(GROUPS - 1, 0)
            step(GROUPS - 1, 1)

        @block.vector
        def _(dve):
            dve.sem_inc(max_drained, MCREDIT)

            def maxima(i, par):
                q = i * 2 + par
                for k, (t, h0, nh) in enumerate(MAX_UNITS):
                    s = (MAX_SLOTS * par + k) % 2
                    w = P * (t + 1)
                    if w <= BANK:
                        per = min(nh, BANK // w) if t < 2 else 1
                        src = PS[:, 2 * s:2 * s + nh // per, 0:per * w]
                        src = src.rearrange("p b (h w) -> p (b h) w", w=w) if nh // per == 1 or per * w == BANK else src
                    else:
                        src = PS[:, 2 * s:2 * s + 2, :].rearrange("p b n -> p (b n)")[:, 0:w][:, None]
                    dve.wait_ge(max_scored, q * MAX_SLOTS + k + 1)
                    dve.tensor_reduce(neg[:, par, h0:h0 + nh, t], src, X, ALU.max, negate=True).then_inc(max_drained, 1)
                dve.wait_ge(max_drained, q * MAX_SLOTS + MAX_SLOTS - 1 + MCREDIT)
                np_ = nparts[:, par]
                dve.tensor_copy(np_[:, :, 0], neg[:, par]).then_inc(neg_chain, 1)
                dve.wait_ge(neg_chain, q * 4 + 1)
                dve.tensor_tensor(nrest[:, par], neg[:, par], np_[:, :, 0], ALU.subtract).then_inc(neg_chain, 1)
                dve.wait_ge(neg_chain, q * 4 + 2)
                dve.tensor_copy(np_[:, :, 1], nrest[:, par]).then_inc(neg_chain, 1)
                dve.wait_ge(neg_chain, q * 4 + 3)
                dve.tensor_tensor(np_[:, :, 2], nrest[:, par], np_[:, :, 1], ALU.subtract).then_inc(neg_chain, 1)
                s = (MAX_SLOTS * par + MAX_SLOTS - 1) % 2
                dve.wait_ge(max_scored, q * MAX_SLOTS + MAX_SLOTS)
                dve.wait_ge(rows_loaded[par], i * 64 + 16 * START)
                dve.tensor_copy(nT[:, par], PS[0:96, 2 * s, 0:P // 2].bitcast(BF16)).then_inc(parts_ready, 1)
                dve.wait_ge(parts_ready, q + 1)
                dve.sem_inc(max_drained, 1)

            maxima(0, 0)
            with dve.Fori(0, GROUPS - 1) as i:
                maxima(i, 1)
                maxima(i + 1, 0)
            maxima(GROUPS - 1, 1)
            divide_outputs(dve, PS, y, inv, 4, turned, inverted, scaled)
            dve.wait_ge(scaled, TILES // PAIR)
            chain = Chain(dve, row_chain)
            chain(dve.tensor_tensor(xs[:, 0], xs[:, 0], y, ALU.add))
            rows.batch(dve, chain, xs, 0)

        @block.scalar
        def _(act):
            act.sem_inc(exped, CREDIT)
            act.sem_inc(o_copied, START)

            def step(i, par):
                q = i * 2 + par
                for u, (g, h0, nh) in enumerate(PROB_UNITS):
                    w = PROB_GROUPS[g][3]
                    at = NU * par + u
                    if at >= PROB_SLOTS:
                        act.wait_ge(summed, i * (2 * NG) + NG * ((at - PROB_SLOTS) // NU) + PROB_UNITS[(at - PROB_SLOTS) % NU][0] + 1 + START)
                    else:
                        act.wait_ge(summed, i * (2 * NG) + START)
                    act.wait_ge(scored, i * (2 * NU) + at + 1)
                    act.activation(probs[:, at % PROB_SLOTS, 0:nh * w], PS[:, 4 + at % SCORE_BANKS, 0:nh * w],
                                   ACT.Exp).then_inc(exped, 1)
                    if u == UNITS_OF[4][3]:
                        copy_out(i, par, 0)
                copy_out(i, par, 1)

            def copy_out(i, par, c):
                q = i * 2 + par
                act.wait_ge(summed, q * NG + (4 if c == 0 else NG) + START)
                act.activation(oT[:, par, bass.ds(i, 1), BANK * c:BANK * (c + 1)].rearrange("p g n -> p (g n)"), PS[:, 7, :],
                               ACT.Copy).then_inc(o_copied, 1)

            with act.Fori(0, GROUPS - 1) as i:
                step(i, 0)
                step(i, 1)
            step(GROUPS - 1, 0)
            step(GROUPS - 1, 1)

        @block.tensor
        def _(pe):
            pe.sem_inc(summed, START)

            def maximum(i, par, k):
                q = i * 2 + par
                s = (MAX_SLOTS * par + k) % 2
                if k == 0:
                    pe.wait_ge(max_loaded[par], (i + 1) * LOADS)
                pe.wait_ge(max_drained, q * MAX_SLOTS + k - 1 + MCREDIT)
                if k == MAX_SLOTS - 1:
                    pe.wait_ge(neg_chain, q * 4 + 4)
                    pe.transpose(PS[0:96, 2 * s, 0:P // 2].bitcast(BF16),
                                 nparts[:, par].rearrange("p h c t -> p (h c t)"), identb[:]).then_inc(max_scored, 1)
                    return
                t, h0, nh = MAX_UNITS[k]
                w = P * (t + 1)
                for n in range(nh):
                    h = h0 + n
                    if w <= BANK:
                        per = BANK // w if t < 2 else 1
                        pieces = [(2 * s + n // per, (n % per) * w, 0, w)]
                    else:
                        pieces = [(2 * s, 0, 0, BANK), (2 * s + 1, 0, BANK, w - BANK)]
                    for bank, at, s0, ws in pieces:
                        last = s0 + ws == w
                        mm = pe.matmul(PS[:, bank, at:at + ws], q1[:, par, h, P * t:P * (t + 1)],
                                       k1[:, par, h, s0:s0 + ws], start=True, stop=not last)
                        if last:
                            mm = pe.matmul(PS[:, bank, at + ws - P:at + ws], identb[:], causal[:], start=False, stop=True)
                mm.then_inc(max_scored, 1)

            def score(i, par, u):
                g, h0, nh = PROB_UNITS[u]
                c, j, lo, w, _ = PROB_GROUPS[g]
                at = NU * par + u
                if u == 0:
                    pe.wait_ge(prob_loaded[par], (i + 1) * (LOADS + 16))
                    pe.wait_ge(rows_loaded[par], (i + 1) * 64 + 16 * START)
                pe.wait_ge(exped, i * (2 * NU) + last_in_bank(at) + 1 + CREDIT)
                for n in range(nh):
                    mm = pe.matmul(PS[:, 4 + at % SCORE_BANKS, n * w:(n + 1) * w], k2[:, par, h0 + n, P * j:P * (j + 1)],
                                   q2[:, par, h0 + n, lo:lo + w], start=True, stop=True)
                mm.then_inc(scored, 1)

            def weigh(i, par, g):
                q = i * 2 + par
                c, j, lo, w, per = PROB_GROUPS[g]
                last = UNITS_OF[g][-1]
                if DIAG[g]:
                    pe.wait_ge(masked, q * len(MASKED) + MASKED.index(last) + 1)
                else:
                    pe.wait_ge(exped, q * NU + last + 1 + CREDIT)
                if j == 0:
                    pe.wait_ge(o_copied, q * 2 + c + START)
                for h in range(QUAD):
                    u = UNITS_OF[g][h // per]
                    s = (NU * par + u) % PROB_SLOTS
                    mm = pe.matmul(PS[32 * h:32 * (h + 1), 7, lo - BANK * c:BANK], vb[:, par, j, h],
                                   probs[:, s, (h % per) * w:(h % per + 1) * w], start=j == 0, stop=j == 4 * c + 3)
                mm.then_inc(summed, 1)

            def step(i, par, ahead):
                i1, par1 = (i, 1) if par == 0 else (i + 1, 0)
                places = 0
                if ahead == 0:
                    pe.wait_ge(max_drained, 2 * GROUPS * MAX_SLOTS + MCREDIT)
                for what, n in STEP:
                    if what == "score":
                        score(i, par, n)
                    elif what == "weigh":
                        weigh(i, par, n)
                    elif n >= MAX_AHEAD and ahead >= 1:
                        maximum(i1, par1, n)
                    elif n < MAX_AHEAD and ahead >= 2:
                        maximum(i + 1, par, n)
                    elif ahead == 0:
                        places += 1
                        t = places // 2 - 2
                        if places % 2 == 0 and 0 <= t < TILES:
                            if t == 0:
                                pe.wait_ge(o_copied, 4 * GROUPS - 2 + START)
                            turn_outputs(pe, PS, oT, ident, 0, t, 4, turned, scaled)

            for k in range(MAX_SLOTS):
                maximum(0, 0, k)
            for k in range(MAX_AHEAD):
                maximum(0, 1, k)
            with pe.Fori(0, GROUPS - 1) as i:
                step(i, 0, ahead=2)
                step(i, 1, ahead=2)
            step(GROUPS - 1, 0, ahead=1)
            step(GROUPS - 1, 1, ahead=0)


PAIR = 2


def turn_outputs(pe, PS, oT, ident, i, t, banks, turned, scaled):
    if t >= banks and t % PAIR == 0:
        pe.wait_ge(scaled, (t - banks) // PAIR + 1)
    for g in range(GROUPS):
        mm = pe.transpose(PS[:, t % banks, P * g:P * (g + 1)], oT[:, i, g, P * t:P * (t + 1)], ident[:])
    if t % PAIR == PAIR - 1:
        mm.then_inc(turned, 1)


def divide_outputs(dve, PS, y, inv, banks, turned, inverted, scaled):
    for u in range(TILES // PAIR):
        t = u * PAIR
        src = PS[:, t % banks:t % banks + PAIR, :].rearrange("p b (h d) -> p b h d", d=32)
        dve.wait_ge(turned, u + 1)
        dve.reciprocal(inv[:, t:t + PAIR], src[:, :, :, HD_A]).then_inc(inverted, 1)
        dve.wait_ge(inverted, u + 1)
        dve.tensor_tensor(y[:, t:t + PAIR].rearrange("p b (h d) -> p b h d", d=HD_A), src[:, :, :, 0:HD_A],
                          over(inv[:, t:t + PAIR, :, None], [P, PAIR, HEADS_A, HD_A]), ALU.mult).then_inc(scaled, 1)


def add_outputs(pool, xs, y, i, scaled, added):
    for u in range(TILES // PAIR):
        pair = slice(u * PAIR, (u + 1) * PAIR)
        pool.wait_ge(scaled, u + 1)
        pool.tensor_tensor(xs[:, i, pair], xs[:, i, pair], y[:, pair], ALU.add).then_inc(added, 1)


def gather_a(nc, PS, xs, ident, oT, rows):
    with ExitStack() as ctx:
        def sb(name, shape, dt):
            return ctx.enter_context(nc.sbuf_tensor(name, shape, dt))

        def sem(name):
            return ctx.enter_context(nc.semaphore(name))

        y = rows.xc[:, 1]
        inv = sb("inv", [P, TILES, HEADS_A], F32)
        turned, inverted, scaled, added = sem("turned"), sem("inverted"), sem("scaled"), sem("added")
        block = ctx.enter_context(nc.Block())

        @block.tensor
        def _(pe):
            for t in range(TILES):
                turn_outputs(pe, PS, oT, ident, 1, t, 8, turned, scaled)

        @block.vector
        def _(dve):
            divide_outputs(dve, PS, y, inv, 8, turned, inverted, scaled)

        @block.gpsimd
        def _(pool):
            add_outputs(pool, xs, y, 1, scaled, added)


class Weights:

    def __init__(self, ctx, nc):
        self.wqT = ctx.enter_context(nc.sbuf_tensor("wqT", [P, P], BF16))
        self.scales = ctx.enter_context(nc.sbuf_tensor("w_scales", [P, P], F32))
        self.bias = ctx.enter_context(nc.sbuf_tensor("w_bias", [P, P], F32))


def ffn(nc, PS, xs, identb, wq, ws, wb, weights, rows, known, out):
    first = out is None
    with ExitStack() as ctx:
        def sb(name, shape, dt):
            return ctx.enter_context(nc.sbuf_tensor(name + ("_1" if first else "_2"), shape, dt))

        def sem(name):
            return ctx.enter_context(nc.semaphore(name + ("_1" if first else "_2")))

        shape = [P, BATCH, TILES, DIM]
        w64 = sb("w64", [P, P, 2], I32)
        wbf = sb("wbf", [P, P], BF16)
        z, acc = sb("fz", shape, F32), sb("acc", shape, F32)
        root = sb("froot", [P, BATCH, TILES], F32)
        rstd = sb("frstd", [P, BATCH, TILES], F32)
        amax = sb("amax", [P, BATCH, TILES], F32)
        scale = sb("fscale", [P, BATCH, TILES], F32)
        inv = sb("finv", [P, 2, BATCH, TILES], F32)
        xq = sb("xq", shape, BF16)
        xqT = sb("xqT", [P, BATCH, SEQ], BF16)

        w_in = sem("fw_in")
        dve_chain = sem("fdve_chain")
        varied, centred, rooted, sized = sem("fvaried"), sem("fcentred"), sem("frooted"), sem("sized")
        w_cast, w_turned, w_copied = sem("w_cast"), sem("w_turned"), sem("w_copied")
        divided, rounded = sem("divided"), sem("rounded")
        turned, copied, multiplied = sem("fturned"), sem("fcopied"), sem("multiplied")
        rescaled, biased, added, stored = sem("rescaled"), sem("biased"), sem("fadded"), sem("fstored")
        block = ctx.enter_context(nc.Block())
        groups = [slice(0, BATCH)] if len(known) == BATCH else [slice(i, i + 1) for i in range(BATCH)]
        order = (1, 0) if len(known) == BATCH else (0, 1)
        HALF = TILES // 2

        def place(n):
            return order[n // 2], range(HALF * (n % 2), HALF * (n % 2 + 1))

        @block.sync
        def _(sp):
            if first:
                sp.dma_start(w64[:].rearrange("p c w -> p (c w)"), wq.bitcast(I32)).then_inc(w_in, 16)
                sp.dma_start(weights.scales[:], over(ws[None], [P, P])).then_inc(w_in, 16)
                sp.dma_start(weights.bias[:], over(wb[None], [P, P])).then_inc(w_in, 16)
            else:
                for n in range(2 * BATCH):
                    i, tiles = place(n)
                    half = slice(tiles.start, tiles.stop)
                    sp.wait_ge(added, n + 1)
                    sp.dma_start(out[:, i, half], xs[:, i, half]).then_inc(stored, 16)
                sp.wait_ge(stored, 16 * 2 * BATCH)

        @block.vector
        def _(dve):
            chain = Chain(dve, dve_chain)

            def steps(n):
                g = groups[n]
                dve.wait_ge(rooted, n + 1)
                chain(dve.reciprocal(rstd[:, g], root[:, g]))
                chain(dve.tensor_tensor(amax[:, g], rows.amax[:, g], rstd[:, g], ALU.mult))
                chain(dve.tensor_scalar(scale[:, g], amax[:, g], 1e-6, 1.0 / 127.0, ALU.max, ALU.mult))
                chain(dve.reciprocal(inv[:, 0, g], scale[:, g]))
                dve.tensor_tensor(inv[:, 1, g], inv[:, 0, g], rstd[:, g], ALU.mult).then_inc(sized, 1)

            def quantise(i):
                if i == 0:
                    dve.wait_ge(divided, TILES)
                else:
                    dve.wait_ge(sized, len(groups))
                    chain(dve.tensor_tensor(z[:, i], rows.xc[:, i], per_row(inv[:, 1, i]), ALU.mult))
                chain(dve.tensor_scalar(z[:, i], z[:, i], 127.0, -128.0, ALU.min, ALU.max))
                dve.tensor_scalar(xq[:, i], z[:, i], MAGIC, MAGIC, ALU.add, ALU.subtract).then_inc(rounded, 1)

            for n, g in enumerate(groups):
                if n not in known:
                    rows.batch(dve, chain, xs, n)
                dve.tensor_scalar(root[:, g], rows.mv[:, g, :, 1], 1e-5, None, ALU.add).then_inc(varied, 1)
                if n == len(groups) - 1:
                    dve.sem_inc(centred, 1)
                steps(n)
            for i in order:
                quantise(i)
            if first:
                dve.wait_ge(w_in, 48)
            for n in range(2 * BATCH):
                i, tiles = place(n)
                dve.wait_ge(multiplied, n + 1)
                for k, t in enumerate(tiles):
                    dve.scalar_tensor_tensor(acc[:, i, t], PS[:, 4 + n, P * k:P * (k + 1)], scale[:, i, t:t + 1],
                                             weights.scales[:], ALU.mult, ALU.mult).then_inc(rescaled, 1)

        @block.gpsimd
        def _(pool):
            if first:
                pool.wait_ge(w_in, 48)
            pool.wait_ge(centred, 1)
            for i in order:
                pool.tensor_tensor(xs[:, i], xs[:, i], over(weights.bias[:, None], [P, TILES, P]), ALU.add).then_inc(biased, 1)
            pool.wait_ge(biased, BATCH)
            for n in range(2 * BATCH):
                i, tiles = place(n)
                half = slice(tiles.start, tiles.stop)
                pool.wait_ge(rescaled, HALF * (n + 1))
                pool.tensor_tensor(xs[:, i, half], xs[:, i, half], acc[:, i, half], ALU.add).then_inc(added, 1)

        @block.scalar
        def _(act):
            for n, g in enumerate(groups):
                act.wait_ge(varied, n + 1)
                act.activation(root[:, g], root[:, g], ACT.Sqrt).then_inc(rooted, 1)
                if n == 0:
                    if first:
                        act.wait_ge(w_in, 48)
                        act.activation(wbf[:], w64[:, :, 0], ACT.Copy).then_inc(w_cast, 1)
                    act.wait_ge(sized, 1)
                    for t in range(TILES):
                        act.activation(z[:, 0, t], rows.xc[:, 0, t], ACT.Copy, scale=inv[:, 1, 0, t:t + 1]).then_inc(divided, 1)
            if first:
                act.wait_ge(w_turned, 1)
                act.activation(weights.wqT[:], PS[:, 6, 0:P // 2].bitcast(BF16), ACT.Copy).then_inc(w_copied, 1)
            for n in range(2 * BATCH):
                i, tiles = place(n)
                act.wait_ge(turned, n + 1)
                act.activation(xqT[:, i, P * tiles.start:P * tiles.stop], PS[:, n, 0:BANK // 2].bitcast(BF16), ACT.Copy).then_inc(copied, 1)

        @block.tensor
        def _(pe):
            if first:
                pe.wait_ge(w_cast, 1)
                pe.transpose(PS[:, 6, 0:P // 2].bitcast(BF16), wbf[:], identb[:]).then_inc(w_turned, 1)

            def turn(n):
                i, tiles = place(n)
                pe.wait_ge(rounded, n // 2 + 1)
                for k, t in enumerate(tiles):
                    mm = pe.transpose(PS[:, n, P // 2 * k:P // 2 * (k + 1)].bitcast(BF16), xq[:, i, t], identb[:])
                mm.then_inc(turned, 1)

            def multiply(n):
                i, tiles = place(n)
                pe.wait_ge(copied, n + 1)
                for k, t in enumerate(tiles):
                    mm = pe.matmul(PS[:, 4 + n, P * k:P * (k + 1)], xqT[:, i, P * t:P * (t + 1)], weights.wqT[:], start=True, stop=True)
                mm.then_inc(multiplied, 1)

            turn(0)
            turn(1)
            if first:
                pe.wait_ge(w_copied, 1)
            multiply(0)
            multiply(1)
            turn(2)
            turn(3)
            multiply(2)
            multiply(3)


def attend_b(nc, PS, xs, ident, identb, causal, norm_w, w_q, w_k, w_v, w_out, scorer_w, scorer_b, rows):
    with ExitStack() as ctx:
        def sb(name, shape, dt):
            return ctx.enter_context(nc.sbuf_tensor(name, shape, dt))

        wq = sb("wq", [P, HEADS_B * HD_B], F32)
        wk = sb("wk", [P, HEADS_B * HD_B], F32)
        wv = sb("wv", [P, HEADS_B * HD_B], F32)
        wo = sb("wo", [P, PAIRS, DIM], F32)
        hT = sb("bhT", [P, BATCH, SEQ], F32)
        masks = sb("masks", [P, BATCH, TILES, KEYS], BF16)
        kT = sb("kT", [P, 2, PAIRS, KEYS], F32)
        vg = sb("vg", [P, BATCH, HEADS_B // 4, 4, HD_B], F32)
        qT = sb("qT", [P, 2, PAIRS, P], F32)
        vw = sb("vw", [P, 2, HEADS_B, HD_B], F32)
        hg = sb("hg", [P, BATCH, 4, PICKED], F32)
        pick_b(nc, PS, xs, ident, causal, norm_w, w_q, w_k, w_v, w_out, scorer_w, scorer_b, wq, wk, wv, wo, hT, masks, kT, vg, qT, vw, hg)
        windows_b(nc, PS, xs, ident, identb, wq, wk, wv, wo, hT, masks, kT, vg, qT, vw, hg, rows)


PROJECTIONS = ["q0", "q1", "k0", "k1", "v0", "v1"]


def project_half(pe, name, bank, h, wq, wk, wv):
    k = int(name[1])
    if name[0] == "v":
        return pe.matmul(bank, h, wv[:, BANK * k:BANK * (k + 1)], start=True, stop=True)
    for r in range(4):
        c = P * (4 * k + r)
        mm = pe.matmul(bank[:, P * r:P * (r + 1)], (wq if name[0] == "q" else wk)[:, c:c + P], h, start=True, stop=True)
    return mm


def take_half(act, name, bank, par, qT, kT, vw):
    k = int(name[1])
    four = bank.rearrange("p (r t) -> p r t", r=4)
    if name[0] == "q":
        return act.activation(qT[:, par, 4 * k:4 * k + 4], four, ACT.Copy, scale=float(HD_B) ** -0.5)
    if name[0] == "k":
        return act.activation(kT[:, par, 4 * k:4 * k + 4, 0:P], four, ACT.Copy)
    return act.activation(vw[:, par, 8 * k:8 * k + 8], bank.rearrange("p (h d) -> p h d", d=HD_B), ACT.Copy)


def pick_b(nc, PS, xs, ident, causal, norm_w, w_q, w_k, w_v, w_out, scorer_w, scorer_b, wq, wk, wv, wo, hT, masks, kT, vg, qT, vw, hg):
    with ExitStack() as ctx:
        def sb(name, shape, dt):
            return ctx.enter_context(nc.sbuf_tensor(name, shape, dt))

        def sem(name):
            return ctx.enter_context(nc.semaphore(name))

        shape = [P, BATCH, TILES, DIM]
        xc, xn, hn = sb("bxc", shape, F32), sb("bxn", shape, F32), sb("bhn", shape, F32)
        raw = sb("braw", [P, BATCH, TILES, 6], F32)
        mv = sb("bmv", [P, BATCH, TILES, 2], F32)
        root = sb("broot", [P, BATCH, TILES], F32)
        rstd = sb("brstd", [P, BATCH, TILES], F32)
        power = sb("bpower", [P, 3, BATCH, TILES], F32)
        rrms = sb("brrms", [P, 2, BATCH, TILES], F32)
        nw = sb("nw", [P, 1], F32)
        scw = sb("scw", [P, BATCH, BATCH], F32)
        scb = sb("scb", [BATCH, 1], F32)
        scores = sb("scores", [BATCH, SEQ], F32)
        left = sb("left", [BATCH, 2, SEQ], F32)
        top = sb("top", [BATCH, PICKED], F32)
        index = sb("index", [BATCH, PICKED], U32)
        indexf = sb("indexf", [BATCH, PICKED], F32)
        rows = sb("rows", [BATCH, BATCH, P], F32)
        picked = sb("picked", [P, BATCH, PICKED], F32)
        token = sb("token", [P, TILES], F32)
        onehot = sb("onehot", [P, BATCH, TILES, PICKED], F32)
        later = sb("later", [P, BATCH, TILES, PICKED], F32)
        strips = sb("strips", [P, BATCH, DIM], F32)
        ident4 = sb("ident4", [P, 4, PICKED], F32)
        eye = sb("eye", [P, PICKED], F32)

        w_in, s_in = sem("bw_in"), sem("bs_in")
        dve_chain = sem("bdve_chain")
        varied, rooted, inverted, normed = (sem(n) for n in ("bvaried", "brooted", "binverted", "bnormed"))
        varied2, rooted2, rmsed = (sem(n) for n in ("bvaried2", "brooted2", "rmsed"))
        summed, turned, copied = sem("bsummed"), sem("bturned"), sem("bcopied")
        scored, indexed, spread, spread_copied = (sem(n) for n in ("bscored", "indexed", "spread", "spread_copied"))
        consts, onehots, masked = sem("consts"), sem("onehots"), sem("bmasked")
        gathered, hg_copied, kg_ready, kg_copied = (sem(n) for n in ("gathered", "hg_copied", "kg_ready", "kg_copied"))
        first_ready, first_taken = sem("first_ready"), sem("first_taken")
        stripped, strips_copied, ident4_made = sem("stripped"), sem("strips_copied"), sem("ident4_made")
        causal_copied, vg_zeroed, scw_zeroed = sem("causal_copied"), sem("vg_zeroed"), sem("scw_zeroed")
        strip_banks = (7, 5)
        block = ctx.enter_context(nc.Block())

        @block.sync
        def _(sp):
            sp.dma_start(nw[:], norm_w[:, None], allow_slow_non_contiguous=True).then_inc(s_in, 16)
            sp.dma_start(scb[:], over(scorer_b[None], [BATCH, 1]), allow_slow_non_contiguous=True).then_inc(s_in, 16)
            sp.wait_ge(scw_zeroed, 1)
            for i in range(BATCH):
                sp.dma_start(scw[:, i, i:i + 1], scorer_w, allow_slow_non_contiguous=True).then_inc(s_in, 16)
            for dst, src in ((wk, w_k), (wv, w_v), (wq, w_q)):
                sp.dma_start(dst[:], src).then_inc(w_in, 16)
            sp.dma_start(wo[:], w_out.rearrange("(r p) n -> p r n", p=P)).then_inc(w_in, 16)
            sp.wait_ge(w_in, 64)

        @block.gpsimd
        def _(pool):
            pool.memset(scw[:], 0.0).then_inc(scw_zeroed, 1)
            pool.memset(vg[:], 0.0).then_inc(vg_zeroed, 1)
            pool.iota(token[:], [[P, TILES]], base=0, channel_multiplier=1, allow_small_or_imprecise_dtypes=True).then_inc(consts, 1)
            pool.memset(rows[:], 0.0).then_inc(consts, 1)
            pool.wait_ge(consts, 2)
            pool.affine_select(out=rows[:], in_=rows[:], compare_op=ALU.not_equal, fill=1.0, base=0,
                               pattern=[[-1, BATCH], [0, P]], channel_multiplier=1).then_inc(consts, 1)
            for i in range(BATCH):
                pool.tensor_copy(masks[:, i, :, 0:P], over(causal[:, None], [P, TILES, P])).then_inc(causal_copied, 1)
            pool.wait_ge(inverted, 1)
            for i in range(BATCH):
                pool.tensor_tensor(xn[:, i], xc[:, i], per_row(rstd[:, i]), ALU.mult).then_inc(normed, 1)
                pool.wait_ge(normed, i + 1)
                pool.tensor_tensor(xs[:, i], xs[:, i], xn[:, i], ALU.add).then_inc(summed, 1)

        @block.vector
        def _(dve):
            chain = Chain(dve, dve_chain)
            for i in range(BATCH):
                moments(dve, chain, xs[:, i], raw[:, i], mv[:, i])
            dve.tensor_scalar(root[:], mv[:, :, :, 1], 1e-5, None, ALU.add).then_inc(varied, 1)
            centres = [dve.tensor_tensor(xc[:, i], xs[:, i], per_row(mv[:, i, :, 0]), ALU.subtract) for i in range(BATCH)]
            dve.wait_ge(rooted, 1)
            chain(*centres, dve.reciprocal(rstd[:], root[:]))
            dve.tensor_tensor(power[:, 0], rstd[:], rstd[:], ALU.mult).then_inc(inverted, 1)
            dve.wait_ge(inverted, 1)
            chain(dve.tensor_tensor(power[:, 1], power[:, 0], mv[:, :, :, 1], ALU.mult))
            dve.tensor_scalar(power[:, 2], power[:, 1], 1e-6, None, ALU.add).then_inc(varied2, 1)
            dve.wait_ge(rooted2, 1)
            chain(dve.reciprocal(rrms[:, 0], power[:, 2]))
            chain(dve.tensor_tensor(rrms[:, 1], rrms[:, 0], rstd[:], ALU.mult))
            for i in range(BATCH):
                dve.tensor_tensor(hn[:, i], xc[:, i], per_row(rrms[:, 1, i]), ALU.mult).then_inc(rmsed, 1)
            chain(dve.tensor_reduce(eye[:], ident[:].rearrange("p (r g) -> p g r", r=4), X, ALU.add))
            dve.tensor_copy(ident4[:], over(eye[:, None], [P, 4, PICKED])).then_inc(ident4_made, 1)
            dve.wait_ge(s_in, 64)
            dve.wait_ge(scored, 1)
            chain(dve.tensor_scalar(scores[:], PS[0:BATCH, 4:6, :].rearrange("p b n -> p (b n)"), scb[:, 0:1], None, ALU.add))
            src = scores[:]
            for r in range(PICKED // 8):
                chain(dve.max(top[:, 8 * r:8 * r + 8], src))
                chain(dve.max_index(index[:, 8 * r:8 * r + 8], top[:, 8 * r:8 * r + 8], src))
                if r < PICKED // 8 - 1:
                    chain(dve.match_replace(left[:, r % 2], top[:, 8 * r:8 * r + 8], src, -3.0e38))
                    src = left[:, r % 2]
            dve.tensor_copy(indexf[:], index[:]).then_inc(indexed, 1)
            dve.wait_ge(spread, 1)
            dve.tensor_copy(picked[:], PS[:, 6, 0:BATCH * PICKED].rearrange("p (b g) -> p b g", b=BATCH)).then_inc(spread_copied, 1)
            dve.wait_ge(spread_copied, 1)
            dve.wait_ge(consts, 3)
            for i in range(BATCH):
                at = over(picked[:, i][:, None], [P, TILES, PICKED])
                own = over(token[:, :, None], [P, TILES, PICKED])
                dve.tensor_tensor(onehot[:, i], at, own, ALU.is_equal).then_inc(onehots, 1)
                chain(dve.tensor_tensor(later[:, i], at, own, ALU.is_gt))
                dve.tensor_scalar(masks[:, i, :, P:KEYS], later[:, i], BIG, None, ALU.mult).then_inc(masked, 1)
            dve.wait_ge(kg_ready, 1)
            for i in range(BATCH):
                dve.tensor_copy(kT[:, i, :, P:KEYS], PS[:, 0].rearrange("p (r b g) -> p r b g", r=PAIRS, b=BATCH)[:, :, i]).then_inc(kg_copied, 1)

        @block.scalar
        def _(act):
            act.wait_ge(varied, 1)
            act.activation(root[:], root[:], ACT.Sqrt).then_inc(rooted, 1)
            act.wait_ge(varied2, 1)
            act.activation(power[:, 2], power[:, 2], ACT.Sqrt).then_inc(rooted2, 1)
            act.wait_ge(s_in, 64)
            for i in range(BATCH):
                for k in range(2):
                    act.wait_ge(turned, 2 * i + k + 1)
                    act.activation(hT[:, i, BANK * k:BANK * (k + 1)], PS[:, 2 * i + k, :], ACT.Copy, scale=nw[:, 0:1]).then_inc(copied, 1)
            for n in range(len(PROJECTIONS) * BATCH):
                act.wait_ge(first_ready, n + 1)
                take_half(act, PROJECTIONS[n % len(PROJECTIONS)], PS[:, n % 4, :], n // len(PROJECTIONS), qT, kT, vw).then_inc(first_taken, 1)
            for i in range(BATCH):
                act.wait_ge(stripped, i + 1)
                act.activation(strips[:, i], PS[:, strip_banks[i], 0:DIM], ACT.Copy).then_inc(strips_copied, 1)
            act.wait_ge(gathered, 1)
            act.activation(hg[:], PS[:, 1, 0:BATCH * P].rearrange("p (b r g) -> p b r g", b=BATCH, r=4), ACT.Copy,
                           scale=nw[:, 0:1]).then_inc(hg_copied, 1)

        @block.tensor
        def _(pe):
            for i in range(BATCH):
                pe.wait_ge(rmsed, i + 1)
                for t in range(TILES):
                    mm = pe.transpose(PS[:, 2 * i + t // 4, P * (t % 4):P * (t % 4 + 1)], hn[:, i, t], ident[:])
                    if t % 4 == 3:
                        mm.then_inc(turned, 1)
            pe.wait_ge(copied, 4)
            for k in range(2):
                for i in range(BATCH):
                    mm = pe.matmul(PS[0:BATCH, 4 + k, :], scw[:, i], hT[:, i, BANK * k:BANK * (k + 1)], start=i == 0, stop=i == BATCH - 1)
            mm.then_inc(scored, 1)
            pe.wait_ge(w_in, 64)
            for n in range(len(PROJECTIONS) * BATCH):
                if n >= 4:
                    pe.wait_ge(first_taken, n - 3)
                project_half(pe, PROJECTIONS[n % len(PROJECTIONS)], PS[:, n % 4, :], hT[:, n // len(PROJECTIONS), 0:P],
                             wq, wk, wv).then_inc(first_ready, 1)
            pe.wait_ge(indexed, 1)
            pe.wait_ge(consts, 3)
            for i in range(BATCH):
                mm = pe.matmul(PS[:, 6, PICKED * i:PICKED * (i + 1)], rows[:, i], indexf[:], start=True, stop=True)
            mm.then_inc(spread, 1)
            for i in range(BATCH):
                pe.wait_ge(onehots, i + 1)
                for t in range(TILES):
                    r = t % 4
                    mm = pe.matmul(PS[PICKED * r:PICKED * (r + 1), strip_banks[i], 0:DIM], onehot[:, i, t], hn[:, i, t],
                                   start=t < 4, stop=t >= 4, skip_group_check=True)
                mm.then_inc(stripped, 1)
            pe.wait_ge(first_taken, len(PROJECTIONS) * BATCH)
            pe.wait_ge(ident4_made, 1)
            for i in range(BATCH):
                pe.wait_ge(strips_copied, i + 1)
                mm = pe.matmul(PS[:, 1, P * i:P * (i + 1)], strips[:, i], ident4[:].rearrange("p r g -> p (r g)"), start=True, stop=True)
            mm.then_inc(gathered, 1)
            pe.wait_ge(hg_copied, 1)
            for r in range(PAIRS):
                mm = pe.matmul(PS[:, 0, BATCH * PICKED * r:BATCH * PICKED * (r + 1)], wk[:, P * r:P * (r + 1)], hg[:, :, 0], start=True, stop=True)
            mm.then_inc(kg_ready, 1)


def windows_b(nc, PS, xs, ident, identb, wq, wk, wv, wo, hT, masks, kT, vg, qT, vw, hg, rows):
    with ExitStack() as ctx:
        def sb(name, shape, dt):
            return ctx.enter_context(nc.sbuf_tensor(name, shape, dt))

        def sem(name):
            return ctx.enter_context(nc.semaphore(name))

        hw = sb("hw", [P, 2, P], F32)
        mw = sb("mw", [P, 2, KEYS], BF16)
        nmax = sb("nmax", [P, 2, HEADS_B], F32)
        pr = sb("pr", [P, 2, HEADS_B, KEYS], F32)
        prg = sb("prg", [P, 2, HEADS_B, PICKED], F32)
        pT = sb("pT", [P, HEADS_B, P], F32)
        pgT = sb("pgT", [P, 4, P], F32)
        sums = sb("bsums", [P, 2, HEADS_B], F32)
        inv = sb("binv", [P, 2, HEADS_B], F32)
        oT = sb("boT", [P, PAIRS, P], F32)
        tile_raw = sb("tile_raw", [P, 6], F32)
        tile_mv = sb("tile_mv", [P, 2], F32)

        h_in = [sem(f"h_in{i}") for i in range(2)]
        m_in = [sem(f"m_in{i}") for i in range(2)]
        t_ready, t_taken = sem("t_ready"), sem("t_taken")
        s_ready, s_maxed, s_taken, exped = sem("s_ready"), sem("s_maxed"), sem("s_taken"), sem("bexped")
        p_summed, p_inverted, p_picked, p_scaled = sem("p_summed"), sem("p_inverted"), sem("p_picked"), sem("p_scaled")
        o_ready, o_taken = sem("o_ready"), sem("o_taken")
        out_ready, out_taken = sem("out_ready"), sem("out_taken")
        row_steps = sem("row_steps")
        vg_ready, vg_copied = sem("vg_ready"), sem("vg_copied")
        sp_met, dve_met = sem("bsp_met"), sem("bdve_met")
        block = ctx.enter_context(nc.Block())

        UNITS = [(0, 6), (6, 6), (12, 4)]
        STEP = ["pg", "p0", "s0", "p1", "w0", "s1", "p2", "w1", "p3", "s2", "w2", "w3",
                "q0", "q1", "k0", "k1", "v0", "v1", "out"]
        FIRST_STEP = ["s0", "q0", "q1", "s1", "k0", "k1", "pg", "p0", "p1", "w0", "p2", "w1", "p3", "s2", "w2", "w3",
                      "v0", "v1", "out"]
        ACT_STEP = ["pg", "p0", "p1", "e0", "p2", "p3", "o0", "e1", "o1", "q0", "e2", "q1", "k0", "k1", "v0", "v1"]
        ACT_FIRST = ["q0", "q1", "k0", "k1", "pg", "p0", "e0", "p1", "e1", "p2", "p3", "o0", "e2", "o1", "v0", "v1"]
        NTI = len([name for name in STEP if name[0] in "pqkv"])
        T0 = NTI
        CREDIT = 2

        def names(i, par, step, first):
            if isinstance(i, int) and (i, par) == (0, 0):
                return first
            if isinstance(i, int) and i == TILES - 1:
                return [name for name in step if name not in PROJECTIONS and (par == 0 or name[0] not in "se")]
            return step

        def t_index(i, par, name):
            items = [name for name in names(i, par, STEP, FIRST_STEP) if name[0] in "pqkv"]
            before = 2 * i * NTI + par * (len(items) if isinstance(i, int) and i == TILES - 1 else NTI)
            return T0 + before + items.index(name)

        def bank_of(i, par, name):
            i = i if isinstance(i, int) else 1
            return PS[:, 4 + t_index(i, par, name) % 2, :]

        @block.sync
        def _(sp):
            def load(i, par):
                sp.dma_start(hw[:, par], hT[:, par, bass.ds(i * P, P)]).then_inc(h_in[par], 16)
                sp.dma_start(mw[:, par], masks[:, par, bass.ds(i, 1)].rearrange("p o k -> p (o k)")).then_inc(m_in[par], 16)

            sp.dma_start(mw[:, 1], masks[:, 1, 0]).then_inc(m_in[1], 16)
            load(1, 0)
            sp.wait_ge(s_ready, 6)
            load(1, 1)
            with sp.Fori(1, TILES - 1) as i:
                for par in range(2):
                    sp.wait_ge(t_ready, t_index(i, par, "pg") + 1)
                    sp.sem_inc(sp_met, 1)
                    sp.wait_ge(s_ready, (i * 2 + par) * 3 + 3)
                    sp.sem_inc(sp_met, 1)
                    load(i + 1, par)

        @block.vector
        def _(dve):
            dve.sem_inc(out_taken, CREDIT)

            def softmax(i, par, u, first=False):
                n = (i * 2 + par) * 3 + u
                h0, nh = UNITS[u]
                s = 2 * ((3 * par + u) % 2)
                per = nh // 2
                full = PS[:, s:s + 2, 0:KEYS * per].rearrange("p b (h k) -> p b h k", h=per)
                mx = nmax[:, par, h0:h0 + nh].rearrange("p (h b) -> p b h", b=2)
                dve.wait_ge(s_ready, n + 1)
                dve.tensor_reduce(mx, full, X, ALU.max).then_inc(s_maxed, 1)
                if u == 0 and not first:
                    dve.wait_ge(t_ready, T0 + (i * 2 + par - 1) * NTI)
                dve.wait_ge(s_maxed, n + 1)
                for b in range(2):
                    ins = dve.tensor_tensor(pr[:, par, h0 + b:h0 + nh:2], full[:, b], over(mx[:, b][:, :, None], [P, per, KEYS]),
                                            ALU.subtract)
                ins.then_inc(s_taken, 1)

            def normalise(i, par, u):
                n = (i * 2 + par) * 3 + u
                h0, nh = UNITS[u]
                unit = slice(h0, h0 + nh)
                dve.wait_ge(exped, n + 1)
                dve.tensor_reduce(sums[:, par, unit], pr[:, par, unit], X, ALU.add).then_inc(p_summed, 1)
                dve.wait_ge(p_summed, n + 1)
                dve.reciprocal(inv[:, par, unit], sums[:, par, unit]).then_inc(p_inverted, 1)
                dve.wait_ge(p_inverted, n + 1)
                dve.tensor_tensor(prg[:, par, unit], pr[:, par, unit, P:KEYS], over(inv[:, par, unit, None], [P, nh, PICKED]),
                                  ALU.mult).then_inc(p_picked, 1)
                dve.tensor_tensor(pr[:, par, unit, 0:P], pr[:, par, unit, 0:P], over(inv[:, par, unit, None], [P, nh, P]),
                                  ALU.mult).then_inc(p_scaled, 1)

            def output(i, par):
                n = i * 2 + par
                tile = xs[:, par, bass.ds(i, 1)].rearrange("p o c -> p (o c)")
                dve.wait_ge(out_ready, n + 1 + CREDIT)
                dve.tensor_tensor(tile, tile, PS[:, 6 + par, 0:DIM], ALU.add).then_inc(out_taken, 1)
                mv, xc = (b[:, par, bass.ds(i, 1)].rearrange("p o c -> p (o c)") for b in (rows.mv, rows.xc))
                dve.wait_ge(out_taken, n + 1 + CREDIT)
                dve.sem_inc(dve_met, 1)
                dve.bn_stats(tile_raw[:], tile).then_inc(row_steps, 1)
                dve.wait_ge(row_steps, n * 5 + 1)
                dve.sem_inc(dve_met, 1)
                dve.bn_aggr(tile_mv[:], tile_raw[:]).then_inc(row_steps, 1)
                dve.wait_ge(row_steps, n * 5 + 2)
                dve.tensor_copy(mv, tile_mv[:]).then_inc(row_steps, 1)
                dve.tensor_tensor(xc, tile, over(tile_mv[:, 0:1], [P, DIM]), ALU.subtract).then_inc(row_steps, 1)
                dve.wait_ge(row_steps, n * 5 + 4)
                dve.tensor_reduce(rows.amax[:, par, bass.ds(i, 1)], xc, X, ALU.max, apply_absolute_value=True).then_inc(row_steps, 1)

            def step(i, par, ahead=True):
                i1, par1 = (i, 1) if par == 0 else (i + 1, 0)
                for name in ("s0", "s1", "n0", "s2", "n1", "n2", "out"):
                    if name == "out":
                        output(i, par)
                    elif ahead:
                        (softmax if name[0] == "s" else normalise)(i1, par1, int(name[1]))

            softmax(0, 0, 0, first=True)
            softmax(0, 0, 1, first=True)
            normalise(0, 0, 0)
            softmax(0, 0, 2, first=True)
            normalise(0, 0, 1)
            normalise(0, 0, 2)
            with dve.Fori(0, TILES - 1) as i:
                step(i, 0)
                step(i, 1)
            step(TILES - 1, 0)
            step(TILES - 1, 1, ahead=False)

        @block.scalar
        def _(act):
            act.sem_inc(o_taken, CREDIT)
            act.sem_inc(t_taken, T0)

            def take(i, par, name):
                n = i * 2 + par
                bank = bank_of(i, par, name)
                four = bank.rearrange("p (r t) -> p r t", r=4)
                act.wait_ge(t_ready, t_index(i, par, name) + 1)
                if name == "q0":
                    act.wait_ge(s_ready, n * 3 + 3)
                if name == "v0":
                    act.wait_ge(o_ready, n * 4 + 4 + CREDIT)
                if name in PROJECTIONS:
                    ins = take_half(act, name, bank, par, qT, kT, vw)
                elif name == "pg":
                    act.wait_ge(o_ready, n * 4 + CREDIT)
                    ins = act.activation(pgT[:], four, ACT.Copy)
                else:
                    k = int(name[1])
                    ins = act.activation(pT[:, 4 * k:4 * k + 4], four, ACT.Copy)
                ins.then_inc(t_taken, 1)

            def take_output(i, par, k):
                n = i * 2 + par
                act.wait_ge(o_ready, n * 4 + 2 * k + 2 + CREDIT)
                act.wait_ge(out_ready, n + CREDIT)
                act.activation(oT[:, 4 * k:4 * k + 4], PS[:, 6 + (par + k) % 2, :].rearrange("p (r t) -> p r t", r=4),
                               ACT.Copy).then_inc(o_taken, 1)

            def exponential(i, par, u):
                n = (i * 2 + par) * 3 + u
                h0, nh = UNITS[u]
                act.wait_ge(s_taken, n + 1)
                v = pr[:, par, h0:h0 + nh]
                act.activation(v, v, ACT.Exp).then_inc(exped, 1)

            def step(i, par):
                i1, par1 = (i, 1) if par == 0 else (i + 1, 0)
                for name in names(i, par, ACT_STEP, ACT_FIRST):
                    if name[0] == "e":
                        exponential(i1, par1, int(name[1]))
                    elif name[0] == "o":
                        take_output(i, par, int(name[1]))
                    else:
                        take(i, par, name)

            exponential(0, 0, 0)
            exponential(0, 0, 1)
            for i in range(BATCH):
                act.wait_ge(vg_ready, i + 1)
                for r in range(4):
                    src = PS[32 * r:32 * (r + 1), 4 + 2 * i:6 + 2 * i, :].rearrange("p b n -> p (b n)").rearrange(
                        "p (g r d) -> p g r d", g=HEADS_B // 4, r=4)[:, :, r]
                    act.activation(vg[32 * r:32 * (r + 1), i, :, r], src, ACT.Copy).then_inc(vg_copied, 1)
            exponential(0, 0, 2)
            step(0, 0)
            step(0, 1)
            with act.Fori(1, TILES - 1) as i:
                step(i, 0)
                step(i, 1)
            step(TILES - 1, 0)
            step(TILES - 1, 1)

        @block.tensor
        def _(pe):
            pe.sem_inc(o_ready, CREDIT)
            pe.sem_inc(out_ready, CREDIT)
            pe.sem_inc(t_ready, T0)

            def item(i, par, name):
                pe.wait_ge(t_taken, t_index(i, par, name) - 1)
                return bank_of(i, par, name)

            def scores(i, par, u, first=False):
                n = (i * 2 + par) * 3 + u
                h0, nh = UNITS[u]
                s = 2 * ((3 * par + u) % 2)
                if u == 0:
                    if not first:
                        pe.wait_ge(t_taken, T0 + (i * 2 + par - 1) * NTI)
                        pe.wait_ge(m_in[par], (i + par) * 16)
                if not (first and u < 2):
                    pe.wait_ge(s_taken, n - 1)
                per = nh // 2
                for k in range(per):
                    for b in range(2):
                        lo = HD_B * b
                        pe.matmul(PS[:, s + b, KEYS * k:KEYS * (k + 1)], qT[lo:lo + HD_B, par, h0 // 2 + k],
                                  kT[lo:lo + HD_B, par, h0 // 2 + k], start=k == 0, stop=False, skip_group_check=True)
                mask = masks[:, par, 0] if first else mw[:, par]
                for b in range(2):
                    mm = pe.matmul(PS[:, s + b, 0:KEYS * per], identb[:], over(mask[:, None], [P, per, KEYS]),
                                   start=False, stop=True, skip_group_check=True)
                mm.then_inc(s_ready, 1)

            def turn_probs(i, par, name):
                bank = item(i, par, name)
                if name == "pg":
                    pe.wait_ge(p_scaled, (i * 2 + par) * 3 + 3)
                for r in range(4):
                    if name == "pg":
                        src = prg[:, par, 4 * r:4 * r + 4].rearrange("p h g -> p (h g)")
                    else:
                        src = pr[:, par, 4 * int(name[1]) + r, 0:P]
                    mm = pe.transpose(bank[:, P * r:P * (r + 1)], src, ident[:])
                mm.then_inc(t_ready, 1)

            def weigh(i, par, g):
                n = i * 2 + par
                if g == 0:
                    pe.wait_ge(o_taken, n * 2 + CREDIT)
                if g == 2:
                    pe.wait_ge(out_taken, n + CREDIT)
                pe.wait_ge(t_taken, t_index(i, par, f"p{g}") + 1)
                for k in range(2):
                    block = PS[:, 6 + (par + g // 2) % 2, P * (2 * (g % 2) + k):P * (2 * (g % 2) + k + 1)]
                    pe.matmul(block, vg[:, par, g, 2 * k:2 * k + 2].rearrange("p h d -> p (h d)"), pgT[:, g],
                              start=True, stop=False, skip_group_check=True)
                    for b in range(2):
                        h = 4 * g + 2 * k + b
                        mm = pe.matmul(block[HD_B * b:HD_B * (b + 1)], vw[:, par, h], pT[:, h], start=False, stop=True,
                                       skip_group_check=True)
                mm.then_inc(o_ready, 1)

            def output(i, par):
                n = i * 2 + par
                pe.wait_ge(o_taken, n * 2 + 2 + CREDIT)
                for r in range(PAIRS):
                    mm = pe.matmul(PS[:, 6 + par, 0:DIM], oT[:, r], wo[:, r], start=r == 0, stop=r == PAIRS - 1)
                mm.then_inc(out_ready, 1)

            def step(i, par):
                i1, par1 = (i, 1) if par == 0 else (i + 1, 0)
                for name in names(i, par, STEP, FIRST_STEP):
                    if name[0] == "s":
                        scores(i1, par1, int(name[1]))
                    elif name[0] == "w":
                        weigh(i, par, int(name[1]))
                    elif name[0] == "p":
                        turn_probs(i, par, name)
                    elif name == "out":
                        output(i, par)
                    else:
                        if name == "q0":
                            if isinstance(i, int) and (i, par) == (0, 0):
                                pe.wait_ge(vg_copied, 4 * BATCH)
                            pe.wait_ge(h_in[par], (i + 1) * 16)
                        project_half(pe, name, item(i, par, name), hw[:, par], wq, wk, wv).then_inc(t_ready, 1)

            scores(0, 0, 0, first=True)
            scores(0, 0, 1, first=True)
            scores(0, 0, 2, first=True)
            for i in range(BATCH):
                for k in range(2):
                    mm = pe.matmul(PS[:, 4 + 2 * i + k, :], hg[:, i].rearrange("p r g -> p (r g)"), wv[:, BANK * k:BANK * (k + 1)],
                                   start=True, stop=True)
                mm.then_inc(vg_ready, 1)
            step(0, 0)
            step(0, 1)
            with pe.Fori(1, TILES - 1) as i:
                step(i, 0)
                step(i, 1)
            step(TILES - 1, 0)
            step(TILES - 1, 1)


_INS = ["L0_attn_a_x", "L0_attn_a_W", "L0_attn_a_b", "L0_attn_b_norm_w", "L0_attn_b_w_q", "L0_attn_b_w_k", "L0_attn_b_w_v",
        "L0_attn_b_w_out", "L0_attn_b_scorer_w", "L0_attn_b_scorer_b", "L0_ffn_weight_q", "L0_ffn_weight_scale",
        "L0_ffn_bias"]


def kernel(**inputs):
    import numpy as _np
    import concourse.bacc as _bacc
    from concourse import mybir as _mybir
    from concourse.bass_utils import run_bass_kernel_spmd as _run

    nc = _bacc.Bacc("TRN2", target_bir_lowering=False, num_devices=1)
    arrays, args = {}, []
    for name in _INS:
        a = _np.ascontiguousarray(inputs[name])
        if a.dtype.kind in "iu":
            a = a.astype(_np.int64)
        arrays[f"in_{name}_dram"] = a
        args.append(nc.dram_tensor(f"in_{name}_dram", a.shape, _mybir.dt.from_np(a.dtype), kind="ExternalInput").ap())
    args.append(nc.dram_tensor("out_dram", (BATCH, SEQ, DIM), F32, kind="ExternalOutput").ap())
    build(nc, *args)
    return _run(nc, [arrays], core_ids=[0]).results[0]["out_dram"]
```
